# Optimizing a Trainium2 kernel written in Bass

```python
import numpy as np
import jax
import jax.numpy as jnp

def _softmax(x, axis=-1):
    return jax.nn.softmax(x, axis=axis)

def _gelu(x):
    return jax.nn.gelu(x, approximate=True)

def _silu(x):
    return jax.nn.silu(x)

def _sigmoid(x):
    return jax.nn.sigmoid(x)

def _layernorm(x, axis=-1, eps=1e-05):
    m = jnp.mean(x, axis=axis, keepdims=True)
    v = jnp.var(x, axis=axis, keepdims=True)
    return (x - m) / jnp.sqrt(v + eps)

def _scatter_add(tgt, idx, src, axis=0):
    return tgt.at[idx].add(src)

def _segment_sum(src, seg, n):
    return jax.ops.segment_sum(src, seg, n)
kernel_name = 'mk_rec_standalone_d1_rec_r8_928428'

def setup_inputs(seed: int=0):
    np.random.seed(seed)
    _w = jnp.asarray

    def _rec_inputs():
        import jax
        import jax.numpy as jnp
        _rk = jax.random.key(seed)
        r_strength = jax.random.uniform(jax.random.fold_in(_rk, 1), (512, 4, 4), jnp.float32, 0.0, 0.999994)
        r_x = 7.22013e-05 + 1.00017 * jax.random.normal(jax.random.fold_in(_rk, 2), (512, 256), jnp.float32)
        return (r_strength, r_x)
    r_strength, r_x = _rec_inputs()

    def _L0_rec_setup():
        import jax, jax.numpy as jnp
        import numpy as np
        B, IN, HID, D, N, OUT = (512, 256, 256, 512, 4, 512)
        H = 8
        HD = D // H

        def _ln(x, g, b):
            m = x.mean(-1, keepdims=True)
            v = ((x - m) ** 2).mean(-1, keepdims=True)
            return (x - m) / jnp.sqrt(v + 1e-05) * g + b
        key = jax.random.key(seed)
        ks = jax.random.split(key, 32)

        def nrm(k, shape, scale=0.02):
            return jax.random.normal(k, shape, jnp.float32) * scale
        inp = {}
        inp['x'] = jax.random.normal(ks[0], (B, IN), jnp.float32)
        inp['strength'] = jax.random.uniform(ks[1], (B, N, N), jnp.float32)
        for t, i in (('er', 2), ('ei', 4)):
            inp[t + '_W1'] = nrm(ks[i], (HID, IN))
            inp[t + '_b1'] = jnp.zeros((HID,), jnp.float32)
            inp[t + '_g1'] = jnp.ones((HID,), jnp.float32)
            inp[t + '_be1'] = jnp.zeros((HID,), jnp.float32)
            inp[t + '_W2'] = nrm(ks[i + 1], (N * D, HID))
            inp[t + '_b2'] = jnp.zeros((N * D,), jnp.float32)
        names = ['Wq_r', 'Wq_i', 'Wk_r', 'Wk_i', 'Wv_r', 'Wv_i', 'Wo_r', 'Wo_i']
        for j, nm in enumerate(names):
            inp[nm] = nrm(ks[6 + j], (D, D))
            inp['b' + nm[1:]] = jnp.zeros((D,), jnp.float32)
        inp['int_Wr'] = jnp.tile(jnp.eye(D, dtype=jnp.float32)[None], (N, 1, 1))
        inp['int_Wi'] = jnp.zeros((N, D, D), jnp.float32)
        inp['meas_Mr'] = nrm(ks[20], (OUT, D), 1.0 / np.sqrt(D))
        inp['meas_Mi'] = nrm(ks[21], (OUT, D), 1.0 / np.sqrt(D))
        inp['post_W'] = nrm(ks[22], (OUT, OUT))
        inp['post_b'] = jnp.zeros((OUT,), jnp.float32)
        inp['post_g'] = jnp.ones((OUT,), jnp.float32)
        inp['post_be'] = jnp.zeros((OUT,), jnp.float32)
        return inp
    _L0_rec_all = _L0_rec_setup()
    _L0_rec_in = {k: v for k, v in _L0_rec_all.items() if k in ('er_W1', 'er_b1', 'er_g1', 'er_be1', 'er_W2', 'er_b2', 'ei_W1', 'ei_b1', 'ei_g1', 'ei_be1', 'ei_W2', 'ei_b2', 'Wq_r', 'bq_r', 'Wq_i', 'bq_i', 'Wk_r', 'bk_r', 'Wk_i', 'bk_i', 'Wv_r', 'bv_r', 'Wv_i', 'bv_i', 'Wo_r', 'bo_r', 'Wo_i', 'bo_i', 'int_Wr', 'int_Wi', 'meas_Mr', 'meas_Mi', 'post_W', 'post_b', 'post_g', 'post_be')}
    del _L0_rec_all
    return {'r_strength': r_strength, 'r_x': r_x, 'L0_rec_er_W1': _L0_rec_in['er_W1'], 'L0_rec_er_b1': _L0_rec_in['er_b1'], 'L0_rec_er_g1': _L0_rec_in['er_g1'], 'L0_rec_er_be1': _L0_rec_in['er_be1'], 'L0_rec_er_W2': _L0_rec_in['er_W2'], 'L0_rec_er_b2': _L0_rec_in['er_b2'], 'L0_rec_ei_W1': _L0_rec_in['ei_W1'], 'L0_rec_ei_b1': _L0_rec_in['ei_b1'], 'L0_rec_ei_g1': _L0_rec_in['ei_g1'], 'L0_rec_ei_be1': _L0_rec_in['ei_be1'], 'L0_rec_ei_W2': _L0_rec_in['ei_W2'], 'L0_rec_ei_b2': _L0_rec_in['ei_b2'], 'L0_rec_Wq_r': _L0_rec_in['Wq_r'], 'L0_rec_bq_r': _L0_rec_in['bq_r'], 'L0_rec_Wq_i': _L0_rec_in['Wq_i'], 'L0_rec_bq_i': _L0_rec_in['bq_i'], 'L0_rec_Wk_r': _L0_rec_in['Wk_r'], 'L0_rec_bk_r': _L0_rec_in['bk_r'], 'L0_rec_Wk_i': _L0_rec_in['Wk_i'], 'L0_rec_bk_i': _L0_rec_in['bk_i'], 'L0_rec_Wv_r': _L0_rec_in['Wv_r'], 'L0_rec_bv_r': _L0_rec_in['bv_r'], 'L0_rec_Wv_i': _L0_rec_in['Wv_i'], 'L0_rec_bv_i': _L0_rec_in['bv_i'], 'L0_rec_Wo_r': _L0_rec_in['Wo_r'], 'L0_rec_bo_r': _L0_rec_in['bo_r'], 'L0_rec_Wo_i': _L0_rec_in['Wo_i'], 'L0_rec_bo_i': _L0_rec_in['bo_i'], 'L0_rec_int_Wr': _L0_rec_in['int_Wr'], 'L0_rec_int_Wi': _L0_rec_in['int_Wi'], 'L0_rec_meas_Mr': _L0_rec_in['meas_Mr'], 'L0_rec_meas_Mi': _L0_rec_in['meas_Mi'], 'L0_rec_post_W': _L0_rec_in['post_W'], 'L0_rec_post_b': _L0_rec_in['post_b'], 'L0_rec_post_g': _L0_rec_in['post_g'], 'L0_rec_post_be': _L0_rec_in['post_be']}

def reference(r_strength, r_x, L0_rec_er_W1, L0_rec_er_b1, L0_rec_er_g1, L0_rec_er_be1, L0_rec_er_W2, L0_rec_er_b2, L0_rec_ei_W1, L0_rec_ei_b1, L0_rec_ei_g1, L0_rec_ei_be1, L0_rec_ei_W2, L0_rec_ei_b2, L0_rec_Wq_r, L0_rec_bq_r, L0_rec_Wq_i, L0_rec_bq_i, L0_rec_Wk_r, L0_rec_bk_r, L0_rec_Wk_i, L0_rec_bk_i, L0_rec_Wv_r, L0_rec_bv_r, L0_rec_Wv_i, L0_rec_bv_i, L0_rec_Wo_r, L0_rec_bo_r, L0_rec_Wo_i, L0_rec_bo_i, L0_rec_int_Wr, L0_rec_int_Wi, L0_rec_meas_Mr, L0_rec_meas_Mi, L0_rec_post_W, L0_rec_post_b, L0_rec_post_g, L0_rec_post_be):
    import jax
    import jax.numpy as jnp

    def _L0_rec_ref(x, strength, er_W1, er_b1, er_g1, er_be1, er_W2, er_b2, ei_W1, ei_b1, ei_g1, ei_be1, ei_W2, ei_b2, Wq_r, bq_r, Wq_i, bq_i, Wk_r, bk_r, Wk_i, bk_i, Wv_r, bv_r, Wv_i, bv_i, Wo_r, bo_r, Wo_i, bo_i, int_Wr, int_Wi, meas_Mr, meas_Mi, post_W, post_b, post_g, post_be):
        import jax, jax.numpy as jnp
        import numpy as np
        B, IN, HID, D, N, OUT = (512, 256, 256, 512, 4, 512)
        H = 8
        HD = D // H

        def _ln(x, g, b):
            m = x.mean(-1, keepdims=True)
            v = ((x - m) ** 2).mean(-1, keepdims=True)
            return (x - m) / jnp.sqrt(v + 1e-05) * g + b
        Bsz = x.shape[0]

        def enc(W1, b1, g, be, W2, b2):
            h = jax.nn.gelu(_ln(x @ W1.T + b1, g, be), approximate=False)
            return (h @ W2.T + b2).reshape(Bsz, N, D)
        sr = enc(er_W1, er_b1, er_g1, er_be1, er_W2, er_b2)
        si = enc(ei_W1, ei_b1, ei_g1, ei_be1, ei_W2, ei_b2)

        def heads(t):
            return t.reshape(Bsz, N, H, HD).transpose(0, 2, 1, 3)
        qr = heads(sr @ Wq_r.T + bq_r)
        qi = heads(si @ Wq_i.T + bq_i)
        kr = heads(sr @ Wk_r.T + bk_r)
        ki = heads(si @ Wk_i.T + bk_i)
        vr = heads(sr @ Wv_r.T + bv_r)
        vi = heads(si @ Wv_i.T + bv_i)
        ar = jnp.einsum('bhnd,bhmd->bhnm', qr, kr) + jnp.einsum('bhnd,bhmd->bhnm', qi, ki)
        ai = jnp.einsum('bhnd,bhmd->bhnm', qi, kr) - jnp.einsum('bhnd,bhmd->bhnm', qr, ki)
        mag = jnp.sqrt(ar ** 2 + ai ** 2 + 1e-08) * HD ** (-0.5)
        w = jax.nn.softmax(mag, axis=-1)
        out_r = jnp.einsum('bhnm,bhmd->bhnd', w, vr).transpose(0, 2, 1, 3).reshape(Bsz, N, D)
        out_i = jnp.einsum('bhnm,bhmd->bhnd', w, vi).transpose(0, 2, 1, 3).reshape(Bsz, N, D)
        attn_r = out_r @ Wo_r.T + bo_r
        attn_i = out_i @ Wo_i.T + bo_i
        R = jnp.einsum('bnd,ned->bne', attn_r, int_Wr) - jnp.einsum('bnd,ned->bne', attn_i, int_Wi)
        I = jnp.einsum('bnd,ned->bne', attn_r, int_Wi) + jnp.einsum('bnd,ned->bne', attn_i, int_Wr)
        Ri, Ii = (R[:, :, None, :], I[:, :, None, :])
        Rj, Ij = (R[:, None, :, :], I[:, None, :, :])
        phase = jnp.arctan2(Ii * Rj - Ri * Ij, Ri * Rj + Ii * Ij)
        f = jnp.cos(phase) * strength[..., None]
        sup_r = jnp.einsum('bijd,bjd->bd', f, R)
        sup_i = jnp.einsum('bijd,bjd->bd', f, I)
        norm = jnp.sqrt(jnp.sum(sup_r ** 2 + sup_i ** 2, axis=-1, keepdims=True) + 1e-08)
        sup_r = sup_r / norm
        sup_i = sup_i / norm
        mr = sup_r @ meas_Mr.T - sup_i @ meas_Mi.T
        mi = sup_r @ meas_Mi.T + sup_i @ meas_Mr.T
        amp = jnp.sqrt(mr ** 2 + mi ** 2)
        out = jax.nn.gelu(_ln(amp @ post_W.T + post_b, post_g, post_be), approximate=False)
        return out
    y = _L0_rec_ref(r_x, r_strength, L0_rec_er_W1, L0_rec_er_b1, L0_rec_er_g1, L0_rec_er_be1, L0_rec_er_W2, L0_rec_er_b2, L0_rec_ei_W1, L0_rec_ei_b1, L0_rec_ei_g1, L0_rec_ei_be1, L0_rec_ei_W2, L0_rec_ei_b2, L0_rec_Wq_r, L0_rec_bq_r, L0_rec_Wq_i, L0_rec_bq_i, L0_rec_Wk_r, L0_rec_bk_r, L0_rec_Wk_i, L0_rec_bk_i, L0_rec_Wv_r, L0_rec_bv_r, L0_rec_Wv_i, L0_rec_bv_i, L0_rec_Wo_r, L0_rec_bo_r, L0_rec_Wo_i, L0_rec_bo_i, L0_rec_int_Wr, L0_rec_int_Wi, L0_rec_meas_Mr, L0_rec_meas_Mi, L0_rec_post_W, L0_rec_post_b, L0_rec_post_g, L0_rec_post_be)
    return y

_drawn_inputs = setup_inputs


def setup_inputs(seed=0):
    import zlib

    import numpy as np

    out = dict(_drawn_inputs(seed))
    spreads = {'L0_rec_er_b1': (0.0, 0.707),
     'L0_rec_er_g1': (1.0, 0.6),
     'L0_rec_er_be1': (0.0, 0.8),
     'L0_rec_er_b2': (0.0, 0.501),
     'L0_rec_ei_b1': (0.0, 0.656),
     'L0_rec_ei_g1': (1.0, 0.6),
     'L0_rec_ei_be1': (0.0, 0.8),
     'L0_rec_ei_b2': (0.0, 0.513),
     'L0_rec_bq_r': (0.0, 0.8),
     'L0_rec_bq_i': (0.0, 0.8),
     'L0_rec_bk_r': (0.0, 0.8),
     'L0_rec_bk_i': (0.0, 0.8),
     'L0_rec_bv_r': (0.0, 0.1),
     'L0_rec_bv_i': (0.0, 0.1),
     'L0_rec_bo_r': (0.0, 0.1),
     'L0_rec_bo_i': (0.0, 0.1),
     'L0_rec_int_Wi': (0.0, 0.1),
     'L0_rec_post_b': (0.0, 0.1),
     'L0_rec_post_g': (1.0, 0.2),
     'L0_rec_post_be': (0.0, 0.1)}
    factors = {'L0_rec_Wq_r': 8.0, 'L0_rec_Wq_i': 8.0, 'L0_rec_Wk_r': 8.0, 'L0_rec_Wk_i': 8.0}
    for name, (base, spread) in spreads.items():
        noise = np.random.default_rng([zlib.crc32(name.encode()), seed]).standard_normal(out[name].shape)
        drawn = base * np.exp(spread * noise) if base else spread * noise
        out[name] = jnp.asarray(drawn.astype(out[name].dtype))
    for name, factor in factors.items():
        out[name] = (out[name] * factor).astype(out[name].dtype)
    return out
```

```python
from contextlib import ExitStack

import concourse.bass as bass
from concourse import mybir

ALU = mybir.AluOpType
ACT = mybir.ActivationFunctionType
AX = mybir.AxisListType
F32 = mybir.dt.float32
BF16 = mybir.dt.bfloat16

P = 128
B, IN, HID, D, N, OUT, H = 512, 256, 256, 512, 4, 512, 8
HALVES = 2
HB = B // HALVES
BT = B // P
KH = HID // P
KD = D // P
C = H // 2
G = HB // 32
BANKS = 8
SLOTS = 3
SLOT = 2048
DW = 3
TINY = 1e-37
EPS = 1e-5
SCALE = (D // H) ** -0.5

def timeline():
    steps = [("enc", b) for b in range(BT)]
    for h in range(HALVES):
        steps += [("nodes", h, 0), ("nodes", h, 1)]
        steps += [("qk", h, 0)]
        if h:
            steps += [("meas", h - 1)]
        steps += [("qk", h, 1)]
        if h:
            steps += [("post", h - 1)]
        steps += [("score", h, 0), ("qk", h, 2), ("score", h, 1), ("qk", h, 3), ("score", h, 2)]
        steps += [("value", h, 0), ("score", h, 3)]
        steps += [("value", h, g) for g in range(1, 4)]
        steps += [("softmax", h)]
        steps += [("value", h, g) for g in range(4, G)]
        steps += [("mix", h, gp) for gp in range(G // 2)]
        steps += [("attn_out", h, 0), ("attn_out", h, 1)]
        for et in range(KD):
            steps += [("inter", h, et, 0), ("inter", h, et, 1), ("super", h, et)]
    return steps + [("meas", HALVES - 1), ("post", HALVES - 1)]


def tiles_of(step):
    s, a = step[0], step[1:]
    if s == "enc":
        return [(("enc", *a), "enc_sum", 1), (("encT", *a), "h_ready", 4)]
    if s == "nodes":
        out = []
        for n in (2 * a[1], 2 * a[1] + 1):
            for dp in range(2):
                out += [(("nodes", a[0], 0, n, dp), "sr_ready", 2), (("nodes", a[0], 1, n, dp), "si_ready", 1)]
        return out
    if s == "qk":
        out = []
        for np_ in range(2):
            for mat, sem, k in (("kr", "qk_by_act", 2), ("ki", "qk_by_dve", 2), ("qr", "qk_by_act", 4), ("qi", "qk_by_dve", 4)):
                out.append((("qk", *a, np_, mat), sem, k))
        return out
    if s == "score":
        return [(("score", *a, g), "sq_ready", 1) for g in range(G)]
    if s == "value":
        return [(("value", *a, 0), "vr_ready", 1), (("value", *a, 1), "vi_ready", 1)]
    if s == "mix":
        return [(("mix", *a, c), "mix_by_dve" if c % 2 else "mix_by_act", 4) for c in range(C)]
    if s == "attn_out":
        return [(("attn_out", *a, et, ri), "ai_ready" if ri else "ar_ready", 1) for et in range(KD) for ri in range(2)]
    if s == "inter":
        return [(("inter", *a, 0), "k1_ready", 1), (("inter", *a, 1), "ri_ready", 1), (("inter", *a, 2), "ri_ready", 1)]
    if s == "meas":
        out = [(("norm", *a), "norm_read", 1)]
        for op in range(2):
            out += [(("meas", *a, op, 0), "mk1_ready", 1), (("meas", *a, op, 1), "m_ready", 1), (("meas", *a, op, 2), "m_ready", 1)]
        return out
    if s == "post":
        return [(("post", *a, bt), "post_sum", 1) for bt in range(HB // P)]
    return []


def loads_of(step):
    s, a = step[0], step[1:]
    if s == "nodes":
        return [("W2", 0, a[1]), ("W2", 1, a[1])]
    if s == "qk":
        return [("Wqk", a[1])]
    if s == "value" and a[1] == 0:
        return [("Wv", 0), ("Wv", 1)]
    if s == "attn_out" and a[1] == 0:
        return [("Wo", 0), ("Wo", 1)]
    if s == "inter":
        return [("Wint", a[1], a[2])]
    if s == "meas":
        return [("M", 0), ("M", 1)]
    if s == "post":
        return [("Wp",)]
    return []


def frees_at(step):
    return step


def build(nc, out, xT, w1, w2r, w2i, wqk, wvr, wvi, wor, woi, wint, mr, mi, wp, cols, rows, ident, mask, strength):
    steps = timeline()

    number, emptied, counts = {}, {}, {}
    last_tile = {}
    for st in steps:
        for key, sem, k in tiles_of(st):
            number[key] = len(number)
            counts[sem] = counts.get(sem, 0) + k
            emptied[number[key]] = (sem, counts[sem])
            last_tile[st] = number[key]

    loads, load_at = [], {}
    for st in steps:
        for ld in loads_of(st):
            key = (st, ld)
            load_at[key] = len(loads)
            loads.append([st, ld])
    last_use = []
    for st, ld in loads:
        if ld[0] == "Wv":
            last_use.append(("value", st[1], G - 1))
        elif ld[0] == "Wo":
            last_use.append(("attn_out", st[1], 1))
        else:
            last_use.append(st)

    units, unit_at = [], {}
    for st in steps:
        if st[0] == "inter":
            for j in range(2):
                unit_at[(st, j)] = len(units)
                units.append((st, j, last_tile[st]))
        if st[0] == "meas":
            for op in range(2):
                for j in range(2):
                    unit_at[(st, op, j)] = len(units)
                    units.append((st, (op, j), number[("meas", st[1], op, 1 + j)]))

    with ExitStack() as ctx:
        def sb(name, shape, dt=F32):
            return ctx.enter_context(nc.sbuf_tensor(name, shape, dt))

        ps = [ctx.enter_context(nc.psum_tensor(f"bank{i}", [P, 512], F32)) for i in range(BANKS)]
        sems = {}

        def sem(name):
            if name not in sems:
                sems[name] = ctx.enter_context(nc.semaphore(name))
            return sems[name]

        ring = sb("ring", [P, SLOTS, SLOT])
        dw = sb("dw", [P, DW, 1024])
        X = sb("X", [P, 12288])
        Y = sb("Y", [P, 8192])
        T = sb("T", [P, 72 * 256])
        hT = sb("hT", [P, 2, KH, B])
        k1s = sb("k1s", [P, 512])
        sq = sb("sq", [P, 2, 512])
        diag = sb("diag", [P, G, 32])
        col = sb("col", [P, cols.shape[1]])
        ncol = sb("ncol", [P, C])
        idn = sb("idn", [P, P])
        msk = sb("msk", [P, 32])
        ones = sb("ones", [P, 2])
        small = sb("small", [P, 40])

        Q = X[:, 0:8192].rearrange("p (u h v q) -> p u h v q", u=2, h=2, v=2)
        K = X[:, 8192:12288].rearrange("p (u h q) -> p u h q", u=2, h=2)
        A = X[:].rearrange("p (r k n b) -> p r k n b", r=3, k=KD, n=N)
        S = Y[:].rearrange("p (e k q) -> p e k q", e=2, k=KD)
        S_node = Y[:].rearrange("p (e k g n b) -> p e k n g b", e=2, k=KD, g=G, n=N)
        MX = Y[:].rearrange("p (r c q) -> p r c q", r=2, c=C)

        def A_rows(r, k, rh):
            return A[:, r, k, :, rh * P:(rh + 1) * P].rearrange("p n (g b) -> p n g b", g=4)

        def t(kb, size):
            return T[:, kb * 256:kb * 256 + size]

        V = t(0, 8192).rearrange("p (g c f) -> p g c f", g=G, c=C)
        PR = t(32, 4096).rearrange("p (u q b) -> p u q b", u=4, q=32)
        sm = [t(48 + j, 256) for j in range(8)]
        st_bc = t(0, 4096).rearrange("p (s b) -> p s b", s=16)
        RI = t(16, 2048).rearrange("p (r n b) -> p r n b", r=2, n=N)
        zsq = t(24, 2048).rearrange("p (r q) -> p r q", r=2)
        n2 = t(32, 1024)
        y0 = t(36, 1024)
        y2 = t(40, 1024)
        pr = t(24, 3072).rearrange("p (r k b) -> p r k b", r=2, k=6)
        cc = t(36, 1536).rearrange("p (k b) -> p k b", k=6)
        PL = t(24, 1536).rearrange("p (k b) -> p k b", k=6)
        PU = t(30, 1536).rearrange("p (k b) -> p k b", k=6)
        prod = t(24, 2048).rearrange("p (r n b) -> p r n b", r=2, n=N)
        U = t(44, 2048).rearrange("p (r n b) -> p r n b", r=2, n=N)
        Efl = t(52, 1024).rearrange("p (n b) -> p n b", n=N)
        Eij = T[:, 56 * 256:59 * 256].bitcast(BF16).rearrange("p (k b) -> p k b", k=6)
        Wt = t(59, 1024).rearrange("p (n b) -> p n b", n=N)
        SUP = t(64, 2048).rearrange("p (r k b) -> p r k b", r=2, k=KD)
        xs = t(0, 1024).rearrange("p (k b) -> p k b", k=2)
        w1s = t(4, 1024).rearrange("p (e k o) -> p e k o", e=2, k=2)
        b1s = t(8, 512)
        hs = t(10, 1024).rearrange("p (u f) -> p u f", u=2)
        hn = t(14, 1024).rearrange("p (u f) -> p u f", u=2)
        ssum = t(44, 1024)
        ssq = t(24, 2048).rearrange("p (r q) -> p r q", r=2)
        ssq1 = t(32, 1024).rearrange("p (k b) -> p k b", k=KD)
        MRI = t(16, 2048).rearrange("p (r o b) -> p r o b", r=2, o=KD)
        msq = t(24, 2048).rearrange("p (r q) -> p r q", r=2)
        m2, my, my2, amp = t(36, 1024), t(40, 1024), t(48, 1024), t(52, 1024)
        ampT = amp.rearrange("p (k b) -> p k b", k=KD)
        prow = t(57, 1536).rearrange("p (j f) -> p j f", j=3)
        pos = t(0, 1024).rearrange("p (u f) -> p u f", u=2)
        pon = t(4, 1024).rearrange("p (u f) -> p u f", u=2)

        bcol = {}
        at = 0
        for name, k in (("b2r", 16), ("b2i", 16), ("bqr", 4), ("bqi", 4), ("bkr", 4), ("bki", 4), ("bvr", 4),
                        ("bvi", 4), ("bor", 4), ("boi", 4), ("gr", 2), ("ber", 2), ("gi", 2), ("bei", 2)):
            bcol[name] = at
            at += k

        def bias(name, j, lo=0, hi=P):
            return col[lo:hi, bcol[name] + j:bcol[name] + j + 1]

        def slot(st, ld):
            return ring[:, load_at[(st, ld)] % SLOTS, :]

        def unit(*key):
            return dw[:, unit_at[key] % DW, :]

        def bank(key):
            return ps[number[key] % BANKS][:, :]

        def full(eng, key):
            eng.wait_ge(sem("tile_full"), number[key] + 1)

        def read_of(eng, key):
            s, n = emptied[number[key]]
            eng.wait_ge(sem(s), n)

        NV, NA, NP = 21, 4, 10
        sup_index = lambda h, et: h * KD + et

        block = ctx.enter_context(nc.Block())

        @block.sync
        def _(sp):
            for b in range(1):
                sp.dma_start(w1s, w1).then_inc(sem("in_enc"), 16)
                sp.dma_start(b1s, rows[0:1, 0:512].to_broadcast([P, 512])).then_inc(sem("in_enc"), 16)
                sp.dma_start(col[:], cols).then_inc(sem("in_const"), 16)
                sp.dma_start(idn[:], ident).then_inc(sem("in_const"), 16)
                sp.dma_start(msk[:], mask).then_inc(sem("in_const"), 16)
            src = {"W2": lambda e, np_: (w2r, w2i)[e][:, np_, :], "Wqk": lambda c: wqk[:, c, :],
                   "Wv": lambda r: (wvr, wvi)[r], "Wo": lambda r: (wor, woi)[r],
                   "Wint": lambda et, np_: wint[:, et, np_, :], "M": lambda r: (mr, mi)[r], "Wp": lambda: wp}
            for n, (st, ld) in enumerate(loads):
                if n >= SLOTS:
                    sp.wait_ge(sem("tile_full"), last_tile[last_use[n - SLOTS]] + 1)
                    if last_use[n - SLOTS][0] in ("inter", "meas"):
                        sp.wait_ge(sem("dw_ready"), max(v for k, v in unit_at.items() if k[0] == last_use[n - SLOTS]) * 2 + 2)
                sp.dma_start(ring[:, n % SLOTS, :], src[ld[0]](*ld[1:])).then_inc(sem(f"slot{n % SLOTS}"), 16)

        @block.tensor
        def _(pe):
            seen = set()

            def begin(key):
                n = number[key]
                if n >= BANKS:
                    s, k = emptied[n - BANKS]
                    pe.wait_ge(sem(s), k)

            def weights(st, ld):
                n = load_at[(st, ld)]
                if n not in seen:
                    seen.add(n)
                    pe.wait_ge(sem(f"slot{n % SLOTS}"), 16 * (n // SLOTS + 1))
                return slot(st, ld)

            pe.wait_ge(sem("in_const"), 48)
            for st in steps:
                s, a = st[0], st[1:]
                if s == "enc":
                    (b,) = a
                    key = ("enc", b)
                    begin(key)
                    if b == 0:
                        pe.wait_ge(sem("in_enc"), 32)
                    pe.wait_ge(sem(f"in_x{b % 2}"), 16 * (b // 2 + 1))
                    for e in range(2):
                        for k in range(KH):
                            mm = pe.matmul(bank(key)[:, e * HID:(e + 1) * HID], xs[:, k, b % 2 * P:b % 2 * P + P],
                                           w1s[:, e, k, :], start=k == 0, stop=k == KH - 1)
                    mm.then_inc(sem("tile_full"), 1)
                    key = ("encT", b)
                    begin(key)
                    pe.wait_ge(sem("hn_ready"), 2 * (b + 1))
                    for j in range(4):
                        mm = pe.transpose(bank(key)[:, j * P:(j + 1) * P], hn[:, b % 2, j * P:(j + 1) * P], idn[:])
                    mm.then_inc(sem("tile_full"), 1)
                if s == "nodes":
                    h, np_ = a
                    pe.wait_ge(sem("h_ready"), 4 * (2 * h + 2))
                    for n in (0, 1):
                        for dp in range(2):
                            for e in range(2):
                                key = ("nodes", h, e, 2 * np_ + n, dp)
                                begin(key)
                                w = weights(st, ("W2", e, np_)).rearrange("p (k n d) -> p k n d", k=KH, n=2)
                                for d in range(2):
                                    for k in range(KH):
                                        d0 = (2 * dp + d) * P
                                        mm = pe.matmul(bank(key)[:, d * HB:(d + 1) * HB], w[:, k, n, d0:d0 + P],
                                                       hT[:, e, k, h * HB:(h + 1) * HB], start=k == 0, stop=k == KH - 1)
                                mm.then_inc(sem("tile_full"), 1)
                if s == "qk":
                    h, c = a
                    w = weights(st, ("Wqk", c)).rearrange("p (m k d) -> p m k d", m=4, k=KD)
                    if c == 0:
                        read_of(pe, ("nodes", h, 0, 3, 1))
                        read_of(pe, ("nodes", h, 1, 3, 1))
                    for np_ in range(2):
                        for mat, e in ((2, 0), (3, 1), (0, 0), (1, 1)):
                            key = ("qk", h, c, np_, ("qr", "qi", "kr", "ki")[mat])
                            begin(key)
                            for k in range(KD):
                                mm = pe.matmul(bank(key), w[:, mat, k, :], S[:, e, k, np_ * 512:(np_ + 1) * 512],
                                               start=k == 0, stop=k == KD - 1)
                            mm.then_inc(sem("tile_full"), 1)
                if s == "score":
                    h, c = a
                    read_of(pe, ("qk", h, c, 1, "qr"))
                    read_of(pe, ("qk", h, c, 1, "qi"))
                    for g in range(G):
                        key = ("score", h, c, g)
                        begin(key)
                        for x in range(2):
                            mm = pe.matmul(bank(key)[:, x * 256:(x + 1) * 256], K[:, c % 2, x, g * P:(g + 1) * P],
                                           Q[:, c % 2, x, :, g * P:(g + 1) * P], start=True, stop=True)
                        mm.then_inc(sem("tile_full"), 1)
                if s == "value":
                    h, g = a
                    for e in range(2):
                        key = ("value", h, g, e)
                        begin(key)
                        w = weights(("value", h, 0), ("Wv", e)).rearrange("p (k f) -> p k f", k=KD)
                        for k in range(KD):
                            mm = pe.matmul(bank(key), S[:, e, k, g * P:(g + 1) * P], w[:, k, :],
                                           start=k == 0, stop=k == KD - 1)
                        mm.then_inc(sem("tile_full"), 1)
                if s == "mix":
                    h, gp = a
                    read_of(pe, ("value", h, 2 * gp + 1, 0))
                    read_of(pe, ("value", h, 2 * gp + 1, 1))
                    pe.wait_ge(sem("prob_by_pool"), h * G // 2 + gp + 1)
                    pe.wait_ge(sem("prob_by_dve"), h * G // 2 + gp + 1)
                    for c in range(C):
                        key = ("mix", h, gp, c)
                        begin(key)
                        for x in range(2):
                            for g in range(2):
                                gg = 2 * gp + g
                                mm = pe.matmul(bank(key)[:, (2 * x + g) * P:(2 * x + g + 1) * P],
                                               V[:, gg, c, x * P:(x + 1) * P],
                                               PR[:, gg % 4, (2 * c + x) * 4:(2 * c + x) * 4 + 4, :], start=True, stop=True)
                        mm.then_inc(sem("tile_full"), 1)
                if s == "attn_out":
                    h, np_ = a
                    if np_ == 0:
                        read_of(pe, ("mix", h, G // 2 - 1, C - 2))
                        read_of(pe, ("mix", h, G // 2 - 1, C - 1))
                    for et in range(KD):
                        for r in range(2):
                            key = ("attn_out", h, np_, et, r)
                            begin(key)
                            w = weights(("attn_out", h, 0), ("Wo", r)).rearrange("p (k f) -> p k f", k=KD)
                            for k in range(C):
                                mm = pe.matmul(bank(key), w[:, k, et * P:(et + 1) * P], MX[:, r, k, np_ * 512:(np_ + 1) * 512],
                                               start=k == 0, stop=k == C - 1)
                            mm.then_inc(sem("tile_full"), 1)
                if s == "inter":
                    h, et, np_ = a
                    w = weights(st, ("Wint", et, np_)).rearrange("p (n r k e) -> p n r k e", n=2, r=2, k=KD)
                    if et == 0:
                        pe.wait_ge(sem("asum_ready"), h * 8 + 8)
                    for q in range(3):
                        key = ("inter", h, et, np_, q)
                        begin(key)
                        for n in range(2):
                            if q == 1:
                                pe.wait_ge(sem("dw_ready"), 2 * unit_at[(st, n)] + 2)
                            for k in range(KD):
                                if q == 0:
                                    lhs, rhs = w[:, n, 0, k, :], A[:, 2, k, 2 * np_ + n, :]
                                else:
                                    lhs = unit(st, n).rearrange("p (q k e) -> p q k e", q=2, k=KD)[:, q - 1, k, :]
                                    rhs = A[:, 2 - q, k, 2 * np_ + n, :]
                                mm = pe.matmul(bank(key)[:, n * HB:(n + 1) * HB], lhs, rhs, start=k == 0, stop=k == KD - 1)
                        mm.then_inc(sem("tile_full"), 1)
                if s == "meas":
                    (h,) = a
                    key = ("norm", h)
                    begin(key)
                    pe.wait_ge(sem("supsq_ready"), h + 1)
                    for bt in range(2):
                        for k in range(KD):
                            mm = pe.matmul(bank(key)[:, 2 * bt:2 * bt + 2], ssq1[:, k, bt * P:(bt + 1) * P], ones[:, 0:2],
                                           start=k == 0, stop=k == KD - 1)
                    mm.then_inc(sem("tile_full"), 1)
                    w = weights(st, ("M", 0)).rearrange("p (k o) -> p k o", k=KD)
                    weights(st, ("M", 1))
                    pe.wait_ge(sem("ssum_ready"), h + 1)
                    sv = ssum.rearrange("p (k b) -> p k b", k=KD)
                    for op in range(2):
                        for q in range(3):
                            key = ("meas", h, op, q)
                            begin(key)
                            if q:
                                pe.wait_ge(sem("dw_ready"), 2 * unit_at[(st, op, q - 1)] + 2)
                            for o in range(2):
                                for k in range(KD):
                                    if q == 0:
                                        lhs, rhs = w[:, k, (2 * op + o) * P:(2 * op + o + 1) * P], sv[:, k, :]
                                    else:
                                        lhs = unit(st, op, q - 1).rearrange("p (k o) -> p k o", k=KD)[:, k, o * P:(o + 1) * P]
                                        rhs = SUP[:, 2 - q, k, :]
                                    mm = pe.matmul(bank(key)[:, o * HB:(o + 1) * HB], lhs, rhs, start=k == 0, stop=k == KD - 1)
                            mm.then_inc(sem("tile_full"), 1)
                if s == "post":
                    (h,) = a
                    w = weights(st, ("Wp",)).rearrange("p (k o) -> p k o", k=KD)
                    pe.wait_ge(sem("amp_ready"), h + 1)
                    for bt in range(2):
                        key = ("post", h, bt)
                        begin(key)
                        for k in range(KD):
                            mm = pe.matmul(bank(key), ampT[:, k, bt * P:(bt + 1) * P], w[:, k, :], start=k == 0, stop=k == KD - 1)
                        mm.then_inc(sem("tile_full"), 1)

        @block.scalar
        def _(act):
            def load_x(b):
                act.dma_start(xs[:, :, b % 2 * P:b % 2 * P + P], xT[:, :, b * P:(b + 1) * P]).then_inc(sem(f"in_x{b % 2}"), 16)

            load_x(0)
            load_x(1)
            act.wait_ge(sem("in_const"), 48)
            for st in steps:
                s, a = st[0], st[1:]
                if s == "enc":
                    (b,) = a
                    act.wait_ge(sem("var_ready"), b + 1)
                    v = small[:, 0:2]
                    act.activation(small[:, 2:4], v, ACT.Abs_reciprocal_sqrt).then_inc(sem("rstd0_ready"), 1)
                    full(act, ("encT", b))
                    if b + 2 < BT:
                        load_x(b + 2)
                    for e in range(2):
                        for k in range(KH):
                            j = 2 * e + k
                            act.activation(hT[:, e, k, b * P:(b + 1) * P], bank(("encT", b))[:, j * P:(j + 1) * P], ACT.Gelu,
                                           bias=bias("bei" if e else "ber", k), scale=bias("gi" if e else "gr", k)
                                           ).then_inc(sem("h_ready"), 1)
                if s == "nodes":
                    h, np_ = a
                    for n in (2 * np_, 2 * np_ + 1):
                        for dp in range(2):
                            key = ("nodes", h, 0, n, dp)
                            full(act, key)
                            for d in range(2):
                                act.activation(S_node[:, 0, 2 * dp + d, n], bank(key)[:, d * HB:(d + 1) * HB].rearrange("p (g b) -> p g b", g=G), ACT.Identity,
                                               bias=bias("b2r", 4 * n + 2 * dp + d)).then_inc(sem("sr_ready"), 1)
                if s == "qk":
                    h, c = a
                    if h == 0 and c == 0:
                        act.wait_ge(sem("ncol_ready"), 1)
                    for np_ in range(2):
                        nn = slice(np_ * 512, (np_ + 1) * 512)
                        key = ("qk", h, c, np_, "kr")
                        full(act, key)
                        src = bank(key)
                        u = c % 2
                        act.activation(K[0:64, u, 0, nn], src[0:64], ACT.Identity, bias=bias("bkr", c, 0, 64)).then_inc(sem("qk_by_act"), 1)
                        act.activation(K[64:128, u, 1, nn], src[64:128], ACT.Identity, bias=bias("bkr", c, 64, 128)).then_inc(sem("qk_by_act"), 1)
                        key = ("qk", h, c, np_, "qr")
                        full(act, key)
                        src = bank(key)
                        act.activation(Q[0:64, u, 0, 0, nn], src[0:64], ACT.Identity, bias=bias("bqr", c, 0, 64)).then_inc(sem("qk_by_act"), 1)
                        act.activation(Q[64:128, u, 0, 1, nn], src[0:64], ACT.Identity, bias=ncol[0:64, c:c + 1], scale=-1.0).then_inc(sem("qk_by_act"), 1)
                        act.activation(Q[64:128, u, 1, 0, nn], src[64:128], ACT.Identity, bias=bias("bqr", c, 64, 128)).then_inc(sem("qk_by_act"), 1)
                        act.activation(Q[0:64, u, 1, 1, nn], src[64:128], ACT.Identity, bias=ncol[64:128, c:c + 1], scale=-1.0).then_inc(sem("qk_by_act"), 1)
                if s == "score":
                    h, c = a
                    for g in range(G):
                        i = (h * C + c) * G + g
                        full(act, ("score", h, c, g))
                        if i >= 2:
                            act.wait_ge(sem("diag_ready"), i - 1)
                        act.activation(sq[:, i % 2, :], bank(("score", h, c, g)), ACT.Square).then_inc(sem("sq_ready"), 1)
                if s == "value":
                    h, g = a
                    if g == 0 and h:
                        act.wait_ge(sem("post_v"), 16 * h)
                        act.wait_ge(sem("outs"), 32 * h)
                    key = ("value", h, g, 0)
                    full(act, key)
                    dst = V[:, g].rearrange("p c (u f) -> p c u f", u=4)[:, :, 0:4:3, :]
                    act.activation(dst, bank(key).rearrange("p (c u f) -> p c u f", c=C, u=2), ACT.Copy).then_inc(sem("vr_ready"), 1)
                if s == "softmax":
                    (h,) = a
                    act.wait_ge(sem("smx_v"), h * 6 + 1)
                    act.activation(sm[1], sm[0], ACT.Abs_reciprocal_sqrt).then_inc(sem("smx_a"), 1)
                    act.wait_ge(sem("smx_v"), h * 6 + 5)
                    act.activation(sm[5], sm[4], ACT.Exp, scale=SCALE).then_inc(sem("smx_a"), 1)
                if s == "mix":
                    h, gp = a
                    for c in range(0, C, 2):
                        key = ("mix", h, gp, c)
                        full(act, key)
                        for x, lo, r in ((0, 0, 0), (0, 64, 1), (1, 0, 1), (1, 64, 0)):
                            src = bank(key)[lo:lo + 64, x * 256:(x + 1) * 256]
                            dst = MX[lo:lo + 64, r, c, gp * 256:(gp + 1) * 256]
                            act.activation(dst, src, ACT.Identity, bias=bias("bvi" if r else "bvr", c, lo, lo + 64)).then_inc(sem("mix_by_act"), 1)
                if s == "attn_out":
                    h, np_ = a
                    for et in range(KD):
                        key = ("attn_out", h, np_, et, 0)
                        full(act, key)
                        act.activation(A_rows(0, et, np_), bank(key).rearrange("p (g n b) -> p n g b", g=4, n=N),
                                       ACT.Identity, bias=bias("bor", et)).then_inc(sem("ar_ready"), 1)
                if s == "inter":
                    h, et, np_ = a
                    key = ("inter", h, et, np_, 0)
                    full(act, key)
                    i = 2 * sup_index(h, et) + np_
                    if i:
                        act.wait_ge(sem("ri_ready"), 2 * i)
                    act.activation(k1s[:], bank(key), ACT.Copy).then_inc(sem("k1_ready"), 1)
                if s == "super":
                    h, et = a
                    q = sup_index(h, et)
                    act.wait_ge(sem("ri_ready"), 4 * q + 4)
                    if q:
                        act.wait_ge(sem("sup_v"), NV * q)
                        act.wait_ge(sem("sup_p"), NP * q)
                    act.activation(zsq[:], RI.rearrange("p r n b -> p r (n b)"), ACT.Square).then_inc(sem("sup_a"), 1)
                    act.wait_ge(sem("in_s"), 16 * h + 16)
                    act.activation(Wt[:], st_bc[:, 0:16:5, :], ACT.Copy).then_inc(sem("sup_a"), 1)
                    act.wait_ge(sem("sup_v"), NV * q + 1)
                    act.activation(y0, n2, ACT.Abs_reciprocal_sqrt).then_inc(sem("sup_a"), 1)
                    act.wait_ge(sem("sup_a"), NA * q + 3)
                    act.activation(y2, y0, ACT.Square).then_inc(sem("sup_a"), 1)
                if s == "meas":
                    (h,) = a
                    act.wait_ge(sem("sup_v"), NV * KD * (h + 1))
                    act.wait_ge(sem("sup_p"), NP * KD * (h + 1))
                    act.activation(ssq[:], SUP.rearrange("p r k b -> p r (k b)"), ACT.Square).then_inc(sem("meas_a"), 1)
                    act.wait_ge(sem("meas_v"), 5 * h + 2)
                    act.activation(small[:, 12:14], small[:, 10:12], ACT.Abs_reciprocal_sqrt).then_inc(sem("meas_a"), 1)
                    for op in range(2):
                        key = ("meas", h, op, 0)
                        full(act, key)
                        act.wait_ge(sem("ri_ready"), 4 * KD * (h + 1))
                        if op or h:
                            act.wait_ge(sem("m_ready"), 4 * h + 2 * op)
                        act.activation(k1s[:], bank(key), ACT.Copy).then_inc(sem("mk1_ready"), 1)
                    act.wait_ge(sem("m_ready"), 4 * h + 4)
                    act.wait_ge(sem("supsq_ready"), h + 1)
                    act.activation(msq[:], MRI.rearrange("p r o b -> p r (o b)"), ACT.Square).then_inc(sem("meas_a"), 1)
                    act.wait_ge(sem("amp_v"), 4 * h + 1)
                    act.activation(my, m2, ACT.Abs_reciprocal_sqrt).then_inc(sem("meas_a"), 1)
                    act.wait_ge(sem("meas_a"), 5 * h + 4)
                    act.activation(my2, my, ACT.Square).then_inc(sem("meas_a"), 1)
                if s == "post":
                    (h,) = a
                    for bt in range(2):
                        i = 2 * h + bt
                        act.wait_ge(sem("post_v"), 8 * i + 3)
                        act.activation(small[:, 26:27], small[:, 25:26], ACT.Abs_reciprocal_sqrt).then_inc(sem("post_a"), 1)
                        act.wait_ge(sem("post_v"), 8 * i + 8)
                        act.activation(pos[:, bt, :], pon[:, bt, :], ACT.Gelu).then_inc(sem("post_a"), 1)
                        act.wait_ge(sem("post_a"), 2 * i + 2)
                        act.dma_start(out[i * P:(i + 1) * P, :], pos[:, bt, :]).then_inc(sem("outs"), 16)
            act.wait_ge(sem("outs"), 16 * BT)

        @block.vector
        def _(dve):
            done = {}

            def mark(ins, name):
                done[name] = done.get(name, 0) + 1
                ins.then_inc(sem(name), 1)
                return done[name]

            def step(ins, name):
                dve.wait_ge(sem(name), mark(ins, name))

            def refine(y, x, y_, name, tmp):
                step(dve.tensor_tensor(tmp, y_, y_, ALU.mult), name)
                step(dve.scalar_tensor_tensor(tmp, tmp, -0.5, x, ALU.mult, ALU.mult), name)
                return dve.scalar_tensor_tensor(y, tmp, 1.5, y_, ALU.add, ALU.mult)

            dve.memset(ones[:], 1.0).then_inc(sem("ones_ready"), 1)
            dve.wait_ge(sem("in_const"), 48)
            dve.tensor_scalar(ncol[:], col[:, bcol["bqr"]:bcol["bqr"] + 4], -1.0, None, ALU.mult).then_inc(sem("ncol_ready"), 1)
            dve.wait_ge(sem("in_enc"), 32)
            for st in steps:
                s, a = st[0], st[1:]
                if s == "enc":
                    (b,) = a
                    u = b % 2
                    full(dve, ("enc", b))
                    dve.tensor_tensor(hs[:, u, :], bank(("enc", b)), b1s, ALU.add).then_inc(sem("enc_sum"), 1)
                    dve.wait_ge(sem("enc_sum"), b + 1)
                    for e in range(2):
                        mark(dve.bn_stats(small[:, 16 + 6 * e:22 + 6 * e], hs[:, u, e * HID:(e + 1) * HID]), "enc_v")
                    dve.wait_ge(sem("enc_v"), done["enc_v"])
                    for e in range(2):
                        mark(dve.bn_aggr(small[:, 4 + 2 * e:6 + 2 * e], small[:, 16 + 6 * e:22 + 6 * e]), "enc_v")
                    dve.wait_ge(sem("enc_v"), done["enc_v"])
                    dve.tensor_scalar(small[:, 0:2], small[:, 5:9:2], EPS, None, ALU.add).then_inc(sem("var_ready"), 1)
                    dve.wait_ge(sem("var_ready"), b + 1)
                    dve.wait_ge(sem("rstd0_ready"), b + 1)
                    step(refine(small[:, 8:10], small[:, 0:2], small[:, 2:4], "enc_v", small[:, 30:32]), "enc_v")
                    if b >= 2:
                        full(dve, ("encT", b - 2))
                    for e in range(2):
                        dve.tensor_scalar(hn[:, u, e * HID:(e + 1) * HID], hs[:, u, e * HID:(e + 1) * HID],
                                          small[:, 4 + 2 * e:5 + 2 * e], small[:, 8 + e:9 + e], ALU.subtract, ALU.mult
                                          ).then_inc(sem("hn_ready"), 1)
                    dve.wait_ge(sem("hn_ready"), 2 * b + 2)
                if s == "nodes":
                    h, np_ = a
                    for n in (2 * np_, 2 * np_ + 1):
                        for dp in range(2):
                            key = ("nodes", h, 1, n, dp)
                            full(dve, key)
                            j = bcol["b2i"] + 4 * n + 2 * dp
                            dve.tensor_tensor(S_node[:, 1, 2 * dp:2 * dp + 2, n], bank(key).rearrange("p (d g b) -> p d g b", d=2, g=G),
                                              col[:, j:j + 2].unsqueeze(2).unsqueeze(3).to_broadcast([P, 2, G, 32]), ALU.add).then_inc(sem("si_ready"), 1)
                if s == "qk":
                    h, c = a
                    u = c % 2
                    for np_ in range(2):
                        nn = slice(np_ * 512, (np_ + 1) * 512)
                        key = ("qk", h, c, np_, "ki")
                        full(dve, key)
                        src = bank(key)
                        dve.tensor_scalar(K[0:64, u, 1, nn], src[0:64], bias("bki", c, 0, 64), None, ALU.add).then_inc(sem("qk_by_dve"), 1)
                        dve.tensor_scalar(K[64:128, u, 0, nn], src[64:128], bias("bki", c, 64, 128), None, ALU.add).then_inc(sem("qk_by_dve"), 1)
                        key = ("qk", h, c, np_, "qi")
                        full(dve, key)
                        src = bank(key)
                        lo, hi = (src[0:64], bias("bqi", c, 0, 64)), (src[64:128], bias("bqi", c, 64, 128))
                        for dst, (x, bb) in ((Q[0:64, u, 1, 0, nn], lo), (Q[64:128, u, 1, 1, nn], lo),
                                             (Q[64:128, u, 0, 0, nn], hi), (Q[0:64, u, 0, 1, nn], hi)):
                            dve.tensor_scalar(dst, x, bb, None, ALU.add).then_inc(sem("qk_by_dve"), 1)
                if s == "score":
                    h, c = a
                    for g in range(G):
                        i = (h * C + c) * G + g
                        dve.wait_ge(sem("masked"), 2 * i + 2)
                        if c == 0 and g == 0 and h:
                            dve.wait_ge(sem("smx_in"), 16 * h)
                        dve.tensor_reduce(diag[:, g, c * 8:(c + 1) * 8], sq[:, i % 2, :].rearrange("p (x v n b) -> p x v n b", x=2, v=2, n=N)[:, :, 0],
                                          AX.X, ALU.add).then_inc(sem("diag_ready"), 1)
                if s == "value":
                    h, g = a
                    if g == 0 and h:
                        dve.wait_ge(sem("post_v"), 16 * h)
                        dve.wait_ge(sem("post_a"), 4 * h)
                        dve.wait_ge(sem("outs"), 32 * h)
                    key = ("value", h, g, 1)
                    full(dve, key)
                    dst = V[:, g].rearrange("p c (u f) -> p c u f", u=4)[:, :, 1:3, :]
                    src = bank(key).rearrange("p (c u f) -> p c u f", c=C, u=2)
                    dve.tensor_copy(dst, src).then_inc(sem("vi_ready"), 1)
                if s == "softmax":
                    (h,) = a
                    X0 = sm[6].rearrange("p (g m q) -> p g m q", g=2, m=4)
                    dve.wait_ge(sem("diag_ready"), (h + 1) * C * G)
                    for m in range(4):
                        for gq in range(4):
                            mark(dve.tensor_copy(X0[32 * gq:32 * gq + 32, :, m, :], diag[32 * m:32 * m + 32, gq:G:4, :]), "smx_in")
                    dve.wait_ge(sem("smx_in"), 16 * (h + 1))
                    step(dve.tensor_scalar(sm[0], sm[6], 1e-8, None, ALU.add), "smx_v")
                    dve.wait_ge(sem("smx_a"), 2 * h + 1)
                    step(refine(sm[3], sm[0], sm[1], "smx_w", sm[2]), "smx_w")
                    step(dve.tensor_tensor(sm[7], sm[0], sm[3], ALU.mult), "smx_v")
                    q4 = lambda z: z.rearrange("p (g m q) -> p g q m", g=2, m=4)
                    mx = sm[2][:, 0:64].rearrange("p (g q) -> p g q", g=2)
                    step(dve.tensor_reduce(mx, q4(sm[7]), AX.X, ALU.max), "smx_v")
                    bc = lambda z: z.unsqueeze(2).to_broadcast([P, 2, 4, 32])
                    v4 = lambda z: z.rearrange("p (g m q) -> p g m q", g=2, m=4)
                    mark(dve.tensor_tensor(v4(sm[4]), v4(sm[7]), bc(mx), ALU.subtract), "smx_v")
                    mark(dve.tensor_copy(small[:, 39:40], ones[:, 0:1]), "smx_v")
                    dve.wait_ge(sem("smx_v"), 6 * h + 5)
                    dve.wait_ge(sem("smx_a"), 2 * h + 2)
                    sums = sm[0][:, 0:64].rearrange("p (g q) -> p g q", g=2)
                    step(dve.tensor_reduce(sums, q4(sm[5]), AX.X, ALU.add), "smx_w")
                    rs = sm[1][:, 0:64].rearrange("p (g q) -> p g q", g=2)
                    step(dve.reciprocal(rs, sums), "smx_w")
                    mark(dve.tensor_tensor(v4(sm[3]), v4(sm[5]), bc(rs), ALU.mult), "smx_v")
                    dve.wait_ge(sem("smx_v"), 6 * h + 6)
                    wk = sm[6].rearrange("p (g q) -> p g q", g=G)
                    for m in range(4):
                        for gq in range(4):
                            mark(dve.tensor_copy(wk[32 * m:32 * m + 32, gq:G:4, :], v4(sm[3])[32 * gq:32 * gq + 32, :, m, :]), "smx_out")
                    dve.wait_ge(sem("smx_out"), 16 * (h + 1))
                if s == "mix":
                    h, gp = a

                    def spread(g):
                        wk = sm[6].rearrange("p (g q) -> p g q", g=G)
                        if g >= 4:
                            full(dve, ("mix", h, g // 2 - 2, C - 1))
                        dve.tensor_tensor(PR[:, g % 4], wk[:, g].unsqueeze(2).to_broadcast([P, 32, 32]),
                                          msk[:].unsqueeze(1).to_broadcast([P, 32, 32]), ALU.mult).then_inc(sem("prob_by_dve"), 1)

                    if gp == 0:
                        spread(1)
                        spread(3)
                    for c in range(1, C, 2):
                        key = ("mix", h, gp, c)
                        full(dve, key)
                        for x, lo, r in ((0, 0, 0), (0, 64, 1), (1, 0, 1), (1, 64, 0)):
                            src = bank(key)[lo:lo + 64, x * 256:(x + 1) * 256]
                            dst = MX[lo:lo + 64, r, c, gp * 256:(gp + 1) * 256]
                            dve.tensor_scalar(dst, src, bias("bvi" if r else "bvr", c, lo, lo + 64), None, ALU.add).then_inc(sem("mix_by_dve"), 1)
                    if 2 * gp + 5 < G:
                        spread(2 * gp + 5)
                if s == "attn_out":
                    h, np_ = a
                    for et in range(KD):
                        key = ("attn_out", h, np_, et, 1)
                        full(dve, key)
                        dve.tensor_scalar(A_rows(1, et, np_), bank(key).rearrange("p (g n b) -> p n g b", g=4, n=N),
                                          bias("boi", et), None, ALU.add).then_inc(sem("ai_ready"), 1)
                if s == "inter":
                    h, et, np_ = a
                    i = 2 * sup_index(h, et) + np_
                    dve.wait_ge(sem("k1_ready"), i + 1)
                    if i >= 2 and np_ == 0:
                        dve.wait_ge(sem("sup_p"), NP * sup_index(h, et))
                        dve.wait_ge(sem("sup_v"), NV * sup_index(h, et))
                    for q, op in ((1, ALU.subtract), (2, ALU.add)):
                        key = ("inter", h, et, np_, q)
                        full(dve, key)
                        dve.tensor_tensor(RI[:, q - 1, 2 * np_:2 * np_ + 2, :], k1s[:].rearrange("p (n b) -> p n b", n=2),
                                          bank(key).rearrange("p (n b) -> p n b", n=2), op).then_inc(sem("ri_ready"), 1)
                if s == "super":
                    h, et = a
                    q = sup_index(h, et)
                    dve.wait_ge(sem("sup_a"), NA * q + 1)
                    dve.wait_ge(sem("ri_ready"), 4 * q + 4)
                    mark(dve.scalar_tensor_tensor(n2, zsq[:, 0], TINY, zsq[:, 1], ALU.max, ALU.add), "sup_v")
                    dve.wait_ge(sem("sup_v"), done["sup_v"])
                    dve.wait_ge(sem("sup_a"), NA * q + 4)
                    step(dve.scalar_tensor_tensor(y2, y2, -0.5, n2, ALU.mult, ALU.mult), "sup_v")
                    step(dve.scalar_tensor_tensor(y0, y2, 1.5, y0, ALU.add, ALU.mult), "sup_v")
                    step(dve.tensor_tensor(U[:].rearrange("p r n b -> p r (n b)"), RI[:].rearrange("p r n b -> p r (n b)"),
                                           y0.unsqueeze(1).to_broadcast([P, 2, 1024]), ALU.mult), "sup_v")
                    dve.wait_ge(sem("sup_p"), NP * q + 4)
                    o = 0
                    for k in (1, 2, 3):
                        mark(dve.tensor_tensor(pr[:, :, o:o + 4 - k, :], U[:, :, 0:4 - k, :], U[:, :, k:4, :], ALU.mult), "sup_v")
                        o += 4 - k
                    dve.wait_ge(sem("sup_v"), done["sup_v"])
                    step(dve.tensor_tensor(cc[:], pr[:, 0], Eij[:], ALU.add), "sup_v")
                    step(dve.tensor_tensor(cc[:], cc[:], pr[:, 1], ALU.add), "sup_v")
                    o = 0
                    for k in (1, 2, 3):
                        low = st_bc[:, 4 * k:4 * k + 5 * (3 - k) + 1:5, :]
                        mark(dve.tensor_tensor(PL[:, o:o + 4 - k, :], cc[:, o:o + 4 - k, :], low, ALU.mult), "sup_v")
                        o += 4 - k
                    dve.wait_ge(sem("sup_v"), done["sup_v"])
                    dve.wait_ge(sem("sup_a"), NA * q + 2)
                    o = 0
                    for k in (1, 2, 3):
                        step(dve.tensor_tensor(Wt[:, 0:4 - k, :], Wt[:, 0:4 - k, :], PL[:, o:o + 4 - k, :], ALU.add), "sup_v")
                        o += 4 - k
                    dve.wait_ge(sem("sup_p"), NP * q + 7)
                    o = 0
                    for k in (1, 2, 3):
                        step(dve.tensor_tensor(Wt[:, k:4, :], Wt[:, k:4, :], PU[:, o:o + 4 - k, :], ALU.add), "sup_v")
                        o += 4 - k
                    step(dve.tensor_tensor(prod[:, 0], RI[:, 0], Wt[:], ALU.mult), "sup_v")
                    step(dve.tensor_tensor(prod[:, 0, 0:2], prod[:, 0, 0:2], prod[:, 0, 2:4], ALU.add), "sup_v")
                    mark(dve.tensor_tensor(SUP[:, 0, et], prod[:, 0, 0], prod[:, 0, 1], ALU.add), "sup_v")
                    assert done["sup_v"] == NV * (q + 1), done["sup_v"]
                if s == "meas":
                    (h,) = a
                    dve.wait_ge(sem("sup_v"), NV * KD * (h + 1))
                    dve.wait_ge(sem("sup_p"), NP * KD * (h + 1))
                    dve.tensor_tensor(ssum, SUP[:, 0].rearrange("p k b -> p (k b)"), SUP[:, 1].rearrange("p k b -> p (k b)"),
                                      ALU.add).then_inc(sem("ssum_ready"), 1)
                    dve.wait_ge(sem("meas_a"), 5 * h + 1)
                    dve.wait_ge(sem("ones_ready"), 1)
                    dve.tensor_tensor(ssq1[:].rearrange("p k b -> p (k b)"), ssq[:, 0], ssq[:, 1], ALU.add).then_inc(sem("supsq_ready"), 1)
                    key = ("norm", h)
                    full(dve, key)
                    dve.tensor_copy(small[:, 34:36], bank(key)[:, 0:4:2]).then_inc(sem("norm_read"), 1)
                    dve.wait_ge(sem("norm_read"), h + 1)
                    mark(dve.tensor_copy(small[:, 38:39], ones[:, 0:1]), "meas_v")
                    step(dve.tensor_scalar(small[:, 10:12], small[:, 34:36], 1e-8, None, ALU.add), "meas_v")
                    dve.wait_ge(sem("meas_a"), 5 * h + 2)
                    step(refine(small[:, 14:16], small[:, 10:12], small[:, 12:14], "meas_v", small[:, 32:34]), "meas_v")
                    for op in range(2):
                        dve.wait_ge(sem("mk1_ready"), 2 * h + op + 1)
                        for q, alu in ((1, ALU.subtract), (2, ALU.add)):
                            key = ("meas", h, op, q)
                            full(dve, key)
                            dve.tensor_tensor(MRI[:, q - 1, 2 * op:2 * op + 2, :], k1s[:].rearrange("p (n b) -> p n b", n=2),
                                              bank(key).rearrange("p (n b) -> p n b", n=2), alu).then_inc(sem("m_ready"), 1)
                    dve.wait_ge(sem("meas_a"), 5 * h + 3)
                    mark(dve.scalar_tensor_tensor(m2, msq[:, 0], TINY, msq[:, 1], ALU.max, ALU.add), "amp_v")
                    dve.wait_ge(sem("amp_v"), 4 * h + 1)
                    dve.wait_ge(sem("meas_a"), 5 * h + 5)
                    step(dve.scalar_tensor_tensor(my2, my2, -0.5, m2, ALU.mult, ALU.mult), "amp_v")
                    step(dve.scalar_tensor_tensor(my, my2, 1.5, my, ALU.add, ALU.mult), "amp_v")
                    dve.tensor_tensor(amp, m2, my, ALU.mult).then_inc(sem("amp_ready"), 1)
                    mark(dve.tensor_copy(small[:, 37:38], ones[:, 0:1]), "amp_v")
                    dve.wait_ge(sem("amp_ready"), h + 1)
                if s == "post":
                    (h,) = a
                    for bt in range(2):
                        i = 2 * h + bt
                        key = ("post", h, bt)
                        full(dve, key)
                        dve.wait_ge(sem("in_post"), 16 * h + 16)
                        dve.scalar_tensor_tensor(pos[:, bt, :], bank(key), small[:, 14 + bt:15 + bt], prow[:, 0], ALU.mult, ALU.add).then_inc(sem("post_sum"), 1)
                        dve.wait_ge(sem("post_sum"), i + 1)
                        step(dve.bn_stats(small[:, 16:22], pos[:, bt, :]), "post_v")
                        step(dve.bn_aggr(small[:, 23:25], small[:, 16:22]), "post_v")
                        step(dve.tensor_scalar(small[:, 25:26], small[:, 24:25], EPS, None, ALU.add), "post_v")
                        dve.wait_ge(sem("post_a"), 2 * i + 1)
                        step(refine(small[:, 27:28], small[:, 25:26], small[:, 26:27], "post_w", small[:, 28:29]), "post_w")
                        mark(dve.tensor_copy(small[:, 36:37], ones[:, 0:1]), "post_v")
                        step(dve.tensor_scalar(pon[:, bt, :], pos[:, bt, :], small[:, 23:24], small[:, 27:28], ALU.subtract, ALU.mult), "post_v")
                        step(dve.tensor_tensor(pon[:, bt, :], pon[:, bt, :], prow[:, 1], ALU.mult), "post_v")
                        mark(dve.tensor_copy(small[:, 36:37], ones[:, 0:1]), "post_w")
                        step(dve.tensor_tensor(pon[:, bt, :], pon[:, bt, :], prow[:, 2], ALU.add), "post_v")
                        mark(dve.tensor_copy(small[:, 29:30], ones[:, 0:1]), "post_v")

        @block.gpsimd
        def _(pool):
            pool.wait_ge(sem("in_const"), 48)
            derived = [0]

            def derive(n):
                st, j, _ = units[n]
                if n >= DW:
                    pool.wait_ge(sem("tile_full"), units[n - DW][2] + 1)
                if st[0] == "inter":
                    ld = ("Wint", st[2], st[3])
                    k = load_at[(st, ld)]
                    pool.wait_ge(sem(f"slot{k % SLOTS}"), 16 * (k // SLOTS + 1))
                    w = ring[:, k % SLOTS, :].rearrange("p (n r f) -> p n r f", n=2, r=2)
                    wr, wi = w[:, j, 0], w[:, j, 1]
                    d = dw[:, n % DW, :].rearrange("p (q f) -> p q f", q=2)
                    pool.tensor_tensor(d[:, 0], wr, wi, ALU.add).then_inc(sem("dw_ready"), 1)
                    pool.tensor_tensor(d[:, 1], wi, wr, ALU.subtract).then_inc(sem("dw_ready"), 1)
                else:
                    op, q = j
                    w = []
                    for r in range(2):
                        k = load_at[(st, ("M", r))]
                        pool.wait_ge(sem(f"slot{k % SLOTS}"), 16 * (k // SLOTS + 1))
                        w.append(ring[:, k % SLOTS, :].rearrange("p (k o) -> p k o", k=KD)[:, :, op * 256:(op + 1) * 256])
                    d = dw[:, n % DW, :].rearrange("p (k o) -> p k o", k=KD)
                    for half in range(2):
                        ks = slice(2 * half, 2 * half + 2)
                        if q == 0:
                            ins = pool.tensor_tensor(d[:, ks], w[0][:, ks], w[1][:, ks], ALU.add)
                        else:
                            ins = pool.tensor_tensor(d[:, ks], w[1][:, ks], w[0][:, ks], ALU.subtract)
                        ins.then_inc(sem("dw_ready"), 1)

            def derive_for(st):
                while derived[0] < len(units) and units[derived[0]][0] == st:
                    derive(derived[0])
                    derived[0] += 1

            for at_, st in enumerate(steps):
                s, a = st[0], st[1:]
                if s == "score":
                    h, c = a
                    for g in range(G):
                        i = (h * C + c) * G + g
                        v = sq[:, i % 2, :].rearrange("p (x v q) -> p x v q", x=2, v=2)
                        pool.wait_ge(sem("sq_ready"), i + 1)
                        pool.tensor_tensor(v[:, :, 0], v[:, :, 0], v[:, :, 1], ALU.add).then_inc(sem("masked"), 1)
                        pool.wait_ge(sem("masked"), 2 * i + 1)
                        m = v[:, :, 0].rearrange("p x (n b) -> p x n b", n=N)
                        pool.tensor_tensor(m, m, msk[:].unsqueeze(1).unsqueeze(1).to_broadcast([P, 2, N, 32]), ALU.mult).then_inc(sem("masked"), 1)
                if s == "mix":
                    h, gp = a

                    def spread(g):
                        wk = sm[6].rearrange("p (g q) -> p g q", g=G)
                        if g >= 4:
                            full(pool, ("mix", h, g // 2 - 2, C - 1))
                        pool.wait_ge(sem("smx_out"), 16 * (h + 1))
                        pool.tensor_tensor(PR[:, g % 4], wk[:, g].unsqueeze(2).to_broadcast([P, 32, 32]),
                                           msk[:].unsqueeze(1).to_broadcast([P, 32, 32]), ALU.mult).then_inc(sem("prob_by_pool"), 1)

                    if gp == 0:
                        spread(0)
                        spread(2)
                    if 2 * gp + 4 < G:
                        spread(2 * gp + 4)
                    if gp == G // 2 - 1:
                        full(pool, ("mix", h, G // 2 - 1, C - 1))
                        pool.dma_start(st_bc[:], strength[0:1, :, h * HB:(h + 1) * HB].to_broadcast([P, 16, HB])).then_inc(sem("in_s"), 16)
                if s == "attn_out":
                    h, np_ = a
                    if np_ == 1:
                        derive_for(("inter", h, 0, 0))
                    for et in range(KD):
                        i = (h * 2 + np_) * KD + et + 1
                        pool.wait_ge(sem("ar_ready"), i)
                        pool.wait_ge(sem("ai_ready"), i)
                        bb = slice(np_ * P, (np_ + 1) * P)
                        pool.tensor_tensor(A[:, 2, et, :, bb], A[:, 0, et, :, bb], A[:, 1, et, :, bb], ALU.add).then_inc(sem("asum_ready"), 1)
                if s == "inter":
                    h, et, np_ = a
                    derive_for(st)
                if s == "super":
                    h, et = a
                    q = sup_index(h, et)
                    if et < KD - 1:
                        derive_for(("inter", h, et + 1, 0))
                    pool.wait_ge(sem("sup_v"), NV * q + 1)
                    n2v = n2.rearrange("p (n b) -> p n b", n=N)
                    pool.tensor_scalar(Efl[:], n2v, TINY, None, ALU.is_le).then_inc(sem("sup_p"), 1)
                    pool.wait_ge(sem("sup_p"), NP * q + 1)
                    o = 0
                    for k in (1, 2, 3):
                        pool.tensor_tensor(Eij[:, o:o + 4 - k, :], Efl[:, 0:4 - k, :], Efl[:, k:4, :], ALU.add).then_inc(sem("sup_p"), 1)
                        o += 4 - k
                    pool.wait_ge(sem("sup_v"), NV * q + 9)
                    o = 0
                    for k in (1, 2, 3):
                        up = st_bc[:, k:k + 5 * (3 - k) + 1:5, :]
                        pool.tensor_tensor(PU[:, o:o + 4 - k, :], cc[:, o:o + 4 - k, :], up, ALU.mult).then_inc(sem("sup_p"), 1)
                        o += 4 - k
                    pool.wait_ge(sem("sup_v"), NV * q + 18)
                    pool.tensor_tensor(prod[:, 1], RI[:, 1], Wt[:], ALU.mult).then_inc(sem("sup_p"), 1)
                    pool.wait_ge(sem("sup_p"), NP * q + 8)
                    pool.tensor_tensor(prod[:, 1, 0:2], prod[:, 1, 0:2], prod[:, 1, 2:4], ALU.add).then_inc(sem("sup_p"), 1)
                    pool.wait_ge(sem("sup_p"), NP * q + 9)
                    pool.tensor_tensor(SUP[:, 1, et], prod[:, 1, 0], prod[:, 1, 1], ALU.add).then_inc(sem("sup_p"), 1)
                if s == "meas":
                    (h,) = a
                    derive_for(st)
                    pool.wait_ge(sem("sup_v"), NV * KD * (h + 1))
                    pool.wait_ge(sem("sup_p"), NP * KD * (h + 1))
                    pool.dma_start(prow[:], rows[0:1, 512:2048].rearrange("o (j f) -> o j f", j=3).to_broadcast([P, 3, 512])).then_inc(sem("in_post"), 16)


def kernel(r_strength, r_x, **w):
    import numpy as np
    import concourse.bacc as bacc
    from concourse.bass_utils import run_bass_kernel_spmd

    g = {k[len("L0_rec_"):]: np.asarray(v) for k, v in w.items()}

    def tiles(m):
        k, n = m.shape
        return m.reshape(k // P, P, n).transpose(1, 0, 2)

    def turned(v):
        return v.reshape(*v.shape[:-1], -1, 2, 64)[..., ::-1, :].reshape(v.shape)

    def columns(v):
        return v.reshape(-1, P).T

    def w2(m):
        m = m.T.reshape(KH, P, 2, 2, D)
        return m.transpose(1, 2, 0, 3, 4).reshape(P, 2, -1)

    qk = np.stack([tiles(m) for m in (g["Wq_r"].T, turned(g["Wq_i"].T), g["Wk_r"].T, turned(g["Wk_i"].T))], 1)
    qk = qk.reshape(P, 4, KD, C, P).transpose(0, 3, 1, 2, 4).reshape(P, C, -1)
    vi = g["Wv_i"].T
    inter = np.stack([g["int_Wr"], g["int_Wi"]], 1)
    inter = inter.reshape(2, 2, 2, KD, P, KD, P)
    inter = inter.transpose(6, 3, 0, 1, 2, 5, 4).reshape(P, KD, 2, -1)
    cols = np.concatenate(
        [columns(g["er_b2"]), columns(g["ei_b2"]), columns(g["bq_r"]), columns(turned(g["bq_i"])), columns(g["bk_r"]),
         columns(turned(g["bk_i"])), columns(g["bv_r"]), columns(turned(g["bv_i"])), columns(g["bo_r"]), columns(g["bo_i"]),
         columns(g["er_g1"]), columns(g["er_be1"]), columns(g["ei_g1"]), columns(g["ei_be1"])], 1)
    rows = np.concatenate([g["er_b1"], g["ei_b1"], g["post_b"], g["post_g"], g["post_be"]])[None, :]
    flat = lambda m: tiles(m).reshape(P, -1)
    arrays = {
        "xT": tiles(np.asarray(r_x).T),
        "w1": np.stack([tiles(g["er_W1"].T), tiles(g["ei_W1"].T)], 1),
        "w2r": w2(g["er_W2"]), "w2i": w2(g["ei_W2"]), "wqk": qk,
        "wvr": flat(g["Wv_r"].T), "wvi": flat(vi),
        "wor": flat(g["Wo_r"].T), "woi": flat(turned(g["Wo_i"]).T),
        "wint": inter, "mr": flat(g["meas_Mr"].T), "mi": flat(g["meas_Mi"].T), "wp": flat(g["post_W"].T),
        "cols": cols, "rows": rows,
        "ident": np.eye(P, dtype=np.float32),
        "mask": np.tile(np.eye(32, dtype=np.float32), (4, 1)),
        "strength": np.asarray(r_strength).reshape(B, 16).T[None],
    }
    nc = bacc.Bacc("TRN2", target_bir_lowering=False, num_devices=1)
    sent, args = {}, {}
    for name, arr in arrays.items():
        sent[f"in_{name}"] = np.ascontiguousarray(arr)
        args[name] = nc.dram_tensor(f"in_{name}", arr.shape, mybir.dt.from_np(arr.dtype), kind="ExternalInput").ap()
    out = nc.dram_tensor("out", (B, OUT), F32, kind="ExternalOutput").ap()
    build(nc, out, **args)
    r = run_bass_kernel_spmd(nc, [sent], core_ids=[0])
    return r.results[0]["out"]
```

```python
from contextlib import ExitStack

import concourse.bass as bass
from concourse import mybir

ALU = mybir.AluOpType
ACT = mybir.ActivationFunctionType
AX = mybir.AxisListType
F32 = mybir.dt.float32
BF16 = mybir.dt.bfloat16

P = 128
B, IN, HID, D, N, OUT, H = 512, 256, 256, 512, 4, 512, 8
HALVES = 2
HB = B // HALVES
BT = B // P
KH = HID // P
KD = D // P
C = H // 2
G = HB // 32
BANKS = 8
SLOTS = 3
SLOT = 2048
DW = 3
AHEAD = 2
TINY = 1e-37
EPS = 1e-5
SCALE = (D // H) ** -0.5

def timeline():
    steps = [("enc",), ("encT",)]
    for h in range(HALVES):
        steps += [("nodes", h, 0)]
        if h:
            steps += [("cosines", h - 1, KD - 1)]
        steps += [("nodes", h, 1)]
        if h:
            steps += [("super", h - 1, KD - 1)]
        steps += [("qk", h, 0)]
        if h:
            steps += [("square", h - 1), ("norm", h - 1), ("rnorm", h - 1)]
        steps += [("qk", h, 1)]
        steps += [("score", h, 0), ("qk", h, 2), ("score", h, 1), ("qk", h, 3), ("score", h, 2)]
        steps += [("value", h, 0), ("score", h, 3)]
        steps += [("value", h, g) for g in range(1, 4)]
        steps += [("softmax", h)]
        steps += [("value", h, g) for g in range(4, G)]
        steps += [("mix", h, gp) for gp in range(G // 2)]
        steps += [("attn_out", h, 0), ("attn_out", h, 1)]
        for et in range(KD):
            steps += [("inter", h, et, 0)]
            if et:
                steps += [("cosines", h, et - 1)]
            steps += [("inter", h, et, 1)]
            if et:
                steps += [("super", h, et - 1)]
    return steps + [("cosines", 1, KD - 1), ("meas", 0), ("super", 1, KD - 1), ("amp", 0), ("square", 1), ("meas", 1),
                    ("norm", 1), ("amp", 1), ("rnorm", 1), ("post", 0), ("post", 1)]


def tiles_of(step):
    s, a = step[0], step[1:]
    if s == "enc":
        return [(("enc", b), "enc_sum", 1) for b in range(BT)]
    if s == "encT":
        return [(("encT", b), "h_ready", 4) for b in range(BT)]
    if s == "nodes":
        out = []
        for n in (2 * a[1], 2 * a[1] + 1):
            for dp in range(2):
                out += [(("nodes", a[0], 0, n, dp), "sr_ready", 2), (("nodes", a[0], 1, n, dp), "si_ready", 1)]
        return out
    if s == "qk":
        out = []
        for np_ in range(2):
            for mat, sem, k in (("kr", "qk_by_act", 2), ("ki", "qk_by_dve", 2), ("qr", "qk_by_act", 4), ("qi", "qk_by_dve", 4)):
                out.append((("qk", *a, np_, mat), sem, k))
        return out
    if s == "score":
        return [(("score", *a, g), "sq_ready", 1) for g in range(G)]
    if s == "value":
        return [(("value", *a, 0), "vr_ready", 1), (("value", *a, 1), "vi_ready", 1)]
    if s == "mix":
        return [(("mix", *a, c), "mix_by_dve" if c % 2 else "mix_by_act", 4) for c in range(C)]
    if s == "attn_out":
        return [(("attn_out", *a, et, ri), "ai_ready" if ri else "ar_ready", 1) for et in range(KD) for ri in range(2)]
    if s == "inter":
        return [(("inter", *a, 0), "rr_ready", 1), (("inter", *a, 1), "rr_ready", 1), (("inter", *a, 2), "i_ready", 1)]
    if s == "norm":
        return [(("norm", *a), "norm_read", 1)]
    if s == "meas":
        out = []
        for op in range(2):
            out += [(("meas", *a, op, 0), "mrr_ready", 1), (("meas", *a, op, 1), "m_ready", 2), (("meas", *a, op, 2), "m_ready", 1)]
        return out
    if s == "post":
        return [(("post", *a, bt), "post_sum", 1) for bt in range(HB // P)]
    return []


def loads_of(step):
    s, a = step[0], step[1:]
    if s == "nodes":
        return [("W2", 0, a[1]), ("W2", 1, a[1])]
    if s == "qk":
        return [("Wqk", a[1])]
    if s == "value" and a[1] == 0:
        return [("Wv", 0), ("Wv", 1)]
    if s == "attn_out" and a[1] == 0:
        return [("Wo", 0), ("Wo", 1)]
    if s == "inter":
        return [("Wint", a[1], a[2])]
    if s == "meas" and a[0] == 0:
        return [("M", 0), ("M", 1)]
    if s == "post" and a[0] == 0:
        return [("Wp",)]
    return []


def build(nc, out, xT, w1, w2r, w2i, wqk, wvr, wvi, wor, woi, wint, mr, mi, wp, cols, rows, ident, mask, strength):
    steps = timeline()

    number, emptied, counts = {}, {}, {}
    last_tile = {}
    for st in steps:
        for key, sem, k in tiles_of(st):
            number[key] = len(number)
            counts[sem] = counts.get(sem, 0) + k
            emptied[number[key]] = (sem, counts[sem])
            last_tile[st] = number[key]

    loads, load_at = [], {}
    for st in steps:
        for ld in loads_of(st):
            key = (st, ld)
            load_at[key] = len(loads)
            loads.append([st, ld])
    last_use = []
    for st, ld in loads:
        if ld[0] == "Wv":
            last_use.append(("value", st[1], G - 1))
        elif ld[0] == "Wo":
            last_use.append(("attn_out", st[1], 1))
        else:
            last_use.append(st)

    units, unit_at = [], {}
    for st in steps:
        if st[0] == "inter" or st == ("meas", 0):
            for op in range(2 if st[0] == "meas" else 1):
                unit_at[(st, op)] = len(units)
                tile = ("meas", 1, op, 2) if st[0] == "meas" else (*st, 2)
                units.append((st, op, number[tile]))

    with ExitStack() as ctx:
        def sb(name, shape, dt=F32):
            return ctx.enter_context(nc.sbuf_tensor(name, shape, dt))

        ps = [ctx.enter_context(nc.psum_tensor(f"bank{i}", [P, 512], F32)) for i in range(BANKS)]
        sems = {}

        def sem(name):
            if name not in sems:
                sems[name] = ctx.enter_context(nc.semaphore(name))
            return sems[name]

        ring = sb("ring", [P, SLOTS, SLOT])
        dw = sb("dw", [P, DW, 1024])
        X = sb("X", [P, 12288])
        Y = sb("Y", [P, 8192])
        T = sb("T", [P, 72 * 256])
        hT = sb("hT", [P, 2, KH, B])
        sq = sb("sq", [P, 2, 512])
        diag = sb("diag", [P, G, 32])
        col = sb("col", [P, cols.shape[1]])
        ncol = sb("ncol", [P, C])
        idn = sb("idn", [P, P])
        msk = sb("msk", [P, 32])
        ones = sb("ones", [P, 2])
        small = sb("small", [P, 40])
        rnorm = sb("rnorm", [P, 2 * HALVES])
        ssum0 = sb("ssum0", [P, KD, HB])

        Q = X[:, 0:8192].rearrange("p (u h v q) -> p u h v q", u=2, h=2, v=2)
        K = X[:, 8192:12288].rearrange("p (u h q) -> p u h q", u=2, h=2)
        A = X[:].rearrange("p (r k n b) -> p r k n b", r=3, k=KD, n=N)
        S = Y[:].rearrange("p (e k q) -> p e k q", e=2, k=KD)
        S_node = Y[:].rearrange("p (e k g n b) -> p e k n g b", e=2, k=KD, g=G, n=N)
        MX = Y[:].rearrange("p (r c q) -> p r c q", r=2, c=C)

        def A_rows(r, k, rh):
            return A[:, r, k, :, rh * P:(rh + 1) * P].rearrange("p n (g b) -> p n g b", g=4)

        def t(kb, size):
            return T[:, kb * 256:kb * 256 + size]

        V = t(0, 8192).rearrange("p (g c f) -> p g c f", g=G, c=C)
        PR = t(32, 4096).rearrange("p (u q b) -> p u q b", u=4, q=32)
        sm = [t(48 + j, 256) for j in range(8)]
        st_bc = t(0, 4096).rearrange("p (s b) -> p s b", s=16)
        yq = [Y[:, j * 2048:(j + 1) * 2048] for j in range(4)]
        RI2 = [[z.rearrange("p (r n b) -> p r n b", r=2, n=N) for z in half]
               for half in ((yq[0], yq[1], yq[2], t(16, 2048)), (yq[0], yq[1], t(16, 2048), yq[0]))]
        zsq2 = [[z.rearrange("p (r q) -> p r q", r=2) for z in half]
                for half in ((yq[3], yq[3], yq[3], t(24, 2048)), (yq[2],) * KD)]
        n2 = t(32, 1024)
        y0 = t(36, 1024)
        y2 = t(40, 1024)
        pr = t(24, 3072).rearrange("p (r k b) -> p r k b", r=2, k=6)
        cc = t(36, 1536).rearrange("p (k b) -> p k b", k=6)
        prod = t(24, 2048).rearrange("p (r n b) -> p r n b", r=2, n=N)
        U = t(44, 2048).rearrange("p (r n b) -> p r n b", r=2, n=N)
        Efl = T[:, 52 * 256:54 * 256].bitcast(BF16).rearrange("p (n b) -> p n b", n=N)
        Eij = T[:, 56 * 256:59 * 256].bitcast(BF16).rearrange("p (k b) -> p k b", k=6)
        Wt, W1, W2 = (t(x, 1024).rearrange("p (n b) -> p n b", n=N) for x in (59, 24, 28))
        SUP2 = [z.rearrange("p (r k b) -> p r k b", r=2, k=KD) for z in (t(64, 2048), yq[3])]
        xs = t(0, 1024).rearrange("p (k b) -> p k b", k=2)
        w1s = t(4, 1024).rearrange("p (e k o) -> p e k o", e=2, k=2)
        b1s = t(8, 512)
        hs = t(10, 2048).rearrange("p (u f) -> p u f", u=BT)
        hn = t(18, 2048).rearrange("p (u f) -> p u f", u=BT)
        stat = t(26, 48).rearrange("p (u e s) -> p u e s", u=BT, e=2)
        aggr = t(27, 16).rearrange("p (u e s) -> p u e s", u=BT, e=2)
        ev = [t(28 + j, 8).rearrange("p (u e) -> p u e", u=BT) for j in range(4)]
        ssq = t(24, 2048).rearrange("p (r q) -> p r q", r=2)
        ssq1 = t(32, 1024).rearrange("p (k b) -> p k b", k=KD)
        MRI2 = [X[:, j * 2048:(j + 1) * 2048].rearrange("p (r o b) -> p r o b", r=2, o=KD) for j in (0, 1)]
        msq = X[:, 4096:6144].rearrange("p (r q) -> p r q", r=2)
        m2, my, my2 = (X[:, j * 1024:(j + 1) * 1024] for j in (6, 7, 8))
        amp2 = [X[:, j * 1024:(j + 1) * 1024] for j in (9, 10)]
        ssum2 = [ssum0[:], X[:, 11264:12288].rearrange("p (k b) -> p k b", k=KD)]
        prow = t(24, 1536).rearrange("p (j f) -> p j f", j=3)
        pos = t(0, 2048).rearrange("p (u f) -> p u f", u=BT)
        pon = t(8, 2048).rearrange("p (u f) -> p u f", u=BT)

        bcol = {}
        at = 0
        for name, k in (("b2r", 16), ("b2i", 16), ("bqr", 4), ("bqi", 4), ("bkr", 4), ("bki", 4), ("bvr", 4),
                        ("bvi", 4), ("bor", 4), ("boi", 4), ("gr", 2), ("ber", 2), ("gi", 2), ("bei", 2)):
            bcol[name] = at
            at += k

        def bias(name, j, lo=0, hi=P):
            return col[lo:hi, bcol[name] + j:bcol[name] + j + 1]

        def slot(st, ld):
            return ring[:, load_at[(st, ld)] % SLOTS, :]

        def unit(*key):
            return dw[:, unit_at[key] % DW, :]

        def bank(key):
            return ps[number[key] % BANKS][:, :]

        def full(eng, key):
            eng.wait_ge(sem("tile_full"), number[key] + 1)

        def read_of(eng, key):
            s, n = emptied[number[key]]
            eng.wait_ge(sem(s), n)

        NV, NA, NP, NR = 18, 3, 7, 3
        sup_index = lambda h, et: h * KD + et

        def superposed(eng, tiles):
            eng.wait_ge(sem("sup_v"), NV * tiles)
            eng.wait_ge(sem("sup_p"), NP * tiles)
            eng.wait_ge(sem("sup_r"), NR * tiles)

        def weighted(eng, dst, k, up):
            o = (0, 3, 5)[k - 1]
            s_ij = st_bc[:, k:k + 5 * (3 - k) + 1:5, :] if up else st_bc[:, 4 * k:4 * k + 5 * (3 - k) + 1:5, :]
            return eng.tensor_tensor(dst[:, k:N] if up else dst[:, 0:N - k], cc[:, o:o + N - k, :], s_ij, ALU.mult)

        def weighted_sum(eng, h, et, r, name, before):
            z = prod[:, r]
            eng.tensor_tensor(z, RI2[h][et][:, r], Wt[:], ALU.mult).then_inc(sem(name), 1)
            eng.wait_ge(sem(name), before + 1)
            eng.tensor_tensor(z[:, 0:2], z[:, 0:2], z[:, 2:4], ALU.add).then_inc(sem(name), 1)
            eng.wait_ge(sem(name), before + 2)
            eng.tensor_tensor(SUP2[h][:, r, et], z[:, 0], z[:, 1], ALU.add).then_inc(sem(name), 1)

        def ssum(eng, h, et):
            ks = slice(0, KD) if et is None else slice(et, et + 1)
            s2 = ssum2[h]
            if h:
                full(eng, ("inter", h, KD - 1, 1, 2))
                superposed(eng, sup_index(h, et) + 1)
            eng.tensor_tensor(s2[:, ks], SUP2[h][:, 0, ks], SUP2[h][:, 1, ks], ALU.add).then_inc(sem("ssum_ready"), 1)

        block = ctx.enter_context(nc.Block())

        @block.sync
        def _(sp):
            sp.dma_start(w1s, w1).then_inc(sem("in_enc"), 16)
            sp.dma_start(b1s, rows[0:1, 0:512].to_broadcast([P, 512])).then_inc(sem("in_b1"), 16)
            sp.dma_start(col[:], cols).then_inc(sem("in_const"), 16)
            sp.dma_start(idn[:], ident).then_inc(sem("in_const"), 16)
            sp.dma_start(msk[:], mask).then_inc(sem("in_const"), 16)
            src = {"W2": lambda e, np_: (w2r, w2i)[e][:, np_, :], "Wqk": lambda c: wqk[:, c, :],
                   "Wv": lambda r: (wvr, wvi)[r], "Wo": lambda r: (wor, woi)[r],
                   "Wint": lambda et, np_: wint[:, et, np_, :], "M": lambda r: (mr, mi)[r], "Wp": lambda: wp}
            for n, (st, ld) in enumerate(loads):
                if n >= SLOTS:
                    sp.wait_ge(sem("tile_full"), last_tile[last_use[n - SLOTS]] + 1)
                    if last_use[n - SLOTS][0] == "inter":
                        sp.wait_ge(sem("dw_ready"), max(v for k, v in unit_at.items() if k[0] == last_use[n - SLOTS]) + 1)
                sp.dma_start(ring[:, n % SLOTS, :], src[ld[0]](*ld[1:])).then_inc(sem(f"slot{n % SLOTS}"), 16)

        @block.tensor
        def _(pe):
            seen = set()

            def begin(key):
                n = number[key]
                if n >= BANKS:
                    s, k = emptied[n - BANKS]
                    pe.wait_ge(sem(s), k)

            def norm(h):
                key = ("norm", h)
                begin(key)
                pe.wait_ge(sem("supsq_ready"), h + 1)
                for bt in range(2):
                    for k in range(KD):
                        mm = pe.matmul(bank(key)[:, 2 * bt:2 * bt + 2], ssq1[:, k, bt * P:(bt + 1) * P], ones[:, 0:2],
                                       start=k == 0, stop=k == KD - 1)
                mm.then_inc(sem("tile_full"), 1)

            def measure(h, op, q, ks, w):
                if q == 2 and h == 0:
                    pe.wait_ge(sem("dw_ready"), unit_at[(("meas", 0), op)] + 1)
                for k in ks:
                    for o in range(2):
                        if q < 2:
                            lhs, rhs = w[q][:, k, (2 * op + o) * P:(2 * op + o + 1) * P], SUP2[h][:, q, k, :]
                        else:
                            lhs = unit(("meas", 0), op).rearrange("p (k o) -> p k o", k=KD)[:, k, o * P:(o + 1) * P]
                            rhs = ssum2[h][:, k, :]
                        mm = pe.matmul(bank(("meas", h, op, q))[:, o * HB:(o + 1) * HB], lhs, rhs,
                                       start=k == 0 and o == 0, stop=k == KD - 1 and o == 1)
                if KD - 1 in ks:
                    mm.then_inc(sem("tile_full"), 1)

            def weights(st, ld):
                n = load_at[(st, ld)]
                if n not in seen:
                    seen.add(n)
                    pe.wait_ge(sem(f"slot{n % SLOTS}"), 16 * (n // SLOTS + 1))
                return slot(st, ld)

            for st in steps:
                s, a = st[0], st[1:]
                if s == "enc":
                    pe.wait_ge(sem("in_enc"), 16)
                    pe.wait_ge(sem("in_x"), 16)
                    for b in range(BT):
                        key = ("enc", b)
                        for e in range(2):
                            for k in range(KH):
                                mm = pe.matmul(bank(key)[:, e * HID:(e + 1) * HID], xs[:, k, b * P:(b + 1) * P],
                                               w1s[:, e, k, :], start=k == 0, stop=k == KH - 1)
                        mm.then_inc(sem("tile_full"), 1)
                    pe.wait_ge(sem("in_const"), 48)
                if s == "encT":
                    for b in range(BT):
                        key = ("encT", b)
                        begin(key)
                        pe.wait_ge(sem("hn_ready"), 2 * (b + 1))
                        for j in range(4):
                            mm = pe.transpose(bank(key)[:, j * P:(j + 1) * P], hn[:, b, j * P:(j + 1) * P], idn[:])
                        mm.then_inc(sem("tile_full"), 1)
                if s == "nodes":
                    h, np_ = a
                    pe.wait_ge(sem("h_ready"), 4 * (2 * h + 2))
                    for n in (0, 1):
                        for dp in range(2):
                            for e in range(2):
                                key = ("nodes", h, e, 2 * np_ + n, dp)
                                begin(key)
                                w = weights(st, ("W2", e, np_)).rearrange("p (k n d) -> p k n d", k=KH, n=2)
                                for d in range(2):
                                    for k in range(KH):
                                        d0 = (2 * dp + d) * P
                                        mm = pe.matmul(bank(key)[:, d * HB:(d + 1) * HB], w[:, k, n, d0:d0 + P],
                                                       hT[:, e, k, h * HB:(h + 1) * HB], start=k == 0, stop=k == KH - 1)
                                mm.then_inc(sem("tile_full"), 1)
                if s == "qk":
                    h, c = a
                    w = weights(st, ("Wqk", c)).rearrange("p (m k d) -> p m k d", m=4, k=KD)
                    if c == 0:
                        read_of(pe, ("nodes", h, 0, 3, 1))
                        read_of(pe, ("nodes", h, 1, 3, 1))
                    for np_ in range(2):
                        for mat, e in ((2, 0), (3, 1), (0, 0), (1, 1)):
                            key = ("qk", h, c, np_, ("qr", "qi", "kr", "ki")[mat])
                            begin(key)
                            for k in range(KD):
                                mm = pe.matmul(bank(key), w[:, mat, k, :], S[:, e, k, np_ * 512:(np_ + 1) * 512],
                                               start=k == 0, stop=k == KD - 1)
                            mm.then_inc(sem("tile_full"), 1)
                if s == "score":
                    h, c = a
                    read_of(pe, ("qk", h, c, 1, "qr"))
                    read_of(pe, ("qk", h, c, 1, "qi"))
                    for g in range(G):
                        key = ("score", h, c, g)
                        begin(key)
                        for x in range(2):
                            mm = pe.matmul(bank(key)[:, x * 256:(x + 1) * 256], K[:, c % 2, x, g * P:(g + 1) * P],
                                           Q[:, c % 2, x, :, g * P:(g + 1) * P], start=True, stop=True)
                        mm.then_inc(sem("tile_full"), 1)
                if s == "value":
                    h, g = a
                    for e in range(2):
                        key = ("value", h, g, e)
                        begin(key)
                        w = weights(("value", h, 0), ("Wv", e)).rearrange("p (k f) -> p k f", k=KD)
                        for k in range(KD):
                            mm = pe.matmul(bank(key), S[:, e, k, g * P:(g + 1) * P], w[:, k, :],
                                           start=k == 0, stop=k == KD - 1)
                        mm.then_inc(sem("tile_full"), 1)
                if s == "mix":
                    h, gp = a
                    read_of(pe, ("value", h, 2 * gp + 1, 0))
                    read_of(pe, ("value", h, 2 * gp + 1, 1))
                    pe.wait_ge(sem("prob_by_pool"), h * G // 2 + gp + 1)
                    pe.wait_ge(sem("prob_by_dve"), h * G // 2 + gp + 1)
                    for c in range(C):
                        key = ("mix", h, gp, c)
                        begin(key)
                        for x in range(2):
                            for g in range(2):
                                gg = 2 * gp + g
                                mm = pe.matmul(bank(key)[:, (2 * x + g) * P:(2 * x + g + 1) * P],
                                               V[:, gg, c, x * P:(x + 1) * P],
                                               PR[:, gg % 4, (2 * c + x) * 4:(2 * c + x) * 4 + 4, :], start=True, stop=True)
                        mm.then_inc(sem("tile_full"), 1)
                if s == "attn_out":
                    h, np_ = a
                    if np_ == 0:
                        read_of(pe, ("mix", h, G // 2 - 1, C - 2))
                        read_of(pe, ("mix", h, G // 2 - 1, C - 1))
                    for et in range(KD):
                        for r in range(2):
                            key = ("attn_out", h, np_, et, r)
                            begin(key)
                            w = weights(("attn_out", h, 0), ("Wo", r)).rearrange("p (k f) -> p k f", k=KD)
                            for k in range(C):
                                mm = pe.matmul(bank(key), w[:, k, et * P:(et + 1) * P], MX[:, r, k, np_ * 512:(np_ + 1) * 512],
                                               start=k == 0, stop=k == C - 1)
                            mm.then_inc(sem("tile_full"), 1)
                if s == "inter":
                    h, et, np_ = a
                    w = weights(st, ("Wint", et, np_)).rearrange("p (n r k e) -> p n r k e", n=2, r=2, k=KD)
                    if et == 0:
                        read_of(pe, ("attn_out", h, 1, KD - 1, 0))
                        read_of(pe, ("attn_out", h, 1, KD - 1, 1))
                    for q in range(3):
                        key = ("inter", h, et, np_, q)
                        begin(key)
                        if q == 2:
                            pe.wait_ge(sem("dw_ready"), unit_at[(st, 0)] + 1)
                            if et == 0:
                                pe.wait_ge(sem("asum_ready"), h * 8 + 8)
                        for n in range(2):
                            for k in range(KD):
                                lhs = w[:, n, q, k, :] if q < 2 else unit(st, 0).rearrange("p (n k e) -> p n k e", n=2, k=KD)[:, n, k, :]
                                rhs = A[:, q, k, 2 * np_ + n, :]
                                mm = pe.matmul(bank(key)[:, n * HB:(n + 1) * HB], lhs, rhs, start=k == 0, stop=k == KD - 1)
                        mm.then_inc(sem("tile_full"), 1)
                if s == "norm":
                    norm(*a)
                if s == "meas":
                    (h,) = a
                    w = [weights(("meas", 0), ("M", r)).rearrange("p (k o) -> p k o", k=KD) for r in range(2)]
                    parts = [(op, q) for op in range(2) for q in range(3)]
                    if h == 0:
                        pe.wait_ge(sem("ssum_ready"), 1)
                        for op, q in parts:
                            begin(("meas", h, op, q))
                            measure(h, op, q, range(KD), w)
                    else:
                        superposed(pe, 2 * KD - 1)
                        pe.wait_ge(sem("ssum_ready"), 1 + KD - 1)
                        for op, q in parts:
                            begin(("meas", h, op, q))
                            measure(h, op, q, range(KD - 1), w)
                        superposed(pe, 2 * KD)
                        pe.wait_ge(sem("ssum_ready"), 1 + KD)
                        for op, q in parts:
                            measure(h, op, q, range(KD - 1, KD), w)
                if s == "post":
                    (h,) = a
                    w = weights(("post", 0), ("Wp",)).rearrange("p (k o) -> p k o", k=KD)
                    pe.wait_ge(sem("amp_ready"), h + 1)
                    for bt in range(2):
                        key = ("post", h, bt)
                        begin(key)
                        for k in range(KD):
                            mm = pe.matmul(bank(key), amp2[h].rearrange("p (k b) -> p k b", k=KD)[:, k, bt * P:(bt + 1) * P], w[:, k, :], start=k == 0, stop=k == KD - 1)
                        mm.then_inc(sem("tile_full"), 1)

        @block.scalar
        def _(act):
            act.dma_start(xs[:], xT).then_inc(sem("in_x"), 16)
            act.wait_ge(sem("in_const"), 48)
            for st in steps:
                s, a = st[0], st[1:]
                if s == "enc":
                    act.wait_ge(sem("var_ready"), 1)
                    act.activation(ev[1][:], ev[0][:], ACT.Abs_reciprocal_sqrt).then_inc(sem("rstd0_ready"), 1)
                if s == "encT":
                    for b in range(BT):
                        full(act, ("encT", b))
                        for e in range(2):
                            for k in range(KH):
                                j = 2 * e + k
                                act.activation(hT[:, e, k, b * P:(b + 1) * P], bank(("encT", b))[:, j * P:(j + 1) * P], ACT.Gelu,
                                               bias=bias("bei" if e else "ber", k), scale=bias("gi" if e else "gr", k)
                                               ).then_inc(sem("h_ready"), 1)
                if s == "nodes":
                    h, np_ = a
                    if h and np_ == 0:
                        superposed(act, sup_index(h - 1, KD - 2) + 1)
                    for n in (2 * np_, 2 * np_ + 1):
                        for dp in range(2):
                            key = ("nodes", h, 0, n, dp)
                            full(act, key)
                            for d in range(2):
                                act.activation(S_node[:, 0, 2 * dp + d, n], bank(key)[:, d * HB:(d + 1) * HB].rearrange("p (g b) -> p g b", g=G), ACT.Identity,
                                               bias=bias("b2r", 4 * n + 2 * dp + d)).then_inc(sem("sr_ready"), 1)
                if s == "qk":
                    h, c = a
                    if h == 0 and c == 0:
                        act.wait_ge(sem("ncol_ready"), 1)
                    for np_ in range(2):
                        nn = slice(np_ * 512, (np_ + 1) * 512)
                        key = ("qk", h, c, np_, "kr")
                        full(act, key)
                        src = bank(key)
                        u = c % 2
                        act.activation(K[0:64, u, 0, nn], src[0:64], ACT.Identity, bias=bias("bkr", c, 0, 64)).then_inc(sem("qk_by_act"), 1)
                        act.activation(K[64:128, u, 1, nn], src[64:128], ACT.Identity, bias=bias("bkr", c, 64, 128)).then_inc(sem("qk_by_act"), 1)
                        key = ("qk", h, c, np_, "qr")
                        full(act, key)
                        src = bank(key)
                        act.activation(Q[0:64, u, 0, 0, nn], src[0:64], ACT.Identity, bias=bias("bqr", c, 0, 64)).then_inc(sem("qk_by_act"), 1)
                        act.activation(Q[64:128, u, 0, 1, nn], src[0:64], ACT.Identity, bias=ncol[0:64, c:c + 1], scale=-1.0).then_inc(sem("qk_by_act"), 1)
                        act.activation(Q[64:128, u, 1, 0, nn], src[64:128], ACT.Identity, bias=bias("bqr", c, 64, 128)).then_inc(sem("qk_by_act"), 1)
                        act.activation(Q[0:64, u, 1, 1, nn], src[64:128], ACT.Identity, bias=ncol[64:128, c:c + 1], scale=-1.0).then_inc(sem("qk_by_act"), 1)
                if s == "score":
                    h, c = a
                    if h and c == 0:
                        act.wait_ge(sem("r_ready"), 2 * KD * h)
                    for g in range(G):
                        i = (h * C + c) * G + g
                        full(act, ("score", h, c, g))
                        if i >= 2:
                            act.wait_ge(sem("diag_ready"), i - 1)
                        act.activation(sq[:, i % 2, :], bank(("score", h, c, g)), ACT.Square).then_inc(sem("sq_ready"), 1)
                if s == "value":
                    h, g = a
                    if g == 0 and h:
                        superposed(act, KD * h)
                        act.wait_ge(sem("supsq_ready"), h)
                        read_of(act, ("norm", h - 1))
                    key = ("value", h, g, 0)
                    full(act, key)
                    dst = V[:, g].rearrange("p c (u f) -> p c u f", u=4)[:, :, 0:4:3, :]
                    act.activation(dst, bank(key).rearrange("p (c u f) -> p c u f", c=C, u=2), ACT.Copy).then_inc(sem("vr_ready"), 1)
                if s == "softmax":
                    (h,) = a
                    act.wait_ge(sem("smx_v"), h * 6 + 1)
                    act.activation(sm[1], sm[0], ACT.Abs_reciprocal_sqrt).then_inc(sem("smx_a"), 1)
                    act.wait_ge(sem("smx_v"), h * 6 + 5)
                    act.activation(sm[5], sm[4], ACT.Exp, scale=SCALE).then_inc(sem("smx_a"), 1)
                if s == "mix":
                    h, gp = a
                    for c in range(0, C, 2):
                        key = ("mix", h, gp, c)
                        full(act, key)
                        for x, lo, r in ((0, 0, 0), (0, 64, 1), (1, 0, 1), (1, 64, 0)):
                            src = bank(key)[lo:lo + 64, x * 256:(x + 1) * 256]
                            dst = MX[lo:lo + 64, r, c, gp * 256:(gp + 1) * 256]
                            act.activation(dst, src, ACT.Identity, bias=bias("bvi" if r else "bvr", c, lo, lo + 64)).then_inc(sem("mix_by_act"), 1)
                if s == "attn_out":
                    h, np_ = a
                    for et in range(KD):
                        key = ("attn_out", h, np_, et, 0)
                        full(act, key)
                        act.activation(A_rows(0, et, np_), bank(key).rearrange("p (g n b) -> p n g b", g=4, n=N),
                                       ACT.Identity, bias=bias("bor", et)).then_inc(sem("ar_ready"), 1)
                if s == "inter":
                    h, et, np_ = a
                    i = 2 * sup_index(h, et) + np_
                    for q in range(2):
                        full(act, ("inter", h, et, np_, q))
                        if q == 0:
                            if i >= 2:
                                act.wait_ge(sem("r_ready"), i - 1)
                            if et == 0:
                                act.wait_ge(sem("diag_ready"), (h + 1) * C * G)
                            dst = sq[:, i % 2, :].rearrange("p (n b) -> p n b", n=2)
                        else:
                            if np_ == 0 and sup_index(h, et) >= 3:
                                superposed(act, sup_index(h, et) - 2)
                            dst = RI2[h][et][:, 0, 2 * np_:2 * np_ + 2, :]
                        act.activation(dst, bank(("inter", h, et, np_, q)).rearrange("p (n b) -> p n b", n=2), ACT.Copy).then_inc(sem("rr_ready"), 1)
                if s == "cosines":
                    h, et = a
                    q = sup_index(h, et)
                    RI = RI2[h][et]
                    act.wait_ge(sem("r_ready"), 2 * q + 2)
                    act.wait_ge(sem("i_ready"), 2 * q + 2)
                    if q:
                        if (h, et) == (0, KD - 1):
                            superposed(act, q)
                        else:
                            act.wait_ge(sem("sup_v"), NV * (q - 1) + 1)
                    act.activation(zsq2[h][et], RI.rearrange("p r n b -> p r (n b)"), ACT.Square).then_inc(sem("sup_a"), 1)
                    act.wait_ge(sem("sup_v"), NV * q + 1)
                    act.activation(y0, n2, ACT.Abs_reciprocal_sqrt).then_inc(sem("sup_a"), 1)
                    act.wait_ge(sem("sup_a"), NA * q + 2)
                    act.activation(y2, y0, ACT.Square).then_inc(sem("sup_a"), 1)
                if s == "square":
                    (h,) = a
                    superposed(act, KD * (h + 1))
                    act.activation(ssq[:], SUP2[h].rearrange("p r k b -> p r (k b)"), ACT.Square).then_inc(sem("norm_a"), 1)
                if s == "rnorm":
                    (h,) = a
                    act.wait_ge(sem("norm_v"), 4 * h + 1)
                    act.activation(small[:, 12:14], small[:, 10:12], ACT.Abs_reciprocal_sqrt).then_inc(sem("norm_a"), 1)
                if s == "meas":
                    (h,) = a
                    for op in range(2):
                        key = ("meas", h, op, 0)
                        full(act, key)
                        if h == 0:
                            act.wait_ge(sem("r_ready"), 2 * KD * HALVES)
                        else:
                            act.wait_ge(sem("m_ready"), 3 * op + 3)
                        act.activation(sq[:, op, :], bank(key), ACT.Copy).then_inc(sem("mrr_ready"), 1)
                if s == "amp":
                    (h,) = a
                    act.wait_ge(sem("m_ready"), 6 * h + 6)
                    if h:
                        act.wait_ge(sem("amp_v"), 1)
                    act.activation(msq[:], MRI2[h].rearrange("p r o b -> p r (o b)"), ACT.Square).then_inc(sem("amp_a"), 1)
                    act.wait_ge(sem("amp_v"), 3 * h + 1)
                    act.activation(my, m2, ACT.Abs_reciprocal_sqrt).then_inc(sem("amp_a"), 1)
                    act.wait_ge(sem("amp_a"), 3 * h + 2)
                    act.activation(my2, my, ACT.Square).then_inc(sem("amp_a"), 1)
                if s == "post":
                    (h,) = a
                    act.wait_ge(sem("post_w"), 4 * h + 1)
                    act.activation(small[:, 20 + 2 * h:22 + 2 * h], small[:, 16 + 2 * h:18 + 2 * h], ACT.Abs_reciprocal_sqrt).then_inc(sem("post_a"), 1)
                    for bt in range(2):
                        i = 2 * h + bt
                        act.wait_ge(sem("post_v"), i + 1)
                        act.activation(pos[:, i, :], pon[:, i, :], ACT.Gelu).then_inc(sem("post_a"), 1)
                        act.wait_ge(sem("post_a"), 3 * h + bt + 2)
                        act.dma_start(out[i * P:(i + 1) * P, :], pos[:, i, :]).then_inc(sem("outs"), 16)
            act.wait_ge(sem("outs"), 16 * BT)

        @block.vector
        def _(dve):
            done = {}

            def mark(ins, name):
                done[name] = done.get(name, 0) + 1
                ins.then_inc(sem(name), 1)
                return done[name]

            def step(ins, name):
                dve.wait_ge(sem(name), mark(ins, name))

            def refine(y, x, y_, name, tmp):
                step(dve.tensor_tensor(tmp, y_, y_, ALU.mult), name)
                step(dve.scalar_tensor_tensor(tmp, tmp, -0.5, x, ALU.mult, ALU.mult), name)
                return dve.scalar_tensor_tensor(y, tmp, 1.5, y_, ALU.add, ALU.mult)

            def rnorms(h):
                full(dve, ("norm", h))
                dve.tensor_copy(small[:, 34:36], bank(("norm", h))[:, 0:4:2]).then_inc(sem("norm_read"), 1)
                dve.wait_ge(sem("norm_read"), h + 1)
                step(dve.tensor_scalar(small[:, 10:12], small[:, 34:36], 1e-8, None, ALU.add), "norm_v")
                dve.wait_ge(sem("norm_a"), 2 * h + 2)
                step(refine(rnorm[:, 2 * h:2 * h + 2], small[:, 10:12], small[:, 12:14], "norm_v", small[:, 34:36]), "norm_v")

            def complex_parts(dst, u, key, name, before):
                halves = lambda z: z.rearrange("p (n b) -> p n b", n=2)
                rr = halves(sq[:, u, :])
                full(dve, (*key, 1))
                dve.tensor_tensor(dst[:, 0], rr, halves(bank((*key, 1))), ALU.subtract).then_inc(sem(name), 1)
                dve.tensor_tensor(dst[:, 1], rr, halves(bank((*key, 1))), ALU.add).then_inc(sem(name), 1)
                full(dve, (*key, 2))
                dve.wait_ge(sem(name), before + 2)
                dve.tensor_tensor(dst[:, 1], halves(bank((*key, 2))), dst[:, 1], ALU.subtract).then_inc(sem(name), 1)

            dve.memset(ones[:], 1.0).then_inc(sem("ones_ready"), 1)
            dve.wait_ge(sem("in_b1"), 16)
            dve.wait_ge(sem("in_const"), 48)
            dve.tensor_scalar(ncol[:], col[:, bcol["bqr"]:bcol["bqr"] + 4], -1.0, None, ALU.mult).then_inc(sem("ncol_ready"), 1)
            for st in steps:
                s, a = st[0], st[1:]
                if s == "enc":
                    for b in range(BT):
                        full(dve, ("enc", b))
                        dve.tensor_tensor(hs[:, b, :], bank(("enc", b)), b1s, ALU.add).then_inc(sem("enc_sum"), 1)
                        dve.wait_ge(sem("enc_sum"), b + 1)
                        for e in range(2):
                            mark(dve.bn_stats(stat[:, b, e, :], hs[:, b, e * HID:(e + 1) * HID]), "enc_v")
                    dve.wait_ge(sem("enc_v"), done["enc_v"])
                    for b in range(BT):
                        for e in range(2):
                            mark(dve.bn_aggr(aggr[:, b, e, :], stat[:, b, e, :]), "enc_v")
                    dve.wait_ge(sem("enc_v"), done["enc_v"])
                    dve.tensor_scalar(ev[0][:], aggr[:, :, :, 1], EPS, None, ALU.add).then_inc(sem("var_ready"), 1)
                    dve.wait_ge(sem("var_ready"), 1)
                    dve.wait_ge(sem("rstd0_ready"), 1)
                    step(refine(ev[2][:], ev[0][:], ev[1][:], "enc_v", ev[3][:]), "enc_v")
                    for b in range(BT):
                        for e in range(2):
                            dve.tensor_scalar(hn[:, b, e * HID:(e + 1) * HID], hs[:, b, e * HID:(e + 1) * HID],
                                              aggr[:, b, e, 0:1], ev[2][:, b, e:e + 1], ALU.subtract, ALU.mult
                                              ).then_inc(sem("hn_ready"), 1)
                if s == "nodes":
                    h, np_ = a
                    if h and np_ == 0:
                        superposed(dve, sup_index(h - 1, KD - 2) + 1)
                    for n in (2 * np_, 2 * np_ + 1):
                        for dp in range(2):
                            key = ("nodes", h, 1, n, dp)
                            full(dve, key)
                            j = bcol["b2i"] + 4 * n + 2 * dp
                            dve.tensor_tensor(S_node[:, 1, 2 * dp:2 * dp + 2, n], bank(key).rearrange("p (d g b) -> p d g b", d=2, g=G),
                                              col[:, j:j + 2].unsqueeze(2).unsqueeze(3).to_broadcast([P, 2, G, 32]), ALU.add).then_inc(sem("si_ready"), 1)
                if s == "qk":
                    h, c = a
                    u = c % 2
                    for np_ in range(2):
                        nn = slice(np_ * 512, (np_ + 1) * 512)
                        key = ("qk", h, c, np_, "ki")
                        full(dve, key)
                        src = bank(key)
                        dve.tensor_scalar(K[0:64, u, 1, nn], src[0:64], bias("bki", c, 0, 64), None, ALU.add).then_inc(sem("qk_by_dve"), 1)
                        dve.tensor_scalar(K[64:128, u, 0, nn], src[64:128], bias("bki", c, 64, 128), None, ALU.add).then_inc(sem("qk_by_dve"), 1)
                        key = ("qk", h, c, np_, "qi")
                        full(dve, key)
                        src = bank(key)
                        lo, hi = (src[0:64], bias("bqi", c, 0, 64)), (src[64:128], bias("bqi", c, 64, 128))
                        for dst, (x, bb) in ((Q[0:64, u, 1, 0, nn], lo), (Q[64:128, u, 1, 1, nn], lo),
                                             (Q[64:128, u, 0, 0, nn], hi), (Q[0:64, u, 0, 1, nn], hi)):
                            dve.tensor_scalar(dst, x, bb, None, ALU.add).then_inc(sem("qk_by_dve"), 1)
                if s == "score":
                    h, c = a
                    for g in range(G):
                        i = (h * C + c) * G + g
                        dve.wait_ge(sem("masked"), 2 * i + 2)
                        if c == 0 and g == 0 and h:
                            dve.wait_ge(sem("smx_in"), 16 * h)
                        dve.tensor_reduce(diag[:, g, c * 8:(c + 1) * 8], sq[:, i % 2, :].rearrange("p (x v n b) -> p x v n b", x=2, v=2, n=N)[:, :, 0],
                                          AX.X, ALU.add).then_inc(sem("diag_ready"), 1)
                if s == "value":
                    h, g = a
                    if g == 0 and h:
                        superposed(dve, KD * h)
                        read_of(dve, ("norm", h - 1))
                    key = ("value", h, g, 1)
                    full(dve, key)
                    dst = V[:, g].rearrange("p c (u f) -> p c u f", u=4)[:, :, 1:3, :]
                    src = bank(key).rearrange("p (c u f) -> p c u f", c=C, u=2)
                    dve.tensor_copy(dst, src).then_inc(sem("vi_ready"), 1)
                if s == "softmax":
                    (h,) = a
                    X0 = sm[6].rearrange("p (g m q) -> p g m q", g=2, m=4)
                    dve.wait_ge(sem("diag_ready"), (h + 1) * C * G)
                    for m in range(4):
                        for gq in range(4):
                            mark(dve.tensor_copy(X0[32 * gq:32 * gq + 32, :, m, :], diag[32 * m:32 * m + 32, gq:G:4, :]), "smx_in")
                    dve.wait_ge(sem("smx_in"), 16 * (h + 1))
                    step(dve.tensor_scalar(sm[0], sm[6], 1e-8, None, ALU.add), "smx_v")
                    dve.wait_ge(sem("smx_a"), 2 * h + 1)
                    step(refine(sm[3], sm[0], sm[1], "smx_w", sm[2]), "smx_w")
                    step(dve.tensor_tensor(sm[7], sm[0], sm[3], ALU.mult), "smx_v")
                    q4 = lambda z: z.rearrange("p (g m q) -> p g q m", g=2, m=4)
                    mx = sm[2][:, 0:64].rearrange("p (g q) -> p g q", g=2)
                    step(dve.tensor_reduce(mx, q4(sm[7]), AX.X, ALU.max), "smx_v")
                    bc = lambda z: z.unsqueeze(2).to_broadcast([P, 2, 4, 32])
                    v4 = lambda z: z.rearrange("p (g m q) -> p g m q", g=2, m=4)
                    mark(dve.tensor_tensor(v4(sm[4]), v4(sm[7]), bc(mx), ALU.subtract), "smx_v")
                    mark(dve.tensor_copy(small[:, 39:40], ones[:, 0:1]), "smx_v")
                    dve.wait_ge(sem("smx_v"), 6 * h + 5)
                    dve.wait_ge(sem("smx_a"), 2 * h + 2)
                    sums = sm[0][:, 0:64].rearrange("p (g q) -> p g q", g=2)
                    step(dve.tensor_reduce(sums, q4(sm[5]), AX.X, ALU.add), "smx_w")
                    rs = sm[1][:, 0:64].rearrange("p (g q) -> p g q", g=2)
                    step(dve.reciprocal(rs, sums), "smx_w")
                    mark(dve.tensor_tensor(v4(sm[3]), v4(sm[5]), bc(rs), ALU.mult), "smx_v")
                    dve.wait_ge(sem("smx_v"), 6 * h + 6)
                    wk = sm[6].rearrange("p (g q) -> p g q", g=G)
                    for m in range(4):
                        for gq in range(4):
                            mark(dve.tensor_copy(wk[32 * m:32 * m + 32, gq:G:4, :], v4(sm[3])[32 * gq:32 * gq + 32, :, m, :]), "smx_out")
                    dve.wait_ge(sem("smx_out"), 16 * (h + 1))
                if s == "mix":
                    h, gp = a

                    def spread(g):
                        wk = sm[6].rearrange("p (g q) -> p g q", g=G)
                        if g >= 4:
                            full(dve, ("mix", h, g // 2 - 2, C - 1))
                        dve.tensor_tensor(PR[:, g % 4], wk[:, g].unsqueeze(2).to_broadcast([P, 32, 32]),
                                          msk[:].unsqueeze(1).to_broadcast([P, 32, 32]), ALU.mult).then_inc(sem("prob_by_dve"), 1)

                    if gp == 0:
                        spread(1)
                        spread(3)
                    for c in range(1, C, 2):
                        key = ("mix", h, gp, c)
                        full(dve, key)
                        for x, lo, r in ((0, 0, 0), (0, 64, 1), (1, 0, 1), (1, 64, 0)):
                            src = bank(key)[lo:lo + 64, x * 256:(x + 1) * 256]
                            dst = MX[lo:lo + 64, r, c, gp * 256:(gp + 1) * 256]
                            dve.tensor_scalar(dst, src, bias("bvi" if r else "bvr", c, lo, lo + 64), None, ALU.add).then_inc(sem("mix_by_dve"), 1)
                    if 2 * gp + 5 < G:
                        spread(2 * gp + 5)
                if s == "attn_out":
                    h, np_ = a
                    for et in range(KD):
                        key = ("attn_out", h, np_, et, 1)
                        full(dve, key)
                        dve.tensor_scalar(A_rows(1, et, np_), bank(key).rearrange("p (g n b) -> p n g b", g=4, n=N),
                                          bias("boi", et), None, ALU.add).then_inc(sem("ai_ready"), 1)
                if s == "inter":
                    h, et, np_ = a
                    i = 2 * sup_index(h, et) + np_
                    dve.wait_ge(sem("rr_ready"), 2 * i + 2)
                    if np_ == 0 and sup_index(h, et) >= 3:
                        superposed(dve, sup_index(h, et) - 2)
                    R, I = (RI2[h][et][:, r, 2 * np_:2 * np_ + 2, :] for r in range(2))
                    dve.tensor_tensor(I, sq[:, i % 2, :].rearrange("p (n b) -> p n b", n=2), R, ALU.add).then_inc(sem("rr_ii_ready"), 1)
                    full(dve, ("inter", h, et, np_, 2))
                    dve.wait_ge(sem("rr_ii_ready"), i + 1)
                    dve.tensor_tensor(I, bank(("inter", h, et, np_, 2)).rearrange("p (n b) -> p n b", n=2), I, ALU.subtract).then_inc(sem("i_ready"), 1)
                if s == "cosines":
                    h, et = a
                    q = sup_index(h, et)
                    RI = RI2[h][et]
                    dve.wait_ge(sem("sup_a"), NA * q + 1)
                    dve.wait_ge(sem("r_ready"), 2 * q + 2)
                    dve.wait_ge(sem("i_ready"), 2 * q + 2)
                    zsq = zsq2[h][et]
                    mark(dve.scalar_tensor_tensor(n2, zsq[:, 0], TINY, zsq[:, 1], ALU.max, ALU.add), "sup_v")
                    dve.wait_ge(sem("sup_v"), done["sup_v"])
                    step(dve.tensor_scalar(Efl[:], n2.rearrange("p (n b) -> p n b", n=N), TINY, None, ALU.is_le), "sup_v")
                    o = 0
                    for k in (1, 2, 3):
                        mark(dve.tensor_tensor(Eij[:, o:o + 4 - k, :], Efl[:, 0:4 - k, :], Efl[:, k:4, :], ALU.add), "sup_v")
                        o += 4 - k
                    dve.wait_ge(sem("sup_v"), NV * q + 5)
                    dve.wait_ge(sem("sup_a"), NA * q + 3)
                    step(dve.scalar_tensor_tensor(y2, y2, -0.5, n2, ALU.mult, ALU.mult), "sup_v")
                    step(dve.scalar_tensor_tensor(y0, y2, 1.5, y0, ALU.add, ALU.mult), "sup_v")
                    step(dve.tensor_tensor(U[:].rearrange("p r n b -> p r (n b)"), RI[:].rearrange("p r n b -> p r (n b)"),
                                           y0.unsqueeze(1).to_broadcast([P, 2, 1024]), ALU.mult), "sup_v")
                    if q:
                        superposed(dve, q)
                    mark(dve.tensor_tensor(pr[:, :, 0:3, :], U[:, :, 0:3, :], U[:, :, 1:4, :], ALU.mult), "sup_v")
                    mark(dve.tensor_tensor(pr[:, :, 3:5, :], U[:, :, 0:2, :], U[:, :, 2:4, :], ALU.mult), "sup_v")
                    dve.wait_ge(sem("sup_v"), done["sup_v"])
                    dve.wait_ge(sem("sup_p"), NP * q + 1)
                    step(dve.tensor_tensor(cc[:], pr[:, 0], Eij[:], ALU.add), "sup_v")
                    step(dve.tensor_tensor(cc[:], cc[:], pr[:, 1], ALU.add), "sup_v")
                if s == "super":
                    h, et = a
                    q = sup_index(h, et)
                    RI = RI2[h][et]
                    if q:
                        superposed(dve, q)
                    dve.wait_ge(sem("in_s"), 16 * h + 16)
                    mark(weighted(dve, Wt, 1, False), "sup_v")
                    mark(weighted(dve, W1, 2, False), "sup_v")
                    mark(weighted(dve, W2, 3, False), "sup_v")
                    dve.wait_ge(sem("sup_v"), done["sup_v"])
                    dve.wait_ge(sem("sup_p"), NP * q + 2)
                    step(dve.tensor_tensor(Wt[:], Wt[:], st_bc[:, 0:16:5, :], ALU.add), "sup_v")
                    dve.wait_ge(sem("sup_p"), NP * q + 3)
                    step(dve.tensor_tensor(Wt[:], Wt[:], W1[:], ALU.add), "sup_v")
                    dve.wait_ge(sem("sup_p"), NP * q + 4)
                    step(dve.tensor_tensor(Wt[:], Wt[:], W2[:], ALU.add), "sup_v")
                    assert done["sup_v"] == NV * (q + 1), done["sup_v"]
                    if et == KD - 1:
                        weighted_sum(dve, h, et, 0, "sup_r", NR * q)
                        if h:
                            ssum(dve, h, et)
                if s == "square":
                    (h,) = a
                    if h == 0:
                        superposed(dve, KD)
                        ssum(dve, h, None)
                    dve.wait_ge(sem("norm_a"), 2 * h + 1)
                    dve.tensor_tensor(ssq1[:].rearrange("p k b -> p (k b)"), ssq[:, 0], ssq[:, 1], ALU.add).then_inc(sem("supsq_ready"), 1)
                if s == "rnorm":
                    rnorms(*a)
                if s == "meas":
                    (h,) = a
                    for op in range(2):
                        dve.wait_ge(sem("mrr_ready"), 2 * h + op + 1)
                        complex_parts(MRI2[h][:, :, 2 * op:2 * op + 2, :], op, ("meas", h, op), "m_ready", 6 * h + 3 * op)
                if s == "amp":
                    (h,) = a
                    dve.wait_ge(sem("amp_a"), 3 * h + 1)
                    step(dve.scalar_tensor_tensor(m2, msq[:, 0], TINY, msq[:, 1], ALU.max, ALU.add), "amp_v")
                    dve.wait_ge(sem("amp_a"), 3 * h + 3)
                    step(dve.scalar_tensor_tensor(my2, my2, -0.5, m2, ALU.mult, ALU.mult), "amp_v")
                    step(dve.scalar_tensor_tensor(my, my2, 1.5, my, ALU.add, ALU.mult), "amp_v")
                    dve.tensor_tensor(amp2[h], m2, my, ALU.mult).then_inc(sem("amp_ready"), 1)
                    dve.wait_ge(sem("amp_ready"), h + 1)
                if s == "post":
                    (h,) = a
                    dve.wait_ge(sem("in_post"), 16)
                    for bt in range(2):
                        i = 2 * h + bt
                        key = ("post", h, bt)
                        full(dve, key)
                        dve.scalar_tensor_tensor(pos[:, i, :], bank(key), rnorm[:, i:i + 1], prow[:, 0], ALU.mult, ALU.add).then_inc(sem("post_sum"), 1)
                        dve.wait_ge(sem("post_sum"), i + 1)
                        step(dve.bn_stats(small[:, 28:34], pos[:, i, :]), "post_s")
                        step(dve.bn_aggr(small[:, 2 * i:2 * i + 2], small[:, 28:34]), "post_s")
                    var, r0, rstd = (small[:, x + 2 * h:x + 2 * h + 2] for x in (16, 20, 24))
                    step(dve.tensor_scalar(var, small[:, 4 * h + 1:4 * h + 4:2], EPS, None, ALU.add), "post_w")
                    dve.wait_ge(sem("post_a"), 3 * h + 1)
                    step(refine(rstd, var, r0, "post_w", small[:, 34:36]), "post_w")
                    for bt in range(2):
                        i = 2 * h + bt
                        step(dve.tensor_scalar(pon[:, i, :], pos[:, i, :], small[:, 2 * i:2 * i + 1], rstd[:, bt:bt + 1], ALU.subtract, ALU.mult), "post_n")
                        step(dve.tensor_tensor(pon[:, i, :], pon[:, i, :], prow[:, 1], ALU.mult), "post_n")
                        step(dve.tensor_tensor(pon[:, i, :], pon[:, i, :], prow[:, 2], ALU.add), "post_v")

        @block.gpsimd
        def _(pool):
            pool.wait_ge(sem("in_const"), 48)
            derived = [0]

            def derive(n):
                st, j, _ = units[n]
                if n >= DW:
                    pool.wait_ge(sem("tile_full"), units[n - DW][2] + 1)
                part = []
                for ld in loads_of(st):
                    k = load_at[(st, ld)]
                    pool.wait_ge(sem(f"slot{k % SLOTS}"), 16 * (k // SLOTS + 1))
                    w = ring[:, k % SLOTS, :]
                    if st[0] == "inter":
                        w = w.rearrange("p (n r f) -> p n r f", n=2, r=2)
                        part = [w[:, :, 0], w[:, :, 1]]
                    else:
                        part.append(w.rearrange("p (k o) -> p k o", k=KD)[:, :, j * 256:(j + 1) * 256])
                d = dw[:, n % DW, :].rearrange("p (a f) -> p a f", a=part[0].shape[1])
                pool.tensor_tensor(d, part[0], part[1], ALU.add).then_inc(sem("dw_ready"), 1)

            def derive_upto(n):
                while derived[0] <= n:
                    derive(derived[0])
                    derived[0] += 1

            for at_, st in enumerate(steps):
                s, a = st[0], st[1:]
                if s == "score":
                    h, c = a
                    for g in range(G):
                        i = (h * C + c) * G + g
                        v = sq[:, i % 2, :].rearrange("p (x v q) -> p x v q", x=2, v=2)
                        pool.wait_ge(sem("sq_ready"), i + 1)
                        pool.tensor_tensor(v[:, :, 0], v[:, :, 0], v[:, :, 1], ALU.add).then_inc(sem("masked"), 1)
                        pool.wait_ge(sem("masked"), 2 * i + 1)
                        m = v[:, :, 0].rearrange("p x (n b) -> p x n b", n=N)
                        pool.tensor_tensor(m, m, msk[:].unsqueeze(1).unsqueeze(1).to_broadcast([P, 2, N, 32]), ALU.mult).then_inc(sem("masked"), 1)
                if s == "mix":
                    h, gp = a

                    def spread(g):
                        wk = sm[6].rearrange("p (g q) -> p g q", g=G)
                        if g >= 4:
                            full(pool, ("mix", h, g // 2 - 2, C - 1))
                        pool.wait_ge(sem("smx_out"), 16 * (h + 1))
                        pool.tensor_tensor(PR[:, g % 4], wk[:, g].unsqueeze(2).to_broadcast([P, 32, 32]),
                                           msk[:].unsqueeze(1).to_broadcast([P, 32, 32]), ALU.mult).then_inc(sem("prob_by_pool"), 1)

                    if gp == 0:
                        spread(0)
                        spread(2)
                    if 2 * gp + 4 < G:
                        spread(2 * gp + 4)
                    if gp == G // 2 - 1:
                        full(pool, ("mix", h, G // 2 - 1, C - 1))
                        pool.dma_start(st_bc[:], strength[0:1, :, h * HB:(h + 1) * HB].to_broadcast([P, 16, HB])).then_inc(sem("in_s"), 16)
                if s == "attn_out":
                    h, np_ = a
                    for et in range(KD):
                        i = (h * 2 + np_) * KD + et + 1
                        pool.wait_ge(sem("ar_ready"), i)
                        pool.wait_ge(sem("ai_ready"), i)
                        bb = slice(np_ * P, (np_ + 1) * P)
                        pool.tensor_tensor(A[:, 2, et, :, bb], A[:, 0, et, :, bb], A[:, 1, et, :, bb], ALU.add).then_inc(sem("asum_ready"), 1)
                    if np_ == 0:
                        derive_upto(unit_at[(("inter", h, 0, 0), 0)])
                if s == "inter":
                    h, et, np_ = a
                    if (et, np_) == (KD - 1, 1) and h == HALVES - 1:
                        derive_upto(len(units) - 1)
                    derive_upto(min(unit_at[(st, 0)] + AHEAD, unit_at[(("inter", h, KD - 1, 1), 0)]))
                    i = 2 * sup_index(h, et) + np_
                    R = RI2[h][et][:, 0, 2 * np_:2 * np_ + 2, :]
                    pool.wait_ge(sem("rr_ii_ready"), i + 1)
                    pool.tensor_tensor(R, sq[:, i % 2, :].rearrange("p (n b) -> p n b", n=2), R, ALU.subtract).then_inc(sem("r_ready"), 1)
                if s == "cosines":
                    h, et = a
                    q = sup_index(h, et)
                    pool.wait_ge(sem("sup_v"), NV * q + 8)
                    if q:
                        superposed(pool, q)
                    pool.tensor_tensor(pr[:, :, 5, :], U[:, :, 0, :], U[:, :, 3, :], ALU.mult).then_inc(sem("sup_p"), 1)
                if s == "super":
                    h, et = a
                    q = sup_index(h, et)
                    pool.wait_ge(sem("sup_v"), NV * q + 12)
                    pool.wait_ge(sem("in_s"), 16 * h + 16)
                    if q:
                        superposed(pool, q)
                    for dst, k, up in ((Wt, 3, True), (W1, 2, True), (W2, 1, True)):
                        weighted(pool, dst, k, up).then_inc(sem("sup_p"), 1)
                    pool.wait_ge(sem("sup_v"), NV * (q + 1))
                    if et < KD - 1:
                        weighted_sum(pool, h, et, 0, "sup_r", NR * q)
                    weighted_sum(pool, h, et, 1, "sup_p", NP * q + 4)
                if s == "amp" and a[0] == 0:
                    superposed(pool, HALVES * KD)
                    pool.wait_ge(sem("supsq_ready"), HALVES)
                    pool.dma_start(prow[:], rows[0:1, 512:2048].rearrange("o (j f) -> o j f", j=3).to_broadcast([P, 3, 512])).then_inc(sem("in_post"), 16)
                if s == "meas" and a[0] == 0:
                    for et in range(KD - 1):
                        ssum(pool, 1, et)


def kernel(r_strength, r_x, **w):
    import numpy as np
    import concourse.bacc as bacc
    from concourse.bass_utils import run_bass_kernel_spmd

    g = {k[len("L0_rec_"):]: np.asarray(v) for k, v in w.items()}

    def tiles(m):
        k, n = m.shape
        return m.reshape(k // P, P, n).transpose(1, 0, 2)

    def turned(v):
        return v.reshape(*v.shape[:-1], -1, 2, 64)[..., ::-1, :].reshape(v.shape)

    def columns(v):
        return v.reshape(-1, P).T

    def w2(m):
        m = m.T.reshape(KH, P, 2, 2, D)
        return m.transpose(1, 2, 0, 3, 4).reshape(P, 2, -1)

    qk = np.stack([tiles(m) for m in (g["Wq_r"].T, turned(g["Wq_i"].T), g["Wk_r"].T, turned(g["Wk_i"].T))], 1)
    qk = qk.reshape(P, 4, KD, C, P).transpose(0, 3, 1, 2, 4).reshape(P, C, -1)
    vi = g["Wv_i"].T
    inter = np.stack([g["int_Wr"], g["int_Wi"]], 1)
    inter = inter.reshape(2, 2, 2, KD, P, KD, P)
    inter = inter.transpose(6, 3, 0, 1, 2, 5, 4).reshape(P, KD, 2, -1)
    cols = np.concatenate(
        [columns(g["er_b2"]), columns(g["ei_b2"]), columns(g["bq_r"]), columns(turned(g["bq_i"])), columns(g["bk_r"]),
         columns(turned(g["bk_i"])), columns(g["bv_r"]), columns(turned(g["bv_i"])), columns(g["bo_r"]), columns(g["bo_i"]),
         columns(g["er_g1"]), columns(g["er_be1"]), columns(g["ei_g1"]), columns(g["ei_be1"])], 1)
    rows = np.concatenate([g["er_b1"], g["ei_b1"], g["post_b"], g["post_g"], g["post_be"]])[None, :]
    flat = lambda m: tiles(m).reshape(P, -1)
    arrays = {
        "xT": tiles(np.asarray(r_x).T),
        "w1": np.stack([tiles(g["er_W1"].T), tiles(g["ei_W1"].T)], 1),
        "w2r": w2(g["er_W2"]), "w2i": w2(g["ei_W2"]), "wqk": qk,
        "wvr": flat(g["Wv_r"].T), "wvi": flat(vi),
        "wor": flat(g["Wo_r"].T), "woi": flat(turned(g["Wo_i"]).T),
        "wint": inter, "mr": flat(g["meas_Mr"].T), "mi": flat(g["meas_Mi"].T), "wp": flat(g["post_W"].T),
        "cols": cols, "rows": rows,
        "ident": np.eye(P, dtype=np.float32),
        "mask": np.tile(np.eye(32, dtype=np.float32), (4, 1)),
        "strength": np.asarray(r_strength).reshape(B, 16).T[None],
    }
    nc = bacc.Bacc("TRN2", target_bir_lowering=False, num_devices=1)
    sent, args = {}, {}
    for name, arr in arrays.items():
        sent[f"in_{name}"] = np.ascontiguousarray(arr)
        args[name] = nc.dram_tensor(f"in_{name}", arr.shape, mybir.dt.from_np(arr.dtype), kind="ExternalInput").ap()
    out = nc.dram_tensor("out", (B, OUT), F32, kind="ExternalOutput").ap()
    build(nc, out, **args)
    r = run_bass_kernel_spmd(nc, [sent], core_ids=[0])
    return r.results[0]["out"]
```

```python
from contextlib import ExitStack

import concourse.bass as bass
from concourse import mybir

ALU = mybir.AluOpType
ACT = mybir.ActivationFunctionType
AX = mybir.AxisListType
F32 = mybir.dt.float32
F32R = mybir.dt.float32r
BF16 = mybir.dt.bfloat16

P = 128
B, IN, HID, D, N, OUT, H = 512, 256, 256, 512, 4, 512, 8
HALVES = 2
HB = B // HALVES
BT = B // P
KH = HID // P
KD = D // P
C = H // 2
G = HB // 32
BANKS = 8
SLOTS = 3
SLOT = 2048
SOFTMAX_AT = 2
SPLITS = 4
DW = 3
AHEAD = 2
TINY = 1e-37
EPS = 1e-5
SCALE = (D // H) ** -0.5

def timeline():
    steps = [("enc",), ("encT",)]
    for h in range(HALVES):
        steps += [("nodes", h, 0)]
        steps += [("nodes", h, 1)]
        if h:
            steps += [("cosines", h - 1, KD - 1)]
        steps += [("k", h, 0)]
        if h:
            steps += [("super", h - 1, KD - 1)]
        steps += [("q", h, 0)]
        if h:
            steps += [("square", h - 1)]
        steps += [("k", h, 1), ("q", h, 1)]
        if h:
            steps += [("norm", h - 1), ("rnorm", h - 1)]
        steps += [("score", h, 0), ("k", h, 2), ("q", h, 2), ("score", h, 1), ("k", h, 3), ("q", h, 3), ("score", h, 2)]
        steps += [("value", h, 0, 0), ("score", h, 3)]
        steps += [("value", h, 0, g) for g in range(1, G)]
        steps += [("value", h, 1, g) for g in range(SOFTMAX_AT)]
        steps += [("softmax", h)]
        steps += [("value", h, 1, g) for g in range(SOFTMAX_AT, G)]
        steps += [("mix", h, gp) for gp in range(G // 2)]
        steps += [("attn_out", h, 0), ("attn_out", h, 1)]
        for et in range(KD):
            steps += [("inter", h, et, 0)]
            if et:
                steps += [("cosines", h, et - 1)]
            steps += [("inter", h, et, 1)]
            if et:
                steps += [("super", h, et - 1)]
    return steps + [("cosines", 1, KD - 1), ("meas", 0), ("super", 1, KD - 1), ("amp", 0), ("square", 1), ("meas", 1),
                    ("norm", 1), ("amp", 1), ("rnorm", 1), ("post", 0), ("post", 1)]


def tiles_of(step):
    s, a = step[0], step[1:]
    if s == "enc":
        return [(("enc", b), "enc_sum", 1) for b in range(BT)]
    if s == "encT":
        return [(("encT", b), "h_ready", 4) for b in range(BT)]
    if s == "nodes":
        return [(("nodes", *a, n, dp), "s_lo_ready", 2) for n in range(N) for dp in range(2)]
    if s in ("k", "q"):
        k = 2 if s == "k" else 4
        return [(("qk", *a, np_, s + p), sem, k) for np_ in range(2) for p, sem in (("r", "qk_by_act"), ("i", "qk_by_dve"))]
    if s == "score":
        return [(("score", *a, g), "sq_ready", 1) for g in range(G)]
    if s == "value":
        return [(("value", *a), "vi_ready" if a[1] else "vr_ready", 1)]
    if s == "mix":
        return [(("mix", *a, c), "mix_by_dve" if c % 2 else "mix_by_act", 4) for c in range(C)]
    if s == "attn_out":
        return [(("attn_out", *a, et, ri), "ai_ready" if ri else "ar_ready", 1) for et in range(KD) for ri in range(2)]
    if s == "inter":
        return [(("inter", *a, 0), "rr_ready", 1), (("inter", *a, 1), "rr_ready", 1), (("inter", *a, 2), "i_ready", 1)]
    if s == "norm":
        return [(("norm", *a), "norm_read", 1)]
    if s == "meas":
        out = []
        for op in range(2):
            out += [(("meas", *a, op, 0), "mrr_ready", 1), (("meas", *a, op, 1), "mrr_ready", 1), (("meas", *a, op, 2), "mi_ready", 1)]
        return out
    if s == "post":
        return [(("post", *a, bt), "post_sum", 1) for bt in range(HB // P)]
    return []


def loads_of(step):
    s, a = step[0], step[1:]
    if s == "nodes":
        return [("W2", a[1], 0), ("W2", a[1], 1)]
    if s == "k":
        return [("Wqk", a[1])]
    if s == "value" and a[2] == 0:
        return [("Wv", a[1])]
    if s == "attn_out" and a[1] == 0:
        return [("Wo", 0), ("Wo", 1)]
    if s == "inter":
        return [("Wint", a[1], a[2])]
    if s == "meas" and a[0] == 0:
        return [("M", 0), ("M", 1)]
    if s == "post" and a[0] == 0:
        return [("Wp",)]
    return []


def build(nc, out, xT, w1, w2r, w2i, wqk, wvr, wvi, wor, woi, wint, mr, mi, wp, cols, rows, ident, mask, strength):
    steps = timeline()

    number, emptied, counts = {}, {}, {}
    last_tile = {}
    for st in steps:
        for key, sem, k in tiles_of(st):
            number[key] = len(number)
            counts[sem] = counts.get(sem, 0) + k
            emptied[number[key]] = (sem, counts[sem])
            last_tile[st] = number[key]

    loads, load_at = [], {}
    for st in steps:
        for ld in loads_of(st):
            key = (st, ld)
            load_at[key] = len(loads)
            loads.append([st, ld])
    last_use = []
    for st, ld in loads:
        if ld[0] == "Wo":
            last_use.append(("attn_out", st[1], 1))
        else:
            last_use.append(st)

    splits, split_at = [], {}
    for st, ld in loads:
        if st[0] in ("k", "value"):
            for j in range(2):
                split_at[(st, j)] = len(splits)
                if st[0] == "k":
                    last = number[("qk", st[1], st[2], 1, "qi" if j else "ki")]
                else:
                    last = number[("value", st[1], st[2], G - 1)]
                splits.append((st, ld, j, last))
    splits_half = len(splits) // HALVES
    assert splits_half % SPLITS == 0

    units, unit_at = [], {}
    for st in steps:
        if st[0] == "inter" or st == ("meas", 0):
            for op in range(2 if st[0] == "meas" else 1):
                unit_at[(st, op)] = len(units)
                tile = ("meas", 1, op, 2) if st[0] == "meas" else (*st, 2)
                units.append((st, op, number[tile]))

    with ExitStack() as ctx:
        def sb(name, shape, dt=F32):
            return ctx.enter_context(nc.sbuf_tensor(name, shape, dt))

        ps = [ctx.enter_context(nc.psum_tensor(f"bank{i}", [P, 512], F32)) for i in range(BANKS)]
        sems = {}

        def sem(name):
            if name not in sems:
                sems[name] = ctx.enter_context(nc.semaphore(name))
            return sems[name]

        ring = sb("ring", [P, SLOTS, SLOT])
        regions = (("X", [P, 12288]),
                   ("Y", [P, 8192]),
                   ("T", [P, 72 * 256]),
                   ("dw", [P, DW, 1024]))
        with ExitStack() as first:
            X, Y, T, dw = (first.enter_context(nc.sbuf_tensor(n, shape, F32)) for n, shape in regions)
        Xs, Ys, Ts, dws = (sb(n + "_split", shape, F32R) for n, shape in regions)
        hT = sb("hT", [P, 2, KH, B])
        sq = sb("sq", [P, 2, 512])
        diag = sb("diag", [P, G, 32])
        col = sb("col", [P, cols.shape[1]])
        ncol = sb("ncol", [P, C])
        idn = sb("idn", [P, P])
        msk = sb("msk", [P, 32])
        ones = sb("ones", [P, 2])
        small = sb("small", [P, 40])
        rnorm = sb("rnorm", [P, 2 * HALVES])
        ssum0 = sb("ssum0", [P, KD, HB])

        Q = T[:, 0:8192].rearrange("p (u h v q) -> p u h v q", u=2, h=2, v=2)
        K = [T[:, x * 256:x * 256 + 2048].rearrange("p (h q) -> p h q", h=2) for x in (44, 32)]
        A = X[:].rearrange("p (r k n b) -> p r k n b", r=3, k=KD, n=N)
        S = [z[:, 0:8192].rearrange("p (e k q) -> p e k q", e=2, k=KD) for z in (Ys, Xs)]
        S_node = [z[:, 0:8192].rearrange("p (e k g n b) -> p e k n g b", e=2, k=KD, g=G, n=N) for z in (Ys, Xs)]
        split_ring = [z.rearrange("p (s f) -> p s f", s=2) for z in
                      (Xs[:, 8192:10240], Xs[:, 10240:12288], dws[:, 1:3, :].rearrange("p a f -> p (a f)"), Ts[:, 56 * 256:64 * 256])]
        MX = Y[:].rearrange("p (r c q) -> p r c q", r=2, c=C)

        def A_rows(r, k, rh):
            return A[:, r, k, :, rh * P:(rh + 1) * P].rearrange("p n (g b) -> p n g b", g=4)

        def t(kb, size):
            return T[:, kb * 256:kb * 256 + size]

        V = t(0, 8192).rearrange("p (g c f) -> p g c f", g=G, c=C)
        PR = t(32, 4096).rearrange("p (u q b) -> p u q b", u=4, q=32)
        sm = [t(48 + j, 256) for j in range(8)]
        st_bc = t(0, 4096).rearrange("p (s b) -> p s b", s=16)
        yq = [Y[:, j * 2048:(j + 1) * 2048] for j in range(4)]
        RI2 = [[z.rearrange("p (r n b) -> p r n b", r=2, n=N) for z in half]
               for half in ((yq[0], yq[1], yq[2], t(16, 2048)), (yq[0], yq[1], t(16, 2048), yq[0]))]
        zsq2 = [[z.rearrange("p (r q) -> p r q", r=2) for z in half]
                for half in ((yq[3], yq[3], yq[3], t(24, 2048)), (yq[2],) * KD)]
        n2 = t(32, 1024)
        y0 = t(36, 1024)
        y2 = t(40, 1024)
        pr = t(24, 3072).rearrange("p (r k b) -> p r k b", r=2, k=6)
        cc = t(36, 1536).rearrange("p (k b) -> p k b", k=6)
        prod = t(24, 2048).rearrange("p (r n b) -> p r n b", r=2, n=N)
        U = t(44, 2048).rearrange("p (r n b) -> p r n b", r=2, n=N)
        Efl = T[:, 52 * 256:54 * 256].bitcast(BF16).rearrange("p (n b) -> p n b", n=N)
        Eij = T[:, 56 * 256:59 * 256].bitcast(BF16).rearrange("p (k b) -> p k b", k=6)
        Wt, W1, W2 = (t(x, 1024).rearrange("p (n b) -> p n b", n=N) for x in (59, 24, 28))
        SUP2 = [z.rearrange("p (r k b) -> p r k b", r=2, k=KD) for z in (t(64, 2048), yq[3])]
        xs = t(0, 1024).rearrange("p (k b) -> p k b", k=2)
        w1s = t(4, 1024).rearrange("p (e k o) -> p e k o", e=2, k=2)
        b1s = t(8, 512)
        hs = t(10, 2048).rearrange("p (u f) -> p u f", u=BT)
        hn = t(18, 2048).rearrange("p (u f) -> p u f", u=BT)
        stat = t(26, 48).rearrange("p (u e s) -> p u e s", u=BT, e=2)
        aggr = t(27, 16).rearrange("p (u e s) -> p u e s", u=BT, e=2)
        ev = [t(28 + j, 8).rearrange("p (u e) -> p u e", u=BT) for j in range(4)]
        ssq = t(24, 2048).rearrange("p (r q) -> p r q", r=2)
        ssq1 = [z.rearrange("p (k b) -> p k b", k=KD) for z in (sq[:].rearrange("p u f -> p (u f)"), t(36, 1024))]
        MRI2 = [X[:, j * 2048:(j + 1) * 2048].rearrange("p (r o b) -> p r o b", r=2, o=KD) for j in (0, 1)]
        msq2 = [z.rearrange("p (r q) -> p r q", r=2) for z in (X[:, 4096:6144], t(24, 2048))]
        m22 = [X[:, 6144:7168], t(40, 1024)]
        my2 = [X[:, 7168:8192], t(44, 1024)]
        amp2 = [X[:, 8192:9216], X[:, 9216:10240]]
        ssum2 = [ssum0[:], X[:, 11264:12288].rearrange("p (k b) -> p k b", k=KD)]
        prow = t(16, 1536).rearrange("p (j f) -> p j f", j=3)
        pos = t(0, 2048).rearrange("p (u f) -> p u f", u=BT)
        pon = t(8, 2048).rearrange("p (u f) -> p u f", u=BT)

        bcol = {}
        at = 0
        for name, k in (("b2r", 16), ("b2i", 16), ("bqr", 4), ("bqi", 4), ("bkr", 4), ("bki", 4), ("bvr", 4),
                        ("bvi", 4), ("bor", 4), ("boi", 4), ("gr", 2), ("ber", 2), ("gi", 2), ("bei", 2)):
            bcol[name] = at
            at += k

        def bias(name, j, lo=0, hi=P):
            return col[lo:hi, bcol[name] + j:bcol[name] + j + 1]

        def slot(st, ld):
            return ring[:, load_at[(st, ld)] % SLOTS, :]

        def unit(*key):
            return dw[:, place(unit_at[key]), :]

        def place(n):
            return turn(n) % DW

        def turn(n):
            st = units[n][0]
            return n - unit_at[(("inter", st[1] if st[0] == "inter" else HALVES - 1, 0, 0), 0)]

        def split(st, j):
            return split_ring[split_at[(st, j)] % SPLITS]

        def split_free(eng, n):
            h = n // splits_half
            if n % splits_half >= SPLITS:
                eng.wait_ge(sem("tile_full"), splits[n - SPLITS][3] + 1)
            elif h:
                full(eng, ("inter", h - 1, KD - 1, 1, 2))
                if n % SPLITS == 3:
                    superposed(eng, KD * h)

        def split_source(n):
            st, ld, j, _ = splits[n]
            return slot(st, ld)[:, j * 1024:(j + 1) * 1024]

        def split_before(st):
            s, a = st[0], st[1:]
            base = a[0] * splits_half if a else 0
            if s == "nodes" and a[1] == 1:
                return base + 2
            if s == "k" and a[1] == 0:
                return base + 3
            if s == "q":
                return base + 2 * (a[1] + 2)
            if s == "value" and a[1] == 0 and a[2] in (0, 1):
                return base + splits_half
            return 0

        def bank(key):
            return ps[number[key] % BANKS][:, :]

        def full(eng, key):
            eng.wait_ge(sem("tile_full"), number[key] + 1)

        def read_of(eng, key):
            s, n = emptied[number[key]]
            eng.wait_ge(sem(s), n)

        NV, NA, NP, NR = 18, 3, 7, 3
        sup_index = lambda h, et: h * KD + et

        def superposed(eng, tiles):
            eng.wait_ge(sem("sup_v"), NV * tiles)
            eng.wait_ge(sem("sup_p"), NP * tiles)
            eng.wait_ge(sem("sup_r"), NR * tiles)

        def unit_vectors_used(eng, q):
            eng.wait_ge(sem("sup_v"), NV * q + 10)
            eng.wait_ge(sem("sup_p"), NP * q + 1)

        def weighted(eng, dst, k, up):
            o = (0, 3, 5)[k - 1]
            s_ij = st_bc[:, k:k + 5 * (3 - k) + 1:5, :] if up else st_bc[:, 4 * k:4 * k + 5 * (3 - k) + 1:5, :]
            return eng.tensor_tensor(dst[:, k:N] if up else dst[:, 0:N - k], cc[:, o:o + N - k, :], s_ij, ALU.mult)

        def weighted_sum(eng, h, et, r, name, before):
            z = prod[:, r]
            eng.tensor_tensor(z, RI2[h][et][:, r], Wt[:], ALU.mult).then_inc(sem(name), 1)
            eng.wait_ge(sem(name), before + 1)
            eng.tensor_tensor(z[:, 0:2], z[:, 0:2], z[:, 2:4], ALU.add).then_inc(sem(name), 1)
            eng.wait_ge(sem(name), before + 2)
            eng.tensor_tensor(SUP2[h][:, r, et], z[:, 0], z[:, 1], ALU.add).then_inc(sem(name), 1)

        def m_parts(eng, h, op):
            rr = sq[:, op, :].rearrange("p (o b) -> p o b", o=2)
            R, I = (MRI2[h][:, r, 2 * op:2 * op + 2, :] for r in range(2))
            read_of(eng, ("meas", h, op, 1))
            eng.tensor_tensor(I, rr, R, ALU.add).then_inc(sem("m_sum_ready"), 1)
            eng.wait_ge(sem("m_sum_ready"), 2 * h + op + 1)
            eng.tensor_tensor(R, rr, R, ALU.subtract).then_inc(sem("mr_ready"), 1)

        def ssum(eng, h, et):
            ks = slice(0, KD) if et is None else slice(et, et + 1)
            s2 = ssum2[h]
            if h:
                full(eng, ("inter", h, KD - 1, 1, 2))
                superposed(eng, sup_index(h, et) + 1)
            eng.tensor_tensor(s2[:, ks], SUP2[h][:, 0, ks], SUP2[h][:, 1, ks], ALU.add).then_inc(sem("ssum_ready"), 1)

        block = ctx.enter_context(nc.Block())

        @block.sync
        def _(sp):
            sp.dma_start(w1s, w1).then_inc(sem("in_enc"), 16)
            sp.dma_start(b1s, rows[0:1, 0:512].to_broadcast([P, 512])).then_inc(sem("in_b1"), 16)
            sp.dma_start(col[:], cols).then_inc(sem("in_const"), 16)
            sp.dma_start(idn[:], ident).then_inc(sem("in_const"), 16)
            sp.dma_start(msk[:], mask).then_inc(sem("in_const"), 16)
            src = {"W2": lambda e, np_: (w2r, w2i)[e][:, np_, :], "Wqk": lambda c: wqk[:, c, :],
                   "Wv": lambda r: (wvr, wvi)[r], "Wo": lambda r: (wor, woi)[r],
                   "Wint": lambda et, np_: wint[:, et, np_, :], "M": lambda r: (mr, mi)[r], "Wp": lambda: wp}
            for n, (st, ld) in enumerate(loads):
                if n >= SLOTS:
                    if last_use[n - SLOTS][0] in ("k", "value"):
                        sp.wait_ge(sem("w_lo_ready"), split_at[(last_use[n - SLOTS], 1)] + 1)
                    elif loads[n - SLOTS][1][0] == "W2":
                        _, h, e = loads[n - SLOTS][0]
                        full(sp, ("nodes", h, e, 2 * loads[n - SLOTS][1][2] + 1, 1))
                    else:
                        sp.wait_ge(sem("tile_full"), last_tile[last_use[n - SLOTS]] + 1)
                    if last_use[n - SLOTS][0] == "inter":
                        sp.wait_ge(sem("dw_ready"), max(v for k, v in unit_at.items() if k[0] == last_use[n - SLOTS]) + 1)
                sp.dma_start(ring[:, n % SLOTS, :], src[ld[0]](*ld[1:])).then_inc(sem(f"slot{n % SLOTS}"), 16)

        @block.tensor
        def _(pe):
            seen = set()

            def begin(key):
                n = number[key]
                if n >= BANKS:
                    s, k = emptied[n - BANKS]
                    pe.wait_ge(sem(s), k)

            def products(dst, lhs, rhs, start, stop):
                for n, (x, y) in enumerate(((0, 0), (0, 1), (1, 0))):
                    mm = pe.matmul(dst, lhs[x], rhs[y], start=start and n == 0, stop=stop and n == 2)
                return mm

            def norm(h):
                key = ("norm", h)
                begin(key)
                pe.wait_ge(sem("supsq_ready"), h + 1)
                for bt in range(2):
                    for k in range(KD):
                        mm = pe.matmul(bank(key)[:, 2 * bt:2 * bt + 2], ssq1[h][:, k, bt * P:(bt + 1) * P], ones[:, 0:2],
                                       start=k == 0, stop=k == KD - 1)
                mm.then_inc(sem("tile_full"), 1)

            def measure(h, op, q, ks, w):
                if q == 2 and h == 0:
                    pe.wait_ge(sem("dw_ready"), unit_at[(("meas", 0), op)] + 1)
                for k in ks:
                    for o in range(2):
                        if q < 2:
                            lhs, rhs = w[q][:, k, (2 * op + o) * P:(2 * op + o + 1) * P], SUP2[h][:, q, k, :]
                        else:
                            lhs = unit(("meas", 0), op).rearrange("p (k o) -> p k o", k=KD)[:, k, o * P:(o + 1) * P]
                            rhs = ssum2[h][:, k, :]
                        mm = pe.matmul(bank(("meas", h, op, q))[:, o * HB:(o + 1) * HB], lhs, rhs,
                                       start=k == 0 and o == 0, stop=k == KD - 1 and o == 1)
                if KD - 1 in ks:
                    mm.then_inc(sem("tile_full"), 1)

            def weights(st, ld):
                n = load_at[(st, ld)]
                if n not in seen:
                    seen.add(n)
                    pe.wait_ge(sem(f"slot{n % SLOTS}"), 16 * (n // SLOTS + 1))
                return slot(st, ld)

            for st in steps:
                s, a = st[0], st[1:]
                if s == "enc":
                    pe.wait_ge(sem("in_enc"), 16)
                    pe.wait_ge(sem("in_x"), 16)
                    for b in range(BT):
                        key = ("enc", b)
                        for e in range(2):
                            for k in range(KH):
                                mm = pe.matmul(bank(key)[:, e * HID:(e + 1) * HID], xs[:, k, b * P:(b + 1) * P],
                                               w1s[:, e, k, :], start=k == 0, stop=k == KH - 1)
                        mm.then_inc(sem("tile_full"), 1)
                    pe.wait_ge(sem("in_const"), 48)
                if s == "encT":
                    for b in range(BT):
                        key = ("encT", b)
                        begin(key)
                        pe.wait_ge(sem("hn_ready"), 2 * (b + 1))
                        for j in range(4):
                            mm = pe.transpose(bank(key)[:, j * P:(j + 1) * P], hn[:, b, j * P:(j + 1) * P], idn[:])
                        mm.then_inc(sem("tile_full"), 1)
                if s == "nodes":
                    h, e = a
                    pe.wait_ge(sem("h_ready"), 4 * (2 * h + 2))
                    for n in range(N):
                        w = weights(st, ("W2", e, n // 2)).rearrange("p (k n d) -> p k n d", k=KH, n=2)
                        for dp in range(2):
                            key = ("nodes", h, e, n, dp)
                            begin(key)
                            for d in range(2):
                                for k in range(KH):
                                    d0 = (2 * dp + d) * P
                                    mm = pe.matmul(bank(key)[:, d * HB:(d + 1) * HB], w[:, k, n % 2, d0:d0 + P],
                                                   hT[:, e, k, h * HB:(h + 1) * HB], start=k == 0, stop=k == KH - 1)
                            mm.then_inc(sem("tile_full"), 1)
                if s in ("k", "q"):
                    h, c = a
                    if c == 0:
                        read_of(pe, ("nodes", h, 1, 3, 1))
                    m = "kq".index(s)
                    pe.wait_ge(sem("w_lo_ready"), split_at[(("k", h, c), m)] + 1)
                    w = split(("k", h, c), m).rearrange("p s (e k d) -> p s e k d", e=2, k=KD)
                    for np_ in range(2):
                        for e in range(2):
                            key = ("qk", h, c, np_, s + "ri"[e])
                            begin(key)
                            for k in range(KD):
                                mm = products(bank(key), [w[:, x, e, k, :] for x in range(2)],
                                              [S[x][:, e, k, np_ * 512:(np_ + 1) * 512] for x in range(2)], k == 0, k == KD - 1)
                            mm.then_inc(sem("tile_full"), 1)
                if s == "score":
                    h, c = a
                    read_of(pe, ("qk", h, c, 1, "qr"))
                    read_of(pe, ("qk", h, c, 1, "qi"))
                    for g in range(G):
                        key = ("score", h, c, g)
                        begin(key)
                        for x in range(2):
                            mm = pe.matmul(bank(key)[:, x * 256:(x + 1) * 256], K[c % 2][:, x, g * P:(g + 1) * P],
                                           Q[:, c % 2, x, :, g * P:(g + 1) * P], start=True, stop=True)
                        mm.then_inc(sem("tile_full"), 1)
                if s == "value":
                    h, e, g = a
                    key = ("value", h, e, g)
                    begin(key)
                    for k in range(KD):
                        first = ("value", h, e, 0)
                        if g == 0 and k % 2 == 0:
                            pe.wait_ge(sem("w_lo_ready"), split_at[(first, k // 2)] + 1)
                        w = split(first, k // 2).rearrange("p s (k f) -> p s k f", k=2)
                        mm = products(bank(key), [S[x][:, e, k, g * P:(g + 1) * P] for x in range(2)],
                                      [w[:, x, k % 2, :] for x in range(2)], k == 0, k == KD - 1)
                    mm.then_inc(sem("tile_full"), 1)
                if s == "mix":
                    h, gp = a
                    read_of(pe, ("value", h, 0, 2 * gp + 1))
                    read_of(pe, ("value", h, 1, 2 * gp + 1))
                    pe.wait_ge(sem("prob_by_pool"), h * G // 2 + gp + 1)
                    pe.wait_ge(sem("prob_by_dve"), h * G // 2 + gp + 1)
                    for c in range(C):
                        key = ("mix", h, gp, c)
                        begin(key)
                        for x in range(2):
                            for g in range(2):
                                gg = 2 * gp + g
                                mm = pe.matmul(bank(key)[:, (2 * x + g) * P:(2 * x + g + 1) * P],
                                               V[:, gg, c, x * P:(x + 1) * P],
                                               PR[:, gg % 4, (2 * c + x) * 4:(2 * c + x) * 4 + 4, :], start=True, stop=True)
                        mm.then_inc(sem("tile_full"), 1)
                if s == "attn_out":
                    h, np_ = a
                    read_of(pe, ("mix", h, 2 * np_ + 1, C - 2))
                    read_of(pe, ("mix", h, 2 * np_ + 1, C - 1))
                    for et in range(KD):
                        for r in range(2):
                            key = ("attn_out", h, np_, et, r)
                            begin(key)
                            w = weights(("attn_out", h, 0), ("Wo", r)).rearrange("p (k f) -> p k f", k=KD)
                            for k in range(C):
                                mm = pe.matmul(bank(key), w[:, k, et * P:(et + 1) * P], MX[:, r, k, np_ * 512:(np_ + 1) * 512],
                                               start=k == 0, stop=k == C - 1)
                            mm.then_inc(sem("tile_full"), 1)
                if s == "inter":
                    h, et, np_ = a
                    w = weights(st, ("Wint", et, np_)).rearrange("p (n r k e) -> p n r k e", n=2, r=2, k=KD)
                    if et == 0:
                        read_of(pe, ("attn_out", h, 1, KD - 1, 0))
                        read_of(pe, ("attn_out", h, 1, KD - 1, 1))
                    for q in range(3):
                        key = ("inter", h, et, np_, q)
                        begin(key)
                        if q == 2:
                            pe.wait_ge(sem("dw_ready"), unit_at[(st, 0)] + 1)
                            if et == 0:
                                pe.wait_ge(sem("asum_ready"), h * 8 + 8)
                        for n in range(2):
                            for k in range(KD):
                                lhs = w[:, n, q, k, :] if q < 2 else unit(st, 0).rearrange("p (n k e) -> p n k e", n=2, k=KD)[:, n, k, :]
                                rhs = A[:, q, k, 2 * np_ + n, :]
                                mm = pe.matmul(bank(key)[:, n * HB:(n + 1) * HB], lhs, rhs, start=k == 0, stop=k == KD - 1)
                        mm.then_inc(sem("tile_full"), 1)
                if s == "norm":
                    norm(*a)
                if s == "meas":
                    (h,) = a
                    w = [weights(("meas", 0), ("M", r)).rearrange("p (k o) -> p k o", k=KD) for r in range(2)]
                    parts = [(op, q) for op in range(2) for q in range(3)]
                    if h == 0:
                        pe.wait_ge(sem("ssum_ready"), 1)
                        for op, q in parts:
                            begin(("meas", h, op, q))
                            measure(h, op, q, range(KD), w)
                    else:
                        for ks in (range(2), range(2, 3), range(3, KD)):
                            superposed(pe, sup_index(h, ks[-1]) + 1)
                            pe.wait_ge(sem("ssum_ready"), 1 + ks[-1] + 1)
                            for op, q in parts:
                                if 0 in ks:
                                    begin(("meas", h, op, q))
                                measure(h, op, q, ks, w)
                if s == "post":
                    (h,) = a
                    w = weights(("post", 0), ("Wp",)).rearrange("p (k o) -> p k o", k=KD)
                    pe.wait_ge(sem(f"amp{h}"), 4 if h else 5)
                    for bt in range(2):
                        key = ("post", h, bt)
                        begin(key)
                        for k in range(KD):
                            mm = pe.matmul(bank(key), amp2[h].rearrange("p (k b) -> p k b", k=KD)[:, k, bt * P:(bt + 1) * P], w[:, k, :], start=k == 0, stop=k == KD - 1)
                        mm.then_inc(sem("tile_full"), 1)

        @block.scalar
        def _(act):
            act.dma_start(xs[:], xT).then_inc(sem("in_x"), 16)
            act.wait_ge(sem("in_const"), 48)
            split_done = 0
            for st in steps:
                s, a = st[0], st[1:]
                while split_done < split_before(st):
                    n = split_done
                    k = load_at[splits[n][:2]]
                    split_free(act, n)
                    act.wait_ge(sem(f"slot{k % SLOTS}"), 16 * (k // SLOTS + 1))
                    act.activation(split_ring[n % SPLITS][:, 0], split_source(n), ACT.Copy).then_inc(sem("w_hi_ready"), 1)
                    split_done += 1
                if s == "enc":
                    act.wait_ge(sem("var_ready"), 1)
                    act.activation(ev[1][:], ev[0][:], ACT.Abs_reciprocal_sqrt).then_inc(sem("rstd0_ready"), 1)
                if s == "encT":
                    for b in range(BT):
                        full(act, ("encT", b))
                        for e in range(2):
                            for k in range(KH):
                                j = 2 * e + k
                                act.activation(hT[:, e, k, b * P:(b + 1) * P], bank(("encT", b))[:, j * P:(j + 1) * P], ACT.Gelu,
                                               bias=bias("bei" if e else "ber", k), scale=bias("gi" if e else "gr", k)
                                               ).then_inc(sem("h_ready"), 1)
                if s == "nodes":
                    h, e = a
                    if h:
                        superposed(act, sup_index(h - 1, e + 1) + 1)
                    for n in range(N):
                        for dp in range(2):
                            key = ("nodes", h, e, n, dp)
                            full(act, key)
                            for d in range(2):
                                act.activation(S_node[0][:, e, 2 * dp + d, n], bank(key)[:, d * HB:(d + 1) * HB].rearrange("p (g b) -> p g b", g=G), ACT.Identity,
                                               bias=bias("b2i" if e else "b2r", 4 * n + 2 * dp + d)).then_inc(sem("s_hi_ready"), 1)
                if s == "k":
                    h, c = a
                    if h and c == 0:
                        unit_vectors_used(act, sup_index(h - 1, KD - 1))
                    u = c % 2
                    for np_ in range(2):
                        nn = slice(np_ * 512, (np_ + 1) * 512)
                        key = ("qk", h, c, np_, "kr")
                        full(act, key)
                        src = bank(key)
                        act.activation(K[u][0:64, 0, nn], src[0:64], ACT.Identity, bias=bias("bkr", c, 0, 64)).then_inc(sem("qk_by_act"), 1)
                        act.activation(K[u][64:128, 1, nn], src[64:128], ACT.Identity, bias=bias("bkr", c, 64, 128)).then_inc(sem("qk_by_act"), 1)
                if s == "q":
                    h, c = a
                    if h == 0 and c == 0:
                        act.wait_ge(sem("ncol_ready"), 1)
                    if h and c < 2:
                        superposed(act, KD * h)
                        if c:
                            act.wait_ge(sem("supsq_ready"), h)
                    u = c % 2
                    for np_ in range(2):
                        nn = slice(np_ * 512, (np_ + 1) * 512)
                        key = ("qk", h, c, np_, "qr")
                        full(act, key)
                        src = bank(key)
                        act.activation(Q[0:64, u, 0, 0, nn], src[0:64], ACT.Identity, bias=bias("bqr", c, 0, 64)).then_inc(sem("qk_by_act"), 1)
                        act.activation(Q[64:128, u, 0, 1, nn], src[0:64], ACT.Identity, bias=ncol[0:64, c:c + 1], scale=-1.0).then_inc(sem("qk_by_act"), 1)
                        act.activation(Q[64:128, u, 1, 0, nn], src[64:128], ACT.Identity, bias=bias("bqr", c, 64, 128)).then_inc(sem("qk_by_act"), 1)
                        act.activation(Q[0:64, u, 1, 1, nn], src[64:128], ACT.Identity, bias=ncol[64:128, c:c + 1], scale=-1.0).then_inc(sem("qk_by_act"), 1)
                if s == "score":
                    h, c = a
                    if h and c == 0:
                        act.wait_ge(sem("r_ready"), 2 * KD * h)
                        read_of(act, ("norm", h - 1))
                    for g in range(G):
                        i = (h * C + c) * G + g
                        full(act, ("score", h, c, g))
                        if i >= 2:
                            act.wait_ge(sem("diag_ready"), i - 1)
                        act.activation(sq[:, i % 2, :], bank(("score", h, c, g)), ACT.Square).then_inc(sem("sq_ready"), 1)
                if s == "value" and a[1] == 0:
                    h, e, g = a
                    key = ("value", h, 0, g)
                    if g in (0, G // 2):
                        full(act, ("score", h, 3 if g else 2, G - 1))
                    full(act, key)
                    dst = V[:, g].rearrange("p c (u f) -> p c u f", u=4)[:, :, 0:4:3, :]
                    act.activation(dst, bank(key).rearrange("p (c u f) -> p c u f", c=C, u=2), ACT.Copy).then_inc(sem("vr_ready"), 1)
                if s == "softmax":
                    (h,) = a
                    act.wait_ge(sem("smx_v"), 5 * h + 1)
                    act.activation(sm[1], sm[0], ACT.Abs_reciprocal_sqrt).then_inc(sem("smx_a"), 1)
                    act.wait_ge(sem("smx_v"), 5 * h + 4)
                    act.activation(sm[5], sm[4], ACT.Exp, scale=SCALE).then_inc(sem("smx_a"), 1)
                if s == "mix":
                    h, gp = a
                    for c in range(0, C, 2):
                        key = ("mix", h, gp, c)
                        full(act, key)
                        for x, lo, r in ((0, 0, 0), (0, 64, 1), (1, 0, 1), (1, 64, 0)):
                            src = bank(key)[lo:lo + 64, x * 256:(x + 1) * 256]
                            dst = MX[lo:lo + 64, r, c, gp * 256:(gp + 1) * 256]
                            act.activation(dst, src, ACT.Identity, bias=bias("bvi" if r else "bvr", c, lo, lo + 64)).then_inc(sem("mix_by_act"), 1)
                if s == "attn_out":
                    h, np_ = a
                    for et in range(KD):
                        key = ("attn_out", h, np_, et, 0)
                        full(act, key)
                        act.activation(A_rows(0, et, np_), bank(key).rearrange("p (g n b) -> p n g b", g=4, n=N),
                                       ACT.Identity, bias=bias("bor", et)).then_inc(sem("ar_ready"), 1)
                if s == "inter":
                    h, et, np_ = a
                    i = 2 * sup_index(h, et) + np_
                    for q in range(2):
                        full(act, ("inter", h, et, np_, q))
                        if q == 0:
                            if i >= 2:
                                act.wait_ge(sem("r_ready"), i - 1)
                            if et == 0:
                                act.wait_ge(sem("diag_ready"), (h + 1) * C * G)
                            dst = sq[:, i % 2, :].rearrange("p (n b) -> p n b", n=2)
                        else:
                            if np_ == 0 and sup_index(h, et) >= 3:
                                superposed(act, sup_index(h, et) - 2)
                            dst = RI2[h][et][:, 0, 2 * np_:2 * np_ + 2, :]
                        act.activation(dst, bank(("inter", h, et, np_, q)).rearrange("p (n b) -> p n b", n=2), ACT.Copy).then_inc(sem("rr_ready"), 1)
                if s == "cosines":
                    h, et = a
                    q = sup_index(h, et)
                    RI = RI2[h][et]
                    act.wait_ge(sem("r_ready"), 2 * q + 2)
                    act.wait_ge(sem("i_ready"), 2 * q + 2)
                    if q:
                        if (h, et) == (0, KD - 1):
                            superposed(act, q)
                        else:
                            act.wait_ge(sem("sup_v"), NV * (q - 1) + 1)
                    act.activation(zsq2[h][et], RI.rearrange("p r n b -> p r (n b)"), ACT.Square).then_inc(sem("sup_a"), 1)
                    act.wait_ge(sem("sup_v"), NV * q + 1)
                    act.activation(y0, n2, ACT.Abs_reciprocal_sqrt).then_inc(sem("sup_a"), 1)
                    act.wait_ge(sem("sup_a"), NA * q + 2)
                    act.activation(y2, y0, ACT.Square).then_inc(sem("sup_a"), 1)
                if s == "square":
                    (h,) = a
                    superposed(act, KD * (h + 1))
                    act.activation(ssq[:], SUP2[h].rearrange("p r k b -> p r (k b)"), ACT.Square).then_inc(sem("norm_a"), 1)
                if s == "rnorm":
                    (h,) = a
                    act.wait_ge(sem("norm_v"), 4 * h + 1)
                    act.activation(small[:, 12:14], small[:, 10:12], ACT.Abs_reciprocal_sqrt).then_inc(sem("norm_a"), 1)
                if s == "meas":
                    (h,) = a
                    for op in range(2):
                        for q in range(2):
                            key = ("meas", h, op, q)
                            full(act, key)
                            if q == 0 and h == 0:
                                act.wait_ge(sem("r_ready"), 2 * KD * HALVES)
                            if q == 0 and h == 1:
                                act.wait_ge(sem("mr_ready"), op + 1)
                            dst = sq[:, op, :].rearrange("p (o b) -> p o b", o=2) if q == 0 else MRI2[h][:, 0, 2 * op:2 * op + 2, :]
                            act.activation(dst, bank(key).rearrange("p (o b) -> p o b", o=2), ACT.Copy).then_inc(sem("mrr_ready"), 1)
                    act.wait_ge(sem("mr_ready"), 2 * h + 2)
                    act.wait_ge(sem("mi_ready"), 2 * h + 2)
                    if h:
                        act.wait_ge(sem("supsq_ready"), h + 1)
                    act.activation(msq2[h], MRI2[h].rearrange("p r o b -> p r (o b)"), ACT.Square).then_inc(sem("amp_a"), 1)
                if s == "amp":
                    (h,) = a
                    act.wait_ge(sem(f"amp{h}"), 1)
                    act.activation(my2[h], m22[h], ACT.Abs_reciprocal_sqrt).then_inc(sem("amp_a"), 1)
                if s == "post":
                    (h,) = a
                    act.wait_ge(sem("post_w"), 4 * h + 1)
                    act.activation(small[:, 20 + 2 * h:22 + 2 * h], small[:, 16 + 2 * h:18 + 2 * h], ACT.Abs_reciprocal_sqrt).then_inc(sem("post_a"), 1)
                    for bt in range(2):
                        i = 2 * h + bt
                        if bt:
                            act.wait_ge(sem("post_v"), h + 1)
                        else:
                            act.wait_ge(sem("post_p"), 2 * h + 2)
                        act.activation(pos[:, i, :], pon[:, i, :], ACT.Gelu).then_inc(sem("post_a"), 1)
                        act.wait_ge(sem("post_a"), 3 * h + bt + 2)
                        act.dma_start(out[i * P:(i + 1) * P, :], pos[:, i, :]).then_inc(sem("outs"), 16)
            act.wait_ge(sem("outs"), 16 * BT)

        @block.vector
        def _(dve):
            done = {}

            def mark(ins, name):
                done[name] = done.get(name, 0) + 1
                ins.then_inc(sem(name), 1)
                return done[name]

            def step(ins, name):
                dve.wait_ge(sem(name), mark(ins, name))

            def refine(y, x, y_, name, tmp):
                step(dve.tensor_tensor(tmp, y_, y_, ALU.mult), name)
                step(dve.scalar_tensor_tensor(tmp, tmp, -0.5, x, ALU.mult, ALU.mult), name)
                return dve.scalar_tensor_tensor(y, tmp, 1.5, y_, ALU.add, ALU.mult)

            def rnorms(h):
                full(dve, ("norm", h))
                dve.tensor_copy(small[:, 34:36], bank(("norm", h))[:, 0:4:2]).then_inc(sem("norm_read"), 1)
                dve.wait_ge(sem("norm_read"), h + 1)
                step(dve.tensor_scalar(small[:, 10:12], small[:, 34:36], 1e-8, None, ALU.add), "norm_v")
                dve.wait_ge(sem("norm_a"), 2 * h + 2)
                step(refine(rnorm[:, 2 * h:2 * h + 2], small[:, 10:12], small[:, 12:14], "norm_v", small[:, 34:36]), "norm_v")

            dve.memset(ones[:], 1.0).then_inc(sem("ones_ready"), 1)
            dve.wait_ge(sem("in_b1"), 16)
            dve.wait_ge(sem("in_const"), 48)
            dve.tensor_scalar(ncol[:], col[:, bcol["bqr"]:bcol["bqr"] + 4], -1.0, None, ALU.mult).then_inc(sem("ncol_ready"), 1)
            for st in steps:
                s, a = st[0], st[1:]
                if s == "enc":
                    for b in range(BT):
                        full(dve, ("enc", b))
                        dve.tensor_tensor(hs[:, b, :], bank(("enc", b)), b1s, ALU.add).then_inc(sem("enc_sum"), 1)
                        dve.wait_ge(sem("enc_sum"), b + 1)
                        for e in range(2):
                            mark(dve.bn_stats(stat[:, b, e, :], hs[:, b, e * HID:(e + 1) * HID]), "enc_v")
                    dve.wait_ge(sem("enc_v"), done["enc_v"])
                    for b in range(BT):
                        for e in range(2):
                            mark(dve.bn_aggr(aggr[:, b, e, :], stat[:, b, e, :]), "enc_v")
                    dve.wait_ge(sem("enc_v"), done["enc_v"])
                    dve.tensor_scalar(ev[0][:], aggr[:, :, :, 1], EPS, None, ALU.add).then_inc(sem("var_ready"), 1)
                    dve.wait_ge(sem("var_ready"), 1)
                    dve.wait_ge(sem("rstd0_ready"), 1)
                    step(refine(ev[2][:], ev[0][:], ev[1][:], "enc_v", ev[3][:]), "enc_v")
                    for b in range(BT):
                        for e in range(2):
                            dve.tensor_scalar(hn[:, b, e * HID:(e + 1) * HID], hs[:, b, e * HID:(e + 1) * HID],
                                              aggr[:, b, e, 0:1], ev[2][:, b, e:e + 1], ALU.subtract, ALU.mult
                                              ).then_inc(sem("hn_ready"), 1)
                if s == "nodes":
                    h, e = a
                    if h and e == 0:
                        full(dve, ("inter", h - 1, KD - 1, 1, 2))
                    for n in range(N):
                        for dp in range(2):
                            key = ("nodes", h, e, n, dp)
                            done["s_lo"] = done.get("s_lo", 0) + 2
                            dve.wait_ge(sem("s_hi_ready"), done["s_lo"])
                            for d in range(2):
                                dve.scalar_tensor_tensor(S_node[1][:, e, 2 * dp + d, n], bank(key)[:, d * HB:(d + 1) * HB].rearrange("p (g b) -> p g b", g=G),
                                                         bias("b2i" if e else "b2r", 4 * n + 2 * dp + d), S_node[0][:, e, 2 * dp + d, n],
                                                         ALU.add, ALU.subtract).then_inc(sem("s_lo_ready"), 1)
                if s == "k":
                    h, c = a
                    if h and c == 0:
                        unit_vectors_used(dve, sup_index(h - 1, KD - 1))
                    u = c % 2
                    for np_ in range(2):
                        nn = slice(np_ * 512, (np_ + 1) * 512)
                        key = ("qk", h, c, np_, "ki")
                        full(dve, key)
                        src = bank(key)
                        dve.tensor_scalar(K[u][0:64, 1, nn], src[0:64], bias("bki", c, 0, 64), None, ALU.add).then_inc(sem("qk_by_dve"), 1)
                        dve.tensor_scalar(K[u][64:128, 0, nn], src[64:128], bias("bki", c, 64, 128), None, ALU.add).then_inc(sem("qk_by_dve"), 1)
                if s == "q":
                    h, c = a
                    if h and c < 2:
                        superposed(dve, KD * h)
                        if c:
                            dve.wait_ge(sem("supsq_ready"), h)
                    u = c % 2
                    for np_ in range(2):
                        nn = slice(np_ * 512, (np_ + 1) * 512)
                        key = ("qk", h, c, np_, "qi")
                        full(dve, key)
                        src = bank(key)
                        lo, hi = (src[0:64], bias("bqi", c, 0, 64)), (src[64:128], bias("bqi", c, 64, 128))
                        for dst, (x, bb) in ((Q[0:64, u, 1, 0, nn], lo), (Q[64:128, u, 1, 1, nn], lo),
                                             (Q[64:128, u, 0, 0, nn], hi), (Q[0:64, u, 0, 1, nn], hi)):
                            dve.tensor_scalar(dst, x, bb, None, ALU.add).then_inc(sem("qk_by_dve"), 1)
                if s == "score":
                    h, c = a
                    for g in range(G):
                        i = (h * C + c) * G + g
                        dve.wait_ge(sem("masked"), 2 * i + 2)
                        if c == 0 and g == 0 and h:
                            dve.wait_ge(sem("smx_in"), 16 * h)
                        dve.tensor_reduce(diag[:, g, c * 8:(c + 1) * 8], sq[:, i % 2, :].rearrange("p (x v n b) -> p x v n b", x=2, v=2, n=N)[:, :, 0],
                                          AX.X, ALU.add).then_inc(sem("diag_ready"), 1)
                if s == "value" and a[1] == 1:
                    h, e, g = a
                    key = ("value", h, 1, g)
                    full(dve, key)
                    dst = V[:, g].rearrange("p c (u f) -> p c u f", u=4)[:, :, 1:3, :]
                    src = bank(key).rearrange("p (c u f) -> p c u f", c=C, u=2)
                    dve.tensor_copy(dst, src).then_inc(sem("vi_ready"), 1)
                if s == "softmax":
                    (h,) = a
                    X0 = sm[6].rearrange("p (g m q) -> p g m q", g=2, m=4)
                    dve.wait_ge(sem("diag_ready"), (h + 1) * C * G)
                    for m in range(4):
                        for gq in range(4):
                            mark(dve.tensor_copy(X0[32 * gq:32 * gq + 32, :, m, :], diag[32 * m:32 * m + 32, gq:G:4, :]), "smx_in")
                    dve.wait_ge(sem("smx_in"), 16 * (h + 1))
                    step(dve.tensor_scalar(sm[0], sm[6], 1e-8, None, ALU.add), "smx_v")
                    dve.wait_ge(sem("smx_a"), 2 * h + 1)
                    step(refine(sm[3], sm[0], sm[1], "smx_w", sm[2]), "smx_w")
                    step(dve.tensor_tensor(sm[7], sm[0], sm[3], ALU.mult), "smx_v")
                    q4 = lambda z: z.rearrange("p (g m q) -> p g q m", g=2, m=4)
                    mx = sm[2][:, 0:64].rearrange("p (g q) -> p g q", g=2)
                    step(dve.tensor_reduce(mx, q4(sm[7]), AX.X, ALU.max), "smx_v")
                    bc = lambda z: z.unsqueeze(2).to_broadcast([P, 2, 4, 32])
                    v4 = lambda z: z.rearrange("p (g m q) -> p g m q", g=2, m=4)
                    mark(dve.tensor_tensor(v4(sm[4]), v4(sm[7]), bc(mx), ALU.subtract), "smx_v")
                    dve.wait_ge(sem("smx_a"), 2 * h + 2)
                    sums = sm[0][:, 0:64].rearrange("p (g q) -> p g q", g=2)
                    step(dve.tensor_reduce(sums, q4(sm[5]), AX.X, ALU.add), "smx_w")
                    rs = sm[1][:, 0:64].rearrange("p (g q) -> p g q", g=2)
                    step(dve.reciprocal(rs, sums), "smx_w")
                    mark(dve.tensor_tensor(v4(sm[3]), v4(sm[5]), bc(rs), ALU.mult), "smx_v")
                    dve.wait_ge(sem("smx_v"), 5 * h + 5)
                    wk = sm[6].rearrange("p (g q) -> p g q", g=G)
                    for m in range(4):
                        for gq in range(4):
                            mark(dve.tensor_copy(wk[32 * m:32 * m + 32, gq:G:4, :], v4(sm[3])[32 * gq:32 * gq + 32, :, m, :]), "smx_out")
                    dve.wait_ge(sem("smx_out"), 16 * (h + 1))
                if s == "mix":
                    h, gp = a

                    def spread(g):
                        wk = sm[6].rearrange("p (g q) -> p g q", g=G)
                        if g >= 4:
                            full(dve, ("mix", h, g // 2 - 2, C - 1))
                        dve.tensor_tensor(PR[:, g % 4], wk[:, g].unsqueeze(2).to_broadcast([P, 32, 32]),
                                          msk[:].unsqueeze(1).to_broadcast([P, 32, 32]), ALU.mult).then_inc(sem("prob_by_dve"), 1)

                    if gp == 0:
                        spread(1)
                        spread(3)
                    for c in range(1, C, 2):
                        key = ("mix", h, gp, c)
                        full(dve, key)
                        for x, lo, r in ((0, 0, 0), (0, 64, 1), (1, 0, 1), (1, 64, 0)):
                            src = bank(key)[lo:lo + 64, x * 256:(x + 1) * 256]
                            dst = MX[lo:lo + 64, r, c, gp * 256:(gp + 1) * 256]
                            dve.tensor_scalar(dst, src, bias("bvi" if r else "bvr", c, lo, lo + 64), None, ALU.add).then_inc(sem("mix_by_dve"), 1)
                    if 2 * gp + 5 < G:
                        spread(2 * gp + 5)
                if s == "attn_out":
                    h, np_ = a
                    for et in range(KD):
                        key = ("attn_out", h, np_, et, 1)
                        full(dve, key)
                        dve.tensor_scalar(A_rows(1, et, np_), bank(key).rearrange("p (g n b) -> p n g b", g=4, n=N),
                                          bias("boi", et), None, ALU.add).then_inc(sem("ai_ready"), 1)
                if s == "inter":
                    h, et, np_ = a
                    i = 2 * sup_index(h, et) + np_
                    dve.wait_ge(sem("rr_ready"), 2 * i + 2)
                    if np_ == 0 and sup_index(h, et) >= 3:
                        superposed(dve, sup_index(h, et) - 2)
                    R, I = (RI2[h][et][:, r, 2 * np_:2 * np_ + 2, :] for r in range(2))
                    dve.tensor_tensor(I, sq[:, i % 2, :].rearrange("p (n b) -> p n b", n=2), R, ALU.add).then_inc(sem("rr_ii_ready"), 1)
                    full(dve, ("inter", h, et, np_, 2))
                    dve.wait_ge(sem("rr_ii_ready"), i + 1)
                    dve.tensor_tensor(I, bank(("inter", h, et, np_, 2)).rearrange("p (n b) -> p n b", n=2), I, ALU.subtract).then_inc(sem("i_ready"), 1)
                if s == "cosines":
                    h, et = a
                    q = sup_index(h, et)
                    RI = RI2[h][et]
                    dve.wait_ge(sem("sup_a"), NA * q + 1)
                    dve.wait_ge(sem("r_ready"), 2 * q + 2)
                    dve.wait_ge(sem("i_ready"), 2 * q + 2)
                    zsq = zsq2[h][et]
                    mark(dve.scalar_tensor_tensor(n2, zsq[:, 0], TINY, zsq[:, 1], ALU.max, ALU.add), "sup_v")
                    dve.wait_ge(sem("sup_v"), done["sup_v"])
                    step(dve.tensor_scalar(Efl[:], n2.rearrange("p (n b) -> p n b", n=N), TINY, None, ALU.is_le), "sup_v")
                    o = 0
                    for k in (1, 2, 3):
                        mark(dve.tensor_tensor(Eij[:, o:o + 4 - k, :], Efl[:, 0:4 - k, :], Efl[:, k:4, :], ALU.add), "sup_v")
                        o += 4 - k
                    dve.wait_ge(sem("sup_v"), NV * q + 5)
                    dve.wait_ge(sem("sup_a"), NA * q + 3)
                    step(dve.scalar_tensor_tensor(y2, y2, -0.5, n2, ALU.mult, ALU.mult), "sup_v")
                    step(dve.scalar_tensor_tensor(y0, y2, 1.5, y0, ALU.add, ALU.mult), "sup_v")
                    step(dve.tensor_tensor(U[:].rearrange("p r n b -> p r (n b)"), RI[:].rearrange("p r n b -> p r (n b)"),
                                           y0.unsqueeze(1).to_broadcast([P, 2, 1024]), ALU.mult), "sup_v")
                    if q:
                        superposed(dve, q)
                    mark(dve.tensor_tensor(pr[:, :, 0:3, :], U[:, :, 0:3, :], U[:, :, 1:4, :], ALU.mult), "sup_v")
                    mark(dve.tensor_tensor(pr[:, :, 3:5, :], U[:, :, 0:2, :], U[:, :, 2:4, :], ALU.mult), "sup_v")
                    dve.wait_ge(sem("sup_v"), done["sup_v"])
                    dve.wait_ge(sem("sup_p"), NP * q + 1)
                    step(dve.tensor_tensor(cc[:], pr[:, 0], Eij[:], ALU.add), "sup_v")
                    step(dve.tensor_tensor(cc[:], cc[:], pr[:, 1], ALU.add), "sup_v")
                if s == "super":
                    h, et = a
                    q = sup_index(h, et)
                    RI = RI2[h][et]
                    if q:
                        superposed(dve, q)
                    dve.wait_ge(sem("in_s"), 16 * h + 16)
                    mark(weighted(dve, Wt, 1, False), "sup_v")
                    mark(weighted(dve, W1, 2, False), "sup_v")
                    mark(weighted(dve, W2, 3, False), "sup_v")
                    dve.wait_ge(sem("sup_v"), done["sup_v"])
                    dve.wait_ge(sem("sup_p"), NP * q + 2)
                    step(dve.tensor_tensor(Wt[:], Wt[:], st_bc[:, 0:16:5, :], ALU.add), "sup_v")
                    dve.wait_ge(sem("sup_p"), NP * q + 3)
                    step(dve.tensor_tensor(Wt[:], Wt[:], W1[:], ALU.add), "sup_v")
                    dve.wait_ge(sem("sup_p"), NP * q + 4)
                    step(dve.tensor_tensor(Wt[:], Wt[:], W2[:], ALU.add), "sup_v")
                    assert done["sup_v"] == NV * (q + 1), done["sup_v"]
                    if et == KD - 1:
                        weighted_sum(dve, h, et, 0, "sup_r", NR * q)
                        if h:
                            dve.wait_ge(sem("amp_a"), 1)
                            dve.scalar_tensor_tensor(m22[0], msq2[0][:, 0], TINY, msq2[0][:, 1], ALU.max, ALU.add).then_inc(sem("amp0"), 1)
                            ssum(dve, h, et)
                if s == "square":
                    (h,) = a
                    if h == 0:
                        superposed(dve, KD)
                        ssum(dve, h, None)
                    dve.wait_ge(sem("norm_a"), 2 * h + 1)
                    dve.tensor_tensor(ssq1[h][:].rearrange("p k b -> p (k b)"), ssq[:, 0], ssq[:, 1], ALU.add).then_inc(sem("supsq_ready"), 1)
                if s == "rnorm":
                    rnorms(*a)
                if s == "meas":
                    (h,) = a
                    for op in range(2):
                        if h:
                            m_parts(dve, h, op)
                        else:
                            dve.wait_ge(sem("mr_ready"), op + 1)
                        full(dve, ("meas", h, op, 2))
                        I = MRI2[h][:, 1, 2 * op:2 * op + 2, :]
                        dve.tensor_tensor(I, bank(("meas", h, op, 2)).rearrange("p (o b) -> p o b", o=2), I, ALU.subtract).then_inc(sem("mi_ready"), 1)
                if s == "amp" and a[0] == 1:
                    m2, my, amp, msq = m22[1], my2[1], amp2[1], msq2[1]
                    dve.wait_ge(sem("amp_a"), 3)
                    step(dve.scalar_tensor_tensor(m2, msq[:, 0], TINY, msq[:, 1], ALU.max, ALU.add), "amp1")
                    dve.wait_ge(sem("amp_a"), 4)
                    step(dve.tensor_tensor(m2, m2, my, ALU.mult), "amp1")
                    step(dve.scalar_tensor_tensor(my, my, -0.5, m2, ALU.mult, ALU.mult), "amp1")
                    mark(dve.scalar_tensor_tensor(amp, my, 1.5, m2, ALU.add, ALU.mult), "amp1")
                if s == "post":
                    (h,) = a
                    dve.wait_ge(sem("in_post"), 16)
                    for bt in range(2):
                        i = 2 * h + bt
                        key = ("post", h, bt)
                        full(dve, key)
                        dve.scalar_tensor_tensor(pos[:, i, :], bank(key), rnorm[:, i:i + 1], prow[:, 0], ALU.mult, ALU.add).then_inc(sem("post_sum"), 1)
                        dve.wait_ge(sem("post_sum"), i + 1)
                        step(dve.bn_stats(small[:, 28:34], pos[:, i, :]), "post_s")
                        step(dve.bn_aggr(small[:, 2 * i:2 * i + 2], small[:, 28:34]), "post_s")
                    var, r0, rstd = (small[:, x + 2 * h:x + 2 * h + 2] for x in (16, 20, 24))
                    step(dve.tensor_scalar(var, small[:, 4 * h + 1:4 * h + 4:2], EPS, None, ALU.add), "post_w")
                    dve.wait_ge(sem("post_a"), 3 * h + 1)
                    step(refine(rstd, var, r0, "post_w", small[:, 34:36]), "post_w")
                    for bt in range(2):
                        i = 2 * h + bt
                        step(dve.tensor_scalar(pon[:, i, :], pos[:, i, :], small[:, 2 * i:2 * i + 1], rstd[:, bt:bt + 1], ALU.subtract, ALU.mult), "post_n")
                        if bt:
                            step(dve.tensor_tensor(pon[:, i, :], pon[:, i, :], prow[:, 1], ALU.mult), "post_n")
                            mark(dve.tensor_tensor(pon[:, i, :], pon[:, i, :], prow[:, 2], ALU.add), "post_v")

        @block.gpsimd
        def _(pool):
            pool.wait_ge(sem("in_const"), 48)
            derived = [0]

            def derive(n):
                st, j, _ = units[n]
                if turn(n) >= DW:
                    pool.wait_ge(sem("tile_full"), units[n - DW][2] + 1)
                else:
                    pool.wait_ge(sem("tile_full"), splits[splits_half * (st[1] + 1) - 1][3] + 1)
                part = []
                for ld in loads_of(st):
                    k = load_at[(st, ld)]
                    pool.wait_ge(sem(f"slot{k % SLOTS}"), 16 * (k // SLOTS + 1))
                    w = ring[:, k % SLOTS, :]
                    if st[0] == "inter":
                        w = w.rearrange("p (n r f) -> p n r f", n=2, r=2)
                        part = [w[:, :, 0], w[:, :, 1]]
                    else:
                        part.append(w.rearrange("p (k o) -> p k o", k=KD)[:, :, j * 256:(j + 1) * 256])
                d = dw[:, place(n), :].rearrange("p (a f) -> p a f", a=part[0].shape[1])
                pool.tensor_tensor(d, part[0], part[1], ALU.add).then_inc(sem("dw_ready"), 1)

            def derive_upto(n):
                while derived[0] <= n:
                    derive(derived[0])
                    derived[0] += 1

            split_done = 0
            for st in steps:
                s, a = st[0], st[1:]
                while split_done < split_before(st):
                    n = split_done
                    pool.wait_ge(sem("w_hi_ready"), n + 1)
                    pool.tensor_tensor(split_ring[n % SPLITS][:, 1], split_source(n), split_ring[n % SPLITS][:, 0], ALU.subtract).then_inc(sem("w_lo_ready"), 1)
                    split_done += 1
                if s == "score":
                    h, c = a
                    for g in range(G):
                        i = (h * C + c) * G + g
                        v = sq[:, i % 2, :].rearrange("p (x v q) -> p x v q", x=2, v=2)
                        pool.wait_ge(sem("sq_ready"), i + 1)
                        pool.tensor_tensor(v[:, :, 0], v[:, :, 0], v[:, :, 1], ALU.add).then_inc(sem("masked"), 1)
                        pool.wait_ge(sem("masked"), 2 * i + 1)
                        m = v[:, :, 0].rearrange("p x (n b) -> p x n b", n=N)
                        pool.tensor_tensor(m, m, msk[:].unsqueeze(1).unsqueeze(1).to_broadcast([P, 2, N, 32]), ALU.mult).then_inc(sem("masked"), 1)
                if s == "mix":
                    h, gp = a

                    def spread(g):
                        wk = sm[6].rearrange("p (g q) -> p g q", g=G)
                        if g >= 4:
                            full(pool, ("mix", h, g // 2 - 2, C - 1))
                        pool.wait_ge(sem("smx_out"), 16 * (h + 1))
                        pool.tensor_tensor(PR[:, g % 4], wk[:, g].unsqueeze(2).to_broadcast([P, 32, 32]),
                                           msk[:].unsqueeze(1).to_broadcast([P, 32, 32]), ALU.mult).then_inc(sem("prob_by_pool"), 1)

                    if gp == 0:
                        spread(0)
                        spread(2)
                    if 2 * gp + 4 < G:
                        spread(2 * gp + 4)
                    if gp == G // 2 - 1:
                        full(pool, ("mix", h, G // 2 - 1, C - 1))
                        pool.dma_start(st_bc[:], strength[0:1, :, h * HB:(h + 1) * HB].to_broadcast([P, 16, HB])).then_inc(sem("in_s"), 16)
                if s == "attn_out":
                    h, np_ = a
                    for et in range(KD):
                        i = (h * 2 + np_) * KD + et + 1
                        pool.wait_ge(sem("ar_ready"), i)
                        pool.wait_ge(sem("ai_ready"), i)
                        bb = slice(np_ * P, (np_ + 1) * P)
                        pool.tensor_tensor(A[:, 2, et, :, bb], A[:, 0, et, :, bb], A[:, 1, et, :, bb], ALU.add).then_inc(sem("asum_ready"), 1)
                    if np_ == 0:
                        derive_upto(unit_at[(("inter", h, 0, 0), 0)])
                if s == "inter":
                    h, et, np_ = a
                    if (et, np_) == (KD - 1, 1) and h == HALVES - 1:
                        derive_upto(len(units) - 1)
                    derive_upto(min(unit_at[(st, 0)] + AHEAD, unit_at[(("inter", h, KD - 1, 1), 0)]))
                    i = 2 * sup_index(h, et) + np_
                    R = RI2[h][et][:, 0, 2 * np_:2 * np_ + 2, :]
                    pool.wait_ge(sem("rr_ii_ready"), i + 1)
                    pool.tensor_tensor(R, sq[:, i % 2, :].rearrange("p (n b) -> p n b", n=2), R, ALU.subtract).then_inc(sem("r_ready"), 1)
                if s == "cosines":
                    h, et = a
                    q = sup_index(h, et)
                    pool.wait_ge(sem("sup_v"), NV * q + 8)
                    if q:
                        superposed(pool, q)
                    pool.tensor_tensor(pr[:, :, 5, :], U[:, :, 0, :], U[:, :, 3, :], ALU.mult).then_inc(sem("sup_p"), 1)
                if s == "super":
                    h, et = a
                    q = sup_index(h, et)
                    pool.wait_ge(sem("sup_v"), NV * q + 12)
                    pool.wait_ge(sem("in_s"), 16 * h + 16)
                    if q:
                        superposed(pool, q)
                    for dst, k, up in ((Wt, 3, True), (W1, 2, True), (W2, 1, True)):
                        weighted(pool, dst, k, up).then_inc(sem("sup_p"), 1)
                    if (h, et) == (1, KD - 2):
                        for k in range(et):
                            ssum(pool, h, k)
                    pool.wait_ge(sem("sup_v"), NV * (q + 1))
                    if et < KD - 1:
                        weighted_sum(pool, h, et, 0, "sup_r", NR * q)
                    weighted_sum(pool, h, et, 1, "sup_p", NP * q + 4)
                    if (h, et) == (1, KD - 2):
                        ssum(pool, h, et)
                if s == "amp" and a[0] == 0:
                    superposed(pool, HALVES * KD)
                    pool.dma_start(prow[:], rows[0:1, 512:2048].rearrange("o (j f) -> o j f", j=3).to_broadcast([P, 3, 512])).then_inc(sem("in_post"), 16)
                    m2, my, amp = m22[0], my2[0], amp2[0]
                    pool.wait_ge(sem("amp0"), 1)
                    pool.wait_ge(sem("amp_a"), 2)
                    pool.tensor_tensor(m2, m2, my, ALU.mult).then_inc(sem("amp0"), 1)
                    pool.wait_ge(sem("amp0"), 2)
                    pool.tensor_tensor(my, my, m2, ALU.mult).then_inc(sem("amp0"), 1)
                    pool.wait_ge(sem("amp0"), 3)
                    pool.tensor_scalar(my, my, -0.5, 1.5, ALU.mult, ALU.add).then_inc(sem("amp0"), 1)
                    pool.wait_ge(sem("amp0"), 4)
                    pool.tensor_tensor(amp, my, m2, ALU.mult).then_inc(sem("amp0"), 1)
                if s == "meas" and a[0] == 0:
                    for op in range(2):
                        m_parts(pool, 0, op)
                if s == "post":
                    (h,) = a
                    i = 2 * h
                    pool.wait_ge(sem("in_post"), 16)
                    pool.wait_ge(sem("post_n"), 3 * h + 1)
                    pool.tensor_tensor(pon[:, i, :], pon[:, i, :], prow[:, 1], ALU.mult).then_inc(sem("post_p"), 1)
                    pool.wait_ge(sem("post_p"), 2 * h + 1)
                    pool.tensor_tensor(pon[:, i, :], pon[:, i, :], prow[:, 2], ALU.add).then_inc(sem("post_p"), 1)


def kernel(r_strength, r_x, **w):
    import numpy as np
    import concourse.bacc as bacc
    from concourse.bass_utils import run_bass_kernel_spmd

    g = {k[len("L0_rec_"):]: np.asarray(v) for k, v in w.items()}

    def tiles(m):
        k, n = m.shape
        return m.reshape(k // P, P, n).transpose(1, 0, 2)

    def turned(v):
        return v.reshape(*v.shape[:-1], -1, 2, 64)[..., ::-1, :].reshape(v.shape)

    def columns(v):
        return v.reshape(-1, P).T

    def w2(m):
        m = m.T.reshape(KH, P, 2, 2, D)
        return m.transpose(1, 2, 0, 3, 4).reshape(P, 2, -1)

    qk = np.stack([tiles(m) for m in (g["Wk_r"].T, turned(g["Wk_i"].T), g["Wq_r"].T, turned(g["Wq_i"].T))], 1)
    qk = qk.reshape(P, 4, KD, C, P).transpose(0, 3, 1, 2, 4).reshape(P, C, -1)
    vi = g["Wv_i"].T
    inter = np.stack([g["int_Wr"], g["int_Wi"]], 1)
    inter = inter.reshape(2, 2, 2, KD, P, KD, P)
    inter = inter.transpose(6, 3, 0, 1, 2, 5, 4).reshape(P, KD, 2, -1)
    cols = np.concatenate(
        [columns(g["er_b2"]), columns(g["ei_b2"]), columns(g["bq_r"]), columns(turned(g["bq_i"])), columns(g["bk_r"]),
         columns(turned(g["bk_i"])), columns(g["bv_r"]), columns(turned(g["bv_i"])), columns(g["bo_r"]), columns(g["bo_i"]),
         columns(g["er_g1"]), columns(g["er_be1"]), columns(g["ei_g1"]), columns(g["ei_be1"])], 1)
    rows = np.concatenate([g["er_b1"], g["ei_b1"], g["post_b"], g["post_g"], g["post_be"]])[None, :]
    flat = lambda m: tiles(m).reshape(P, -1)
    arrays = {
        "xT": tiles(np.asarray(r_x).T),
        "w1": np.stack([tiles(g["er_W1"].T), tiles(g["ei_W1"].T)], 1),
        "w2r": w2(g["er_W2"]), "w2i": w2(g["ei_W2"]), "wqk": qk,
        "wvr": flat(g["Wv_r"].T), "wvi": flat(vi),
        "wor": flat(g["Wo_r"].T), "woi": flat(turned(g["Wo_i"]).T),
        "wint": inter, "mr": flat(g["meas_Mr"].T), "mi": flat(g["meas_Mi"].T), "wp": flat(g["post_W"].T),
        "cols": cols, "rows": rows,
        "ident": np.eye(P, dtype=np.float32),
        "mask": np.tile(np.eye(32, dtype=np.float32), (4, 1)),
        "strength": np.asarray(r_strength).reshape(B, 16).T[None],
    }
    nc = bacc.Bacc("TRN2", target_bir_lowering=False, num_devices=1)
    sent, args = {}, {}
    for name, arr in arrays.items():
        sent[f"in_{name}"] = np.ascontiguousarray(arr)
        args[name] = nc.dram_tensor(f"in_{name}", arr.shape, mybir.dt.from_np(arr.dtype), kind="ExternalInput").ap()
    out = nc.dram_tensor("out", (B, OUT), F32, kind="ExternalOutput").ap()
    build(nc, out, **args)
    r = run_bass_kernel_spmd(nc, [sent], core_ids=[0])
    return r.results[0]["out"]
```
